# Optimizing a Trainium2 kernel written in Bass

```python
import numpy as np
import jax
import jax.numpy as jnp

def _softmax(x, axis=-1):
    return jax.nn.softmax(x, axis=axis)

def _gelu(x):
    return jax.nn.gelu(x, approximate=True)

def _silu(x):
    return jax.nn.silu(x)

def _sigmoid(x):
    return jax.nn.sigmoid(x)

def _layernorm(x, axis=-1, eps=1e-05):
    m = jnp.mean(x, axis=axis, keepdims=True)
    v = jnp.var(x, axis=axis, keepdims=True)
    return (x - m) / jnp.sqrt(v + eps)

def _scatter_add(tgt, idx, src, axis=0):
    return tgt.at[idx].add(src)

def _segment_sum(src, seg, n):
    return jax.ops.segment_sum(src, seg, n)
kernel_name = 'mk_lm_tower_d2_tok_ids512_r4_3ffe05'

def setup_inputs(seed: int=0):
    np.random.seed(seed)
    _w = jnp.asarray

    def _rec_inputs():
        import jax
        import jax.numpy as jnp
        _rk = jax.random.key(seed)
        x = jax.random.randint(jax.random.fold_in(_rk, 1), (4, 1024), 0, 12564, jnp.int32)
        itok_BS_2_50255 = jax.random.randint(jax.random.fold_in(_rk, 21), (4, 1024), 2, 12564, jnp.int32)
        return (x, itok_BS_2_50255)
    x, itok_BS_2_50255 = _rec_inputs()

    def _L0_tok_setup():
        import jax, jax.numpy as jnp
        import numpy as np
        VOCAB = 50257
        EMB_DIM = 128
        BATCH, SEQ = (8, 1024)
        key = jax.random.key(seed)
        k1, k2, k3 = jax.random.split(key, 3)
        input_one = jax.random.randint(k1, (BATCH, SEQ), 0, VOCAB, dtype=jnp.int64 if jax.config.jax_enable_x64 else jnp.int32)
        input_two = jax.random.randint(k2, (BATCH, SEQ), 0, VOCAB, dtype=jnp.int64 if jax.config.jax_enable_x64 else jnp.int32)
        weight = jax.random.normal(k3, (VOCAB, EMB_DIM), dtype=jnp.float32)
        return {'input_one': input_one, 'input_two': input_two, 'weight': weight}
    _L0_tok_all = _L0_tok_setup()
    _L0_tok_in = {k: v for k, v in _L0_tok_all.items() if k in ('weight',)}
    del _L0_tok_all

    def _L0_attn_setup():
        import jax, jax.numpy as jnp
        import numpy as np
        D_MODEL = 128
        D_STATE = 64
        CLAMP = 1000000.0

        def _layernorm(y, gamma, beta, eps=1e-05):
            mu = jnp.mean(y, axis=-1, keepdims=True)
            var = jnp.mean(jnp.square(y - mu), axis=-1, keepdims=True)
            return (y - mu) * jax.lax.rsqrt(var + eps) * gamma + beta
        key = jax.random.key(seed)
        kx, kA, kB, kC = jax.random.split(key, 4)
        B, L = (16, 1024)
        x = jax.random.normal(kx, (B, L, D_MODEL), dtype=jnp.float32)
        A = jax.random.normal(kA, (D_STATE, D_STATE), dtype=jnp.float32) * 0.01
        Bm = jax.random.normal(kB, (D_STATE, D_MODEL), dtype=jnp.float32) * 0.01
        C = jax.random.normal(kC, (D_MODEL, D_STATE), dtype=jnp.float32) * 0.01
        gamma = jnp.ones((D_MODEL,), dtype=jnp.float32)
        beta = jnp.zeros((D_MODEL,), dtype=jnp.float32)
        return {'x': x, 'A': A, 'Bm': Bm, 'C': C, 'gamma': gamma, 'beta': beta}
    _L0_attn_all = _L0_attn_setup()
    _L0_attn_in = {k: v for k, v in _L0_attn_all.items() if k in ('A', 'Bm', 'C', 'gamma', 'beta')}
    del _L0_attn_all

    def _L0_ffn_setup():
        import jax, jax.numpy as jnp
        import numpy as np
        B, S, D, F, E = (8, 1024, 128, 512, 8)
        INIT_LAMBDA = 0.2
        LN_EPS = 1e-05
        LN_MERGE = 0.03
        key = jax.random.key(seed)
        ks = jax.random.split(key, 12)
        n = lambda k, shp, s=1.0: jax.random.normal(k, shp, dtype=jnp.float32) * s
        return {'hidden_states': n(ks[0], (B, S, D)), 'gfc1_w': n(ks[1], (D, D), 0.01), 'gfc1_b': jnp.zeros((D,), jnp.float32), 'gfc2_w': n(ks[2], (E, D), 0.01), 'gfc2_b': jnp.full((E,), INIT_LAMBDA, dtype=jnp.float32), 'W1': n(ks[3], (F, D), 0.02), 'b1': jnp.zeros((F,), jnp.float32), 'W2': n(ks[4], (D, F), 0.02), 'b2': jnp.zeros((D,), jnp.float32), 'ln_g': jnp.ones((D,), jnp.float32), 'ln_b': jnp.zeros((D,), jnp.float32), 'tv_W1': n(ks[5], (E, F, D), 0.02), 'tv_b1': n(ks[6], (E, F), 0.02), 'tv_W2': n(ks[7], (E, D, F), 0.02), 'tv_b2': n(ks[8], (E, D), 0.02), 'tv_ln_g': n(ks[9], (E, D), 0.02), 'tv_ln_b': n(ks[10], (E, D), 0.02)}
    _L0_ffn_all = _L0_ffn_setup()
    _L0_ffn_in = {k: v for k, v in _L0_ffn_all.items() if k in ('gfc1_w', 'gfc1_b', 'gfc2_w', 'gfc2_b', 'W1', 'b1', 'W2', 'b2', 'ln_g', 'ln_b', 'tv_W1', 'tv_b1', 'tv_W2', 'tv_b2', 'tv_ln_g', 'tv_ln_b')}
    del _L0_ffn_all

    def _L1_attn_setup():
        import jax, jax.numpy as jnp
        import numpy as np
        B, N, C, H = (64, 200, 128, 8)
        D = C // H
        BASE = 10000.0

        def _rope(x):
            d = x.shape[-1]
            inv_freq = 1.0 / BASE ** (jnp.arange(0, d, 2, dtype=jnp.float32) / d)
            t = jnp.arange(x.shape[1], dtype=jnp.float32)
            freqs = jnp.outer(t, inv_freq)
            emb = jnp.concatenate([freqs, freqs], axis=-1)
            cos = jnp.cos(emb)[None, :, None, :]
            sin = jnp.sin(emb)[None, :, None, :]
            x1, x2 = (x[..., :d // 2], x[..., d // 2:])
            return x * cos + jnp.concatenate([-x2, x1], axis=-1) * sin
        key = jax.random.key(seed)
        k0, k1, k2 = jax.random.split(key, 3)
        x = jax.random.normal(k0, (B, N, C), jnp.float32)
        Wqk = jax.random.normal(k1, (C, 2 * C), jnp.float32) * C ** (-0.5)
        bqk = jnp.zeros((2 * C,), jnp.float32)
        lepe_w = jax.random.normal(k2, (C, 1, 3), jnp.float32) * 0.3
        lepe_b = jnp.zeros((C,), jnp.float32)
        return {'x': x, 'Wqk': Wqk, 'bqk': bqk, 'lepe_w': lepe_w, 'lepe_b': lepe_b}
    _L1_attn_all = _L1_attn_setup()
    _L1_attn_in = {k: v for k, v in _L1_attn_all.items() if k in ('Wqk', 'bqk', 'lepe_w', 'lepe_b')}
    del _L1_attn_all

    def _L1_ffn_setup():
        import jax, jax.numpy as jnp
        import numpy as np
        EPS = 1e-05
        NUM_HEADS = 8
        TOP_K = 2
        CAP_FACTOR = 2

        def layernorm(x, g, b):
            m = jnp.mean(x, axis=-1, keepdims=True)
            v = jnp.var(x, axis=-1, keepdims=True)
            return (x - m) * jax.lax.rsqrt(v + EPS) * g + b
        key = jax.random.key(seed)
        ks = jax.random.split(key, 16)
        B, S, H, E, F = (2, 512, 128, 64, 512)
        s = 0.02
        return {'x': jax.random.normal(ks[0], (B, S, H), jnp.float32), 'ln1_g': jnp.ones((H,), jnp.float32), 'ln1_b': jnp.zeros((H,), jnp.float32), 'wq': jax.random.normal(ks[1], (H, H), jnp.float32) * s, 'wk': jax.random.normal(ks[2], (H, H), jnp.float32) * s, 'wv': jax.random.normal(ks[3], (H, H), jnp.float32) * s, 'wo': jax.random.normal(ks[4], (H, H), jnp.float32) * s, 'ln2_g': jnp.ones((H,), jnp.float32), 'ln2_b': jnp.zeros((H,), jnp.float32), 'wr': jax.random.normal(ks[5], (H, E), jnp.float32) * s, 'w1': jax.random.normal(ks[6], (E, H, F), jnp.float32) * s, 'b1': jnp.zeros((E, F), jnp.float32), 'w2': jax.random.normal(ks[7], (E, F, H), jnp.float32) * s, 'b2': jnp.zeros((E, H), jnp.float32)}
    _L1_ffn_all = _L1_ffn_setup()
    _L1_ffn_in = {k: v for k, v in _L1_ffn_all.items() if k in ('ln1_g', 'ln1_b', 'wq', 'wk', 'wv', 'wo', 'ln2_g', 'ln2_b', 'wr', 'w1', 'b1', 'w2', 'b2')}
    del _L1_ffn_all
    return {'x': x, 'itok_BS_2_50255': itok_BS_2_50255, 'L0_tok_weight': _L0_tok_in['weight'], 'L0_attn_A': _L0_attn_in['A'], 'L0_attn_Bm': _L0_attn_in['Bm'], 'L0_attn_C': _L0_attn_in['C'], 'L0_attn_gamma': _L0_attn_in['gamma'], 'L0_attn_beta': _L0_attn_in['beta'], 'L0_ffn_gfc1_w': _L0_ffn_in['gfc1_w'], 'L0_ffn_gfc1_b': _L0_ffn_in['gfc1_b'], 'L0_ffn_gfc2_w': _L0_ffn_in['gfc2_w'], 'L0_ffn_gfc2_b': _L0_ffn_in['gfc2_b'], 'L0_ffn_W1': _L0_ffn_in['W1'], 'L0_ffn_b1': _L0_ffn_in['b1'], 'L0_ffn_W2': _L0_ffn_in['W2'], 'L0_ffn_b2': _L0_ffn_in['b2'], 'L0_ffn_ln_g': _L0_ffn_in['ln_g'], 'L0_ffn_ln_b': _L0_ffn_in['ln_b'], 'L0_ffn_tv_W1': _L0_ffn_in['tv_W1'], 'L0_ffn_tv_b1': _L0_ffn_in['tv_b1'], 'L0_ffn_tv_W2': _L0_ffn_in['tv_W2'], 'L0_ffn_tv_b2': _L0_ffn_in['tv_b2'], 'L0_ffn_tv_ln_g': _L0_ffn_in['tv_ln_g'], 'L0_ffn_tv_ln_b': _L0_ffn_in['tv_ln_b'], 'L1_attn_Wqk': _L1_attn_in['Wqk'], 'L1_attn_bqk': _L1_attn_in['bqk'], 'L1_attn_lepe_w': _L1_attn_in['lepe_w'], 'L1_attn_lepe_b': _L1_attn_in['lepe_b'], 'L1_ffn_ln1_g': _L1_ffn_in['ln1_g'], 'L1_ffn_ln1_b': _L1_ffn_in['ln1_b'], 'L1_ffn_wq': _L1_ffn_in['wq'], 'L1_ffn_wk': _L1_ffn_in['wk'], 'L1_ffn_wv': _L1_ffn_in['wv'], 'L1_ffn_wo': _L1_ffn_in['wo'], 'L1_ffn_ln2_g': _L1_ffn_in['ln2_g'], 'L1_ffn_ln2_b': _L1_ffn_in['ln2_b'], 'L1_ffn_wr': _L1_ffn_in['wr'], 'L1_ffn_w1': _L1_ffn_in['w1'], 'L1_ffn_b1': _L1_ffn_in['b1'], 'L1_ffn_w2': _L1_ffn_in['w2'], 'L1_ffn_b2': _L1_ffn_in['b2']}

def reference(x, itok_BS_2_50255, L0_tok_weight, L0_attn_A, L0_attn_Bm, L0_attn_C, L0_attn_gamma, L0_attn_beta, L0_ffn_gfc1_w, L0_ffn_gfc1_b, L0_ffn_gfc2_w, L0_ffn_gfc2_b, L0_ffn_W1, L0_ffn_b1, L0_ffn_W2, L0_ffn_b2, L0_ffn_ln_g, L0_ffn_ln_b, L0_ffn_tv_W1, L0_ffn_tv_b1, L0_ffn_tv_W2, L0_ffn_tv_b2, L0_ffn_tv_ln_g, L0_ffn_tv_ln_b, L1_attn_Wqk, L1_attn_bqk, L1_attn_lepe_w, L1_attn_lepe_b, L1_ffn_ln1_g, L1_ffn_ln1_b, L1_ffn_wq, L1_ffn_wk, L1_ffn_wv, L1_ffn_wo, L1_ffn_ln2_g, L1_ffn_ln2_b, L1_ffn_wr, L1_ffn_w1, L1_ffn_b1, L1_ffn_w2, L1_ffn_b2):
    import jax
    import jax.numpy as jnp

    def _L0_tok_ref(input_one, input_two, weight):
        import jax, jax.numpy as jnp
        import numpy as np
        VOCAB = 50257
        EMB_DIM = 128
        BATCH, SEQ = (8, 1024)
        e1 = weight[input_one]
        e2 = weight[input_two]
        same = (input_one == input_two)[..., None]
        return e1 + jnp.where(same, 0.0, e2)

    def _L0_attn_ref(x, A, Bm, C, gamma, beta):
        import jax, jax.numpy as jnp
        import numpy as np
        D_MODEL = 128
        D_STATE = 64
        CLAMP = 1000000.0

        def _layernorm(y, gamma, beta, eps=1e-05):
            mu = jnp.mean(y, axis=-1, keepdims=True)
            var = jnp.mean(jnp.square(y - mu), axis=-1, keepdims=True)
            return (y - mu) * jax.lax.rsqrt(var + eps) * gamma + beta
        Bsz = x.shape[0]
        uB = jnp.einsum('bld,sd->lbs', x, Bm)

        def step(state, uBt):
            state = state @ A.T + uBt
            return (state, state @ C.T)
        s0 = jnp.zeros((Bsz, A.shape[0]), dtype=x.dtype)
        _, y = jax.lax.scan(step, s0, uB)
        y = jnp.transpose(y, (1, 0, 2))
        act = jax.nn.gelu(y, approximate=False)
        out = _layernorm(act, gamma, beta)
        return jnp.nan_to_num(out, nan=0.0, posinf=CLAMP, neginf=-CLAMP)

    def _L0_ffn_ref(hidden_states, gfc1_w, gfc1_b, gfc2_w, gfc2_b, W1, b1, W2, b2, ln_g, ln_b, tv_W1, tv_b1, tv_W2, tv_b2, tv_ln_g, tv_ln_b):
        import jax, jax.numpy as jnp
        import numpy as np
        B, S, D, F, E = (8, 1024, 128, 512, 8)
        INIT_LAMBDA = 0.2
        LN_EPS = 1e-05
        LN_MERGE = 0.03
        x = hidden_states
        gh = jax.nn.relu(jnp.einsum('bsd,hd->bsh', x, gfc1_w) + gfc1_b)
        g = (jnp.einsum('bsh,eh->bse', gh, gfc2_w) + gfc2_b).mean(axis=1)
        W1m = W1 + jnp.einsum('be,efd->bfd', g, tv_W1)
        b1m = b1 + g @ tv_b1
        W2m = W2 + jnp.einsum('be,edf->bdf', g, tv_W2)
        b2m = b2 + g @ tv_b2
        lng = ln_g + LN_MERGE * (tv_ln_g - ln_g).sum(axis=0)
        lnb = ln_b + LN_MERGE * (tv_ln_b - ln_b).sum(axis=0)
        h = jax.nn.relu(jnp.einsum('bsd,bfd->bsf', x, W1m) + b1m[:, None, :])
        out = jnp.einsum('bsf,bdf->bsd', h, W2m) + b2m[:, None, :]
        res = x + out
        mu = res.mean(axis=-1, keepdims=True)
        var = res.var(axis=-1, keepdims=True)
        return (res - mu) * jax.lax.rsqrt(var + LN_EPS) * lng + lnb

    def _L1_attn_ref(x, Wqk, bqk, lepe_w, lepe_b):
        import jax, jax.numpy as jnp
        import numpy as np
        B, N, C, H = (64, 200, 128, 8)
        D = C // H
        BASE = 10000.0

        def _rope(x):
            d = x.shape[-1]
            inv_freq = 1.0 / BASE ** (jnp.arange(0, d, 2, dtype=jnp.float32) / d)
            t = jnp.arange(x.shape[1], dtype=jnp.float32)
            freqs = jnp.outer(t, inv_freq)
            emb = jnp.concatenate([freqs, freqs], axis=-1)
            cos = jnp.cos(emb)[None, :, None, :]
            sin = jnp.sin(emb)[None, :, None, :]
            x1, x2 = (x[..., :d // 2], x[..., d // 2:])
            return x * cos + jnp.concatenate([-x2, x1], axis=-1) * sin
        b, n, c = x.shape
        h, d = (H, C // H)
        qk = x @ Wqk + bqk
        q = jax.nn.elu(qk[..., :c]) + 1.0
        k = jax.nn.elu(qk[..., c:]) + 1.0
        qh = q.reshape(b, n, h, d)
        kh = k.reshape(b, n, h, d)
        vh = x.reshape(b, n, h, d)
        q_r = _rope(qh).transpose(0, 2, 1, 3)
        k_r = _rope(kh).transpose(0, 2, 1, 3)
        qh = qh.transpose(0, 2, 1, 3)
        kh = kh.transpose(0, 2, 1, 3)
        vh = vh.transpose(0, 2, 1, 3)
        kmean = kh.mean(axis=2)
        z = 1.0 / (jnp.einsum('bhnd,bhd->bhn', qh, kmean) + 1e-06)
        scale = n ** (-0.5)
        kv = jnp.einsum('bhnd,bhne->bhde', k_r * scale, vh * scale)
        out = jnp.einsum('bhnd,bhde->bhne', q_r, kv) * z[..., None]
        out = out.transpose(0, 2, 1, 3).reshape(b, n, c)
        v_ncw = x.transpose(0, 2, 1)
        lepe = jax.lax.conv_general_dilated(v_ncw, lepe_w, window_strides=(1,), padding=[(1, 1)], feature_group_count=c, dimension_numbers=('NCH', 'OIH', 'NCH'))
        lepe = lepe + lepe_b[None, :, None]
        return out + lepe.transpose(0, 2, 1)

    def _L1_ffn_ref(x, ln1_g, ln1_b, wq, wk, wv, wo, ln2_g, ln2_b, wr, w1, b1, w2, b2):
        import jax, jax.numpy as jnp
        import numpy as np
        EPS = 1e-05
        NUM_HEADS = 8
        TOP_K = 2
        CAP_FACTOR = 2

        def layernorm(x, g, b):
            m = jnp.mean(x, axis=-1, keepdims=True)
            v = jnp.var(x, axis=-1, keepdims=True)
            return (x - m) * jax.lax.rsqrt(v + EPS) * g + b
        B, S, H = x.shape
        NH = NUM_HEADS
        dh = H // NH
        x1 = layernorm(x, ln1_g, ln1_b)
        q = (x1 @ wq).reshape(B, S, NH, dh)
        k = (x1 @ wk).reshape(B, S, NH, dh)
        v = (x1 @ wv).reshape(B, S, NH, dh)
        scores = jnp.einsum('bqhd,bkhd->bhqk', q, k) * dh ** (-0.5)
        p = jax.nn.softmax(scores, axis=-1)
        attn_out = jnp.einsum('bhqk,bkhd->bqhd', p, v).reshape(B, S, H) @ wo
        x = x + attn_out
        x2 = layernorm(x, ln2_g, ln2_b).reshape(B * S, H)
        T = B * S
        E = wr.shape[1]
        C = CAP_FACTOR * (T * TOP_K // E)
        probs = jax.nn.softmax(x2 @ wr, axis=-1)
        gate_v, gate_i = jax.lax.top_k(probs, TOP_K)
        gate_v = gate_v / jnp.sum(gate_v, axis=-1, keepdims=True)
        ef = gate_i.reshape(-1)
        gf = gate_v.reshape(-1)
        oh = jax.nn.one_hot(ef, E, dtype=x2.dtype)
        pos = jnp.sum((jnp.cumsum(oh, axis=0) - oh) * oh, axis=1).astype(jnp.int32)
        keep = (pos < C).astype(x2.dtype)
        posc = jnp.minimum(pos, C - 1)
        tok = jnp.repeat(x2, TOP_K, axis=0) * keep[:, None]
        buf = jnp.zeros((E, C, H), x2.dtype).at[ef, posc].add(tok)
        h = jax.nn.gelu(jnp.einsum('ech,ehf->ecf', buf, w1) + b1[:, None, :])
        y = jnp.einsum('ecf,efh->ech', h, w2) + b2[:, None, :]
        ys = y[ef, posc] * (gf * keep)[:, None]
        moe_out = ys.reshape(T, TOP_K, H).sum(axis=1).reshape(B, S, H)
        return x + moe_out
    h = _L0_tok_ref(x, itok_BS_2_50255, L0_tok_weight)
    h = h + _L0_attn_ref(_layernorm(h, axis=-1), L0_attn_A, L0_attn_Bm, L0_attn_C, L0_attn_gamma, L0_attn_beta)
    h = h + _L0_ffn_ref(_layernorm(h, axis=-1), L0_ffn_gfc1_w, L0_ffn_gfc1_b, L0_ffn_gfc2_w, L0_ffn_gfc2_b, L0_ffn_W1, L0_ffn_b1, L0_ffn_W2, L0_ffn_b2, L0_ffn_ln_g, L0_ffn_ln_b, L0_ffn_tv_W1, L0_ffn_tv_b1, L0_ffn_tv_W2, L0_ffn_tv_b2, L0_ffn_tv_ln_g, L0_ffn_tv_ln_b)
    h = h + _L1_attn_ref(_layernorm(h, axis=-1), L1_attn_Wqk, L1_attn_bqk, L1_attn_lepe_w, L1_attn_lepe_b)
    h = h + _L1_ffn_ref(_layernorm(h, axis=-1), L1_ffn_ln1_g, L1_ffn_ln1_b, L1_ffn_wq, L1_ffn_wk, L1_ffn_wv, L1_ffn_wo, L1_ffn_ln2_g, L1_ffn_ln2_b, L1_ffn_wr, L1_ffn_w1, L1_ffn_b1, L1_ffn_w2, L1_ffn_b2)
    return h

_drawn_inputs = setup_inputs


def setup_inputs(seed=0):
    import zlib

    import numpy as np

    out = dict(_drawn_inputs(seed))
    spreads = {'L0_attn_gamma': (1.0, 0.2),
     'L0_attn_beta': (0.0, 0.1),
     'L0_ffn_gfc1_b': (0.0, 0.8),
     'L0_ffn_gfc2_b': (0.20000000298023224, 0.6),
     'L0_ffn_b1': (0.0, 0.621),
     'L0_ffn_b2': (0.0, 0.1),
     'L0_ffn_ln_g': (1.0, 0.2),
     'L0_ffn_ln_b': (0.0, 0.1),
     'L1_attn_bqk': (0.0, 0.8),
     'L1_attn_lepe_b': (0.0, 0.1),
     'L1_ffn_ln1_g': (1.0, 0.6),
     'L1_ffn_ln1_b': (0.0, 0.8),
     'L1_ffn_ln2_g': (1.0, 0.6),
     'L1_ffn_ln2_b': (0.0, 0.712),
     'L1_ffn_b1': (0.0, 0.8),
     'L1_ffn_b2': (0.0, 0.395)}
    factors = {'L0_ffn_gfc1_w': 8.0,
     'L0_ffn_gfc2_w': 8.0,
     'L0_ffn_tv_W1': 4.231,
     'L0_ffn_tv_b1': 8.0,
     'L0_ffn_tv_W2': 3.703,
     'L0_ffn_tv_b2': 8.0,
     'L0_ffn_tv_ln_g': 8.0,
     'L0_ffn_tv_ln_b': 8.0,
     'L1_attn_Wqk': 8.0,
     'L1_ffn_wq': 8.0,
     'L1_ffn_wk': 8.0,
     'L1_ffn_wv': 8.0,
     'L1_ffn_wo': 8.0,
     'L1_ffn_w1': 5.126,
     'L1_ffn_w2': 4.631}
    for name, (base, spread) in spreads.items():
        noise = np.random.default_rng([zlib.crc32(name.encode()), seed]).standard_normal(out[name].shape)
        drawn = base * np.exp(spread * noise) if base else spread * noise
        out[name] = jnp.asarray(drawn.astype(out[name].dtype))
    for name, factor in factors.items():
        out[name] = (out[name] * factor).astype(out[name].dtype)
    return out
```

```python
from contextlib import ExitStack

import numpy as np
import concourse.bass as bass
from concourse import mybir

F32 = mybir.dt.float32
BF16 = mybir.dt.bfloat16
I32 = mybir.dt.int32
U32 = mybir.dt.uint32
ALU = mybir.AluOpType
ACT = mybir.ActivationFunctionType
AXX = mybir.AxisListType.X

P = 128
B, S, H = 4, 1024, 128
T = B * S
NT = T // P
TB = S // P
GT = 4
NG = NT // GT
GC = GT * P
EPS = 1e-5
RSQRT_MAGIC = 1597463007.0
D_STATE = 64
CHUNK = 16
NC = S // CHUNK
CLAMP = 1e6
FLT_MAX = 3.4028234e38
FFN = 512
NE0 = 8
NM = FFN // P
NH, DH = 8, 16
E1 = 64
CAP = 2 * (T * 2 // E1)
HALVES = CAP // P
ROW = H + 2


class Chain:

    def __init__(self, eng, sem):
        self.eng, self.sem, self.n = eng, sem, 0

    def step(self, ins):
        self.n += 1
        ins.then_inc(self.sem, 1)
        return ins

    def wait(self):
        self.eng.wait_ge(self.sem, self.n)

    def do(self, ins):
        self.step(ins)
        self.wait()


class Norm:

    def __init__(self, stage, tag, src, xn, banks, copy_out, ident, again=None):
        self.src, self.xn, self.banks, self.copy_out, self.ident = src, xn, banks, copy_out, ident
        self.again = again
        if again is not None:
            self.rstd2 = stage.sb(f"{tag}_rstd2", [P, NT], F32)
            self.shift2 = stage.sb(f"{tag}_shift2", [P, NT], F32)
        self.stats = stage.sb(f"{tag}_stats", [P, NT, 6], F32)
        self.mv = stage.sb(f"{tag}_meanvar", [P, NT, 2], F32)
        self.var = stage.sb(f"{tag}_var", [P, NT], F32)
        self.rstd = stage.sb(f"{tag}_rstd", [P, NT], F32)
        self.shift = stage.sb(f"{tag}_shift", [P, NT], F32)
        self.stats_ready = stage.sem(f"{tag}_stats_ready")
        self.xn_ready = stage.sem(f"{tag}_xn_ready")
        self.turned = stage.sem(f"{tag}_turned")
        self.x_t_ready = stage.sem(f"{tag}_x_t_ready")

    def dve(self, dve, chain, g):
        if g % 2:
            return
        tiles = range(GT * g, GT * (g + 2))
        for n in tiles:
            chain.step(dve.bn_stats(self.stats[:, n, :], self.src(n)))
        chain.wait()
        for n in tiles:
            chain.step(dve.bn_aggr(self.mv[:, n, :], self.stats[:, n, :]))
        chain.wait()
        cols = slice(tiles[0], tiles[-1] + 1)
        mean, var = self.mv[:, cols, 0], self.mv[:, cols, 1]
        r, shift = self.rstd[:, cols], self.shift[:, cols]
        chain.do(dve.tensor_scalar(self.var[:, cols], var, EPS, None, ALU.add))
        self.rsqrt(dve, chain, r, self.var[:, cols], shift)
        if self.again is None:
            dve.scalar_tensor_tensor(shift, mean, -1.0, r, ALU.mult, ALU.mult).then_inc(self.stats_ready, 2)
            return
        r2, shift2 = self.rstd2[:, cols], self.shift2[:, cols]
        chain.step(dve.scalar_tensor_tensor(shift, mean, -1.0, r, ALU.mult, ALU.mult))
        chain.do(dve.tensor_tensor(shift2, r, r, ALU.mult))
        chain.do(dve.tensor_tensor(shift2, shift2, var, ALU.mult))
        chain.do(dve.tensor_scalar(self.var[:, cols], shift2, EPS, None, ALU.add))
        self.rsqrt(dve, chain, r2, self.var[:, cols], shift2)
        chain.do(dve.tensor_tensor(shift2, shift, r2, ALU.mult))
        dve.tensor_tensor(r2, r2, r, ALU.mult).then_inc(self.stats_ready, 2)

    def rsqrt(self, dve, chain, r, var, sq):
        chain.do(dve.tensor_scalar(r.bitcast(I32), var.bitcast(I32), -0.5, RSQRT_MAGIC, ALU.mult, ALU.add))
        for _ in range(3):
            chain.do(dve.tensor_tensor(sq, r, r, ALU.mult))
            chain.do(dve.scalar_tensor_tensor(sq, sq, -0.5, var, ALU.mult, ALU.mult))
            chain.do(dve.scalar_tensor_tensor(r, sq, 1.5, r, ALU.add, ALU.mult))

    def act_apply(self, act, g):
        act.wait_ge(self.stats_ready, g + 1)
        for n in range(GT * g, GT * g + GT):
            last = act.activation(self.xn(n), self.src(n), ACT.Identity,
                                  bias=self.shift[:, n:n + 1], scale=self.rstd[:, n:n + 1])
        if self.again is not None:
            if g >= 2:
                act.wait_ge(self.turned, g - 1)
            for n in range(GT * g, GT * g + GT):
                last = act.activation(self.again(n), self.src(n), ACT.Identity,
                                      bias=self.shift2[:, n:n + 1], scale=self.rstd2[:, n:n + 1])
        last.then_inc(self.xn_ready, 1)

    def pe(self, pe, g):
        pe.wait_ge(self.xn_ready, g + 1)
        if g >= 2:
            pe.wait_ge(self.x_t_ready, g - 1)
        bank = self.banks[g % 2]
        for j in range(GT):
            last = pe.transpose(bank[:, j * P:(j + 1) * P], (self.again or self.xn)(GT * g + j), self.ident[:])
        last.then_inc(self.turned, 1)

    def act_copy(self, act, g):
        act.wait_ge(self.turned, g + 1)
        self.copy_out(act, g, self.banks[g % 2]).then_inc(self.x_t_ready, 1)


def tile_of(t):
    return lambda n: t[:, n, :]


class Stage:

    def __init__(self, nc, k, tag, recycle=False):
        self.nc, self.tag, self.ctx, self.recycle, self.sems = nc, tag, ExitStack(), recycle, []

    def __enter__(self):
        self.ctx.__enter__()
        return self

    def __exit__(self, *exc):
        if self.recycle and exc[0] is None:
            self.nc.clear_and_free_semaphores(self.sems)
            self.nc.all_engine_barrier()
        return self.ctx.__exit__(*exc)

    def sb(self, name, shape, dt):
        return self.ctx.enter_context(self.nc.sbuf_tensor(self.tag + name, shape, dt))

    def sem(self, name):
        self.sems.append(self.nc.alloc_semaphore(name=self.tag + name))
        return self.sems[-1]


def embed_and_scan(nc, d, k):
    hres = k.hres
    with Stage(nc, k, "scan_", recycle=True) as st:
        sb, sem = st.sb, st.sem
        ids = sb("ids", [P, 2, NT], I32)
        differ = sb("differ", [P, NT], F32)
        e1 = sb("e1", [P, NT, H], F32)
        e2 = sb("e2", [P, NT, H], F32)
        x_t = sb("x_t", [P, T], F32)
        xs = sb("xs", [D_STATE, T], F32)
        q_pow = sb("q_pow", [D_STATE, CHUNK, D_STATE], F32)
        p_pow = sb("p_pow", [D_STATE, 2, D_STATE], F32)
        q_big = sb("q_big", [D_STATE, 6, D_STATE], F32)
        bm_t = sb("bm_t", [P, D_STATE], F32)
        c_t = sb("c_t", [D_STATE, H], F32)
        carry = sb("carry", [D_STATE, 2, B, NC + 1], F32)
        gamma = sb("gamma", [P, H], F32)
        beta = sb("beta", [P, H], F32)
        gel = sb("gel", [P, NT, H], F32)
        yn = sb("yn", [P, NT, H], F32)
        ya = sb("ya", [P, 2, GC], F32)
        yb = sb("yb", [P, 2, GC], F32)
        yc = sb("yc", [P, 2, GC], F32)
        yd = sb("yd", [P, 2, GC], F32)
        finite = sb("finite", [P, 2, GC], F32)
        known = sb("known", [P, 2, GC], F32)

        ids_in, small_in = sem("ids_in"), sem("small_in")
        gathered = [sem(f"gathered{g}") for g in range(NG)]
        dve_chain = sem("dve_chain")
        h0_ready = sem("h0_ready")
        pow_done, pow_kept = sem("pow_done"), sem("pow_kept")
        step_done = [sem(f"step_done{s}") for s in range(2)]
        step_kept = [sem(f"step_kept{s}") for s in range(2)]
        carry_done, carry_kept = sem("carry_done"), sem("carry_kept")
        fix_done, fix_kept = sem("fix_done"), sem("fix_kept")
        y_done, y_kept = sem("y_done"), sem("y_kept")
        st2_ready, yn_ready, scaled, guarded = sem("st2_ready"), sem("yn_ready"), sem("scaled"), sem("guarded")
        pool_chain, h1_ready = sem("pool_chain"), sem("h1_ready")
        norm = Norm(st, "n0", tile_of(hres), tile_of(e1), [k.ps[0], k.ps[1]],
                    lambda act, g, bank: act.activation(x_t[:, g * GC:(g + 1) * GC], bank[:], ACT.Copy), k.ident)
        norm2 = Norm(st, "n1", tile_of(gel), tile_of(yn), None, None, None)

        def at_pos(t, i, s):
            half = T // 2
            return t[:, s * half:(s + 1) * half].rearrange("c (m i) -> c i m", i=CHUNK)[:, i, :]

        with nc.Block() as block:
            @block.sync
            def _(sp):
                sp.dma_start(ids[:], d["ids"]).then_inc(ids_in, 16)
                for dst, src in ((k.ident[:], d["ident"]), (bm_t[:], d["bm_t"]), (c_t[:], d["c_t"]),
                                 (q_pow[:, 0, :], d["a_t"]), (p_pow[:, 0, :], d["a"]),
                                 (gamma[:], d["gamma_b"]), (beta[:], d["beta_b"])):
                    sp.dma_start(dst, src).then_inc(small_in, 16)

            @block.gpsimd
            def _(pool):
                pool.wait_ge(ids_in, 16)
                for n in range(NT):
                    for j, e in ((0, e1), (1, e2)):
                        pool.indirect_dma_start(e[:, n, :], None, d["table"],
                                                bass.IndirectOffsetOnAxis(ap=ids[:, j, n:n + 1], axis=0)
                                                ).then_inc(gathered[n // GT], 16)
                chain = Chain(pool, pool_chain)
                beta4 = beta[:, None, :].to_broadcast([P, GT, H])
                for g in range(NG):
                    s = g % 2
                    pool.wait_ge(scaled, g + 1)
                    if g >= 2:
                        pool.wait_ge(h1_ready, g - 1)
                    v = yb[:, s, :]
                    chain.do(pool.tensor_tensor(v.rearrange("p (n c) -> p n c", c=H),
                                                ya[:, s, :].rearrange("p (n c) -> p n c", c=H), beta4, ALU.add))
                    pool.tensor_scalar(yc[:, s, :], v, -CLAMP, CLAMP, ALU.max, ALU.min).then_inc(guarded, 1)
                    pool.tensor_scalar(finite[:, s, :], v, 0.0, 0.0, ALU.mult, ALU.is_equal).then_inc(guarded, 1)
                    pool.memset(yd[:, s, :], 0.0).then_inc(guarded, 1)

            @block.vector
            def _(dve):
                chain = Chain(dve, dve_chain)
                dve.wait_ge(ids_in, 16)
                chain.do(dve.tensor_tensor(differ[:], ids[:, 0, :], ids[:, 1, :], ALU.not_equal))
                dve.wait_ge(small_in, 16 * 7)
                chain.do(dve.memset(carry[:], 0.0))
                n = 0
                for j in range(9):
                    dve.wait_ge(pow_done, 2 * (j + 1))
                    a = 1 << j
                    if a < CHUNK:
                        dve.tensor_copy(q_pow[:, a:2 * a, :], k.ps[2][0:D_STATE, 0:a * D_STATE].rearrange("s (m t) -> s m t", t=D_STATE)).then_inc(pow_kept, 1)
                    else:
                        dve.tensor_copy(q_big[:, j - 3, :], k.ps[2][0:D_STATE, 0:D_STATE]).then_inc(pow_kept, 1)
                    if j == 3:
                        chain.do(dve.tensor_copy(q_big[:, 0, :], k.ps[2][0:D_STATE, 7 * D_STATE:8 * D_STATE]))
                    dve.tensor_copy(p_pow[:, (j + 1) % 2, :], k.ps[3][0:D_STATE, 0:D_STATE]).then_inc(pow_kept, 1)
                for g in range(NG):
                    dve.wait_ge(gathered[g], 16 * 2 * GT)
                    for n in range(GT * g, GT * g + GT):
                        chain.step(dve.scalar_tensor_tensor(hres[:, n, :], e2[:, n, :], differ[:, n:n + 1],
                                                            e1[:, n, :], ALU.mult, ALU.add))
                    chain.wait()
                    if g % 2:
                        norm.dve(dve, chain, g - 1)
                for i in range(CHUNK):
                    dve.wait_ge(step_done[0], i + 1)
                    dve.tensor_copy(at_pos(xs, i, 0), k.ps[i % 2][0:D_STATE, 0:P]).then_inc(step_kept[0], 1)
                dve.wait_ge(step_kept[0], CHUNK)
                dve.wait_ge(step_kept[1], CHUNK)
                fin = xs[:].rearrange("s (b c i) -> s b c i", b=B, i=CHUNK)[:, :, :, CHUNK - 1]
                chain.do(dve.tensor_copy(carry[:, 0, :, 1:NC + 1], fin))
                dve.sem_inc(carry_kept, 1)
                for j in range(6):
                    sh = 1 << j
                    old, new = carry[:, j % 2], carry[:, (j + 1) % 2]
                    dve.wait_ge(carry_done, j + 1)
                    acc = k.ps[4 + j % 2][0:D_STATE, 0:B * (NC - sh)].rearrange("s (b c) -> s b c", b=B)
                    chain.step(dve.tensor_copy(new[:, :, 1:1 + sh], old[:, :, 1:1 + sh]))
                    chain.step(dve.tensor_tensor(new[:, :, 1 + sh:], acc, old[:, :, 1 + sh:], ALU.add))
                    chain.wait()
                    dve.sem_inc(carry_kept, 1)
                for i in range(CHUNK):
                    dve.wait_ge(fix_done, i + 1)
                    v = xs[:].rearrange("s (m i) -> s i m", i=CHUNK)[:, i, :]
                    dve.tensor_tensor(v, k.ps[i % 4][0:D_STATE, 0:B * NC], v, ALU.add).then_inc(fix_kept, 1)
                gamma4 = gamma[:, None, :].to_broadcast([P, GT, H])

                def stats(g):
                    if g % 2 == 0:
                        dve.wait_ge(y_kept, g + 2)
                    norm2.dve(dve, chain, g)

                def scale(g):
                    dve.wait_ge(norm2.xn_ready, g + 1)
                    if g >= 2:
                        dve.wait_ge(guarded, 3 * (g - 1))
                    dve.tensor_tensor(ya[:, g % 2, :].rearrange("p (n c) -> p n c", c=H),
                                      yn[:, GT * g:GT * g + GT, :], gamma4, ALU.mult).then_inc(scaled, 1)

                def guard(g):
                    s = g % 2
                    dve.wait_ge(guarded, 3 * (g + 1))
                    chain.do(dve.tensor_tensor(known[:, s, :], yb[:, s, :], yb[:, s, :], ALU.is_equal))
                    chain.do(dve.copy_predicated(yd[:, s, :], known[:, s, :].bitcast(U32), yc[:, s, :]))
                    chain.do(dve.copy_predicated(yd[:, s, :], finite[:, s, :].bitcast(U32), yb[:, s, :]))
                    hv = hres[:, GT * g:GT * g + GT, :]
                    dve.tensor_tensor(hv, hv, yd[:, s, :].rearrange("p (n c) -> p n c", c=H), ALU.add).then_inc(h1_ready, 1)

                for g in range(NG + 2):
                    if g < NG:
                        stats(g)
                    if 1 <= g <= NG:
                        scale(g - 1)
                    if g >= 2:
                        guard(g - 2)
                dve.wait_ge(h1_ready, NG)

            @block.scalar
            def _(act):
                act.wait_ge(small_in, 16 * 7)
                for g in range(NG + 1):
                    if g < NG:
                        norm.act_apply(act, g)
                    if g >= 1:
                        norm.act_copy(act, g - 1)
                for i in range(CHUNK):
                    act.wait_ge(step_done[1], i + 1)
                    act.activation(at_pos(xs, i, 1), k.ps[2 + i % 2][0:D_STATE, 0:P], ACT.Copy).then_inc(step_kept[1], 1)

                def gelu(g):
                    act.wait_ge(y_done, g + 1)
                    act.activation(gel[:, GT * g:GT * g + GT, :].rearrange("p n c -> p (n c)"), k.ps[4 + g % 4][:],
                                   ACT.Gelu).then_inc(y_kept, 1)

                for g in range(NG):
                    gelu(g)
                for g in range(NG):
                    norm2.act_apply(act, g)

            @block.tensor
            def _(pe):
                pe.wait_ge(small_in, 16 * 7)
                for j in range(9):
                    a = 1 << j
                    if j:
                        pe.wait_ge(pow_kept, 2 * j)
                    p_a = p_pow[:, j % 2, :]
                    if a < CHUNK:
                        pe.matmul(k.ps[2][0:D_STATE, 0:a * D_STATE], p_a, q_pow[:, 0:a, :].rearrange("s m t -> s (m t)"),
                                  start=True, stop=True).then_inc(pow_done, 1)
                        q_a = q_pow[:, a - 1, :]
                    else:
                        q_a = q_big[:, j - 4, :]
                        if j == 4:
                            pe.wait_ge(dve_chain, 3)
                        pe.matmul(k.ps[2][0:D_STATE, 0:D_STATE], p_a, q_a, start=True, stop=True).then_inc(pow_done, 1)
                    pe.matmul(k.ps[3][0:D_STATE, 0:D_STATE], q_a, p_a, start=True, stop=True).then_inc(pow_done, 1)
                for g in range(NG):
                    norm.pe(pe, g)
                pe.wait_ge(norm.x_t_ready, NG)
                pe.wait_ge(pow_kept, 18)
                for i in range(CHUNK):
                    for s in range(2):
                        out = k.ps[2 * s + i % 2][0:D_STATE, 0:P]
                        if i >= 2:
                            pe.wait_ge(step_kept[s], i - 1)
                        mm = pe.matmul(out, bm_t[:], at_pos(x_t, i, s), start=True, stop=(i == 0))
                        if i >= 1:
                            pe.wait_ge(step_kept[s], i)
                            mm = pe.matmul(out, q_pow[:, 0, :], at_pos(xs, i - 1, s), start=False, stop=True)
                        mm.then_inc(step_done[s], 1)
                for j in range(6):
                    sh = 1 << j
                    pe.wait_ge(carry_kept, j + 1)
                    pe.matmul(k.ps[4 + j % 2][0:D_STATE, 0:B * (NC - sh)].rearrange("s (b c) -> s b c", b=B),
                              q_big[:, j, :], carry[:, j % 2, :, 1:1 + NC - sh], start=True, stop=True).then_inc(carry_done, 1)
                pe.wait_ge(carry_kept, 7)
                for i in range(CHUNK):
                    if i >= 4:
                        pe.wait_ge(fix_kept, i - 3)
                    pe.matmul(k.ps[i % 4][0:D_STATE, 0:B * NC].rearrange("s (b c) -> s b c", b=B), q_pow[:, i, :],
                              carry[:, 0, :, 0:NC], start=True, stop=True).then_inc(fix_done, 1)
                pe.wait_ge(fix_kept, CHUNK)
                for g in range(NG):
                    if g >= 4:
                        pe.wait_ge(y_kept, g - 3)
                    for j in range(GT):
                        n = GT * g + j
                        last = pe.matmul(k.ps[4 + g % 4][:, j * P:(j + 1) * P], xs[:, n * P:(n + 1) * P], c_t[:],
                                         start=True, stop=True)
                    last.then_inc(y_done, 1)


def task_ffn(nc, d, k):
    hres = k.hres
    R = P // NE0
    G1, G2 = FFN // R, H // R
    K9 = NE0 + 1
    with Stage(nc, k, "ffn_") as st:
        sb, sem = st.sb, st.sem
        xn = sb("xn", [P, NT, H], F32)
        x_t = sb("x_t", [P, T], F32)
        gfc1_t = sb("gfc1_t", [P, H], F32)
        gfc1_b = sb("gfc1_b", [P, 1], F32)
        gfc2_rep = sb("gfc2_rep", [P, NE0, R], F32)
        gfc2_b_rep = sb("gfc2_b_rep", [P, 1], F32)
        gfc2_t = sb("gfc2_t", [P, NE0], F32)
        gfc2_b = sb("gfc2_b", [NE0, 1], F32)
        delta = sb("delta", [P, R], F32)
        tv_w1 = sb("tv_w1", [P, G1, H], F32)
        tv_w2 = sb("tv_w2", [P, G2, FFN], F32)
        w1_t = sb("w1_t", [P, FFN], F32)
        w2_t = sb("w2_t", [P, NM, H], F32)
        tv_b1 = sb("tv_b1", [K9, FFN], F32)
        tv_b2 = sb("tv_b2", [K9, H], F32)
        tv_ln = sb("tv_ln", [K9, 2 * H], F32)
        merge_w = sb("merge_w", [K9, P], F32)
        gate_out = sb("gate_out", [P, 2, GC], F32)
        sums = sb("sums", [P, NG], F32)
        mean = sb("mean", [P, B], F32)
        g_rep = sb("g_rep", [P, B], F32)
        g9 = sb("g9", [K9, B], F32)
        g9_wide = sb("g9_wide", [K9, B, P], F32)
        spread = sb("spread", [P, B, R], F32)
        w1m = sb("w1m", [P, B, FFN], F32)
        w2m = sb("w2m", [P, NM, B, H], F32)
        b1m = sb("b1m", [P, NM, B], F32)
        ln_gb = sb("ln_gb", [P, 2 * H], F32)
        hid = sb("hid", [P, 2, NM, GC], F32)
        rn = sb("rn", [P, NT, H], F32)

        gate_in, merge_in = sem("gate_in"), sem("merge_in")
        dve_chain = sem("dve_chain")
        gate_done, gate_summed = sem("gate_done"), sem("gate_summed")
        mean_ready, g_done, g_ready = sem("mean_ready"), sem("g_done"), sem("g_ready")
        merged, merge_kept = sem("merged"), sem("merge_kept")
        bias_done, bias_kept = sem("bias_done"), sem("bias_kept")
        hid_done = sem("hid_done")
        hid_act, hid_dve = sem("hid_act"), sem("hid_dve")
        res_done = sem("res_done")
        lnb_added, h2_ready = sem("lnb_added"), sem("h2_ready")
        norm = Norm(st, "n0", tile_of(hres), tile_of(xn), [k.ps[0], k.ps[1]],
                    lambda act, g, bank: act.activation(x_t[:, g * GC:(g + 1) * GC], bank[:], ACT.Copy), k.ident)
        res = lambda n: k.ps[4 + n // GT % 4][:, n % GT * P:(n % GT + 1) * P]
        norm2 = Norm(st, "n1", res, tile_of(rn), None, None, None)
        gate_loads = ((gfc1_t[:], "gfc1_t"), (gfc1_b[:], "gfc1_b"), (gfc2_rep[:], "gfc2_rep"),
                      (gfc2_b_rep[:], "gfc2_b_rep"), (gfc2_t[:], "gfc2_t"), (gfc2_b[:], "gfc2_b"), (delta[:], "delta"))
        merge_loads = ((tv_w1[:], "tv_w1"), (tv_w2[:], "tv_w2"), (w1_t[:], "w1_t"), (w2_t[:], "w2_t"),
                       (tv_b1[:], "tv_b1"), (tv_b2[:], "tv_b2"), (tv_ln[:], "tv_ln"), (merge_w[:], "merge_w"))

        with nc.Block() as block:
            @block.sync
            def _(sp):
                for dst, src in gate_loads:
                    sp.dma_start(dst, d[src]).then_inc(gate_in, 16)
                for dst, src in merge_loads:
                    sp.dma_start(dst, d[src]).then_inc(merge_in, 16)

            @block.gpsimd
            def _(pool):
                lnb4 = ln_gb[:, None, H:2 * H].to_broadcast([P, GT, H])
                pool.wait_ge(bias_kept, 2)
                for g in range(NG):
                    pool.wait_ge(norm.xn_ready, g + 1)
                    hv = hres[:, GT * g:GT * g + GT, :]
                    pool.tensor_tensor(hv, hv, lnb4, ALU.add).then_inc(lnb_added, 1)

            @block.vector
            def _(dve):
                chain = Chain(dve, dve_chain)
                chain.step(dve.memset(g9[:], 1.0))
                for g in range(NG):
                    norm.dve(dve, chain, g)
                dve.wait_ge(gate_summed, NG)
                pair = sums[:].rearrange("p (b t) -> p b t", t=2)
                chain.do(dve.tensor_tensor(mean[:], pair[:, :, 0], pair[:, :, 1], ALU.add))
                chain.do(dve.tensor_scalar(mean[:], mean[:], 1.0 / S, None, ALU.mult))
                dve.sem_inc(mean_ready, 1)
                dve.wait_ge(gate_in, 16 * len(gate_loads))
                dve.wait_ge(g_done, 1)
                chain.do(dve.tensor_scalar(g_rep[:], k.ps[4][:, 0:B], gfc2_b_rep[:, 0:1], None, ALU.add))
                chain.do(dve.tensor_scalar(g9[0:NE0, :], k.ps[4][0:NE0, B:2 * B], gfc2_b[:, 0:1], None, ALU.add))
                for b in range(B):
                    chain.step(dve.tensor_scalar(spread[:, b, :], delta[:], g_rep[:, b:b + 1], None, ALU.mult))
                chain.do(dve.tensor_copy(g9_wide[:], g9[:, :, None].to_broadcast([K9, B, P])))
                dve.sem_inc(g_ready, 1)
                dve.wait_ge(merge_in, 16 * len(merge_loads))
                for q in range(4):
                    dve.wait_ge(merged, q + 1)
                    acc = k.ps[q][:].rearrange("p (j b r) -> p b r j", j=8, b=B)
                    out = w1m[:].rearrange("p b (r g) -> p b r g", g=G1)[:, :, :, 8 * q:8 * q + 8]
                    base = w1_t[:].rearrange("p (r g) -> p r g", g=G1)[:, None, :, 8 * q:8 * q + 8]
                    for b in range(B):
                        last = dve.tensor_tensor(out[:, b], acc[:, b], base[:, 0], ALU.add)
                    last.then_inc(merge_kept, 1)
                for m in range(NM):
                    dve.wait_ge(merged, 4 + m + 1)
                    acc = k.ps[4 + m][:].rearrange("p (j b r) -> p b r j", j=G2, b=B)
                    for b in range(B):
                        last = dve.tensor_tensor(w2m[:, m, b, :].rearrange("p (r g) -> p r g", g=G2), acc[:, b],
                                                 w2_t[:, m, :].rearrange("p (r g) -> p r g", g=G2), ALU.add)
                    last.then_inc(merge_kept, 1)
                dve.wait_ge(bias_done, 1)
                dve.tensor_copy(b1m[:].rearrange("p m b -> p (m b)"), k.ps[0][:, 0:NM * B]).then_inc(bias_kept, 1)
                dve.tensor_copy(ln_gb[:], k.ps[1][:, 0:2 * H]).then_inc(bias_kept, 1)
                dve.wait_ge(bias_kept, 2)
                lng4 = ln_gb[:, None, 0:H].to_broadcast([P, GT, H])

                def hidden(u):
                    for m in (2, 3):
                        dve.wait_ge(hid_done, NM * u + m + 1)
                        if u >= 2:
                            dve.wait_ge(res_done, u - 1)
                        dve.tensor_scalar(hid[:, u % 2, m, :], k.ps[m][:], b1m[:, m, u // 2:u // 2 + 1], 0.0,
                                          ALU.add, ALU.max).then_inc(hid_dve, 1)

                def finish(g):
                    dve.wait_ge(norm2.xn_ready, g + 1)
                    rv = rn[:, GT * g:GT * g + GT, :]
                    hv = hres[:, GT * g:GT * g + GT, :]
                    chain.do(dve.tensor_tensor(rv, rv, lng4, ALU.mult))
                    dve.wait_ge(lnb_added, g + 1)
                    dve.tensor_tensor(hv, hv, rv, ALU.add).then_inc(h2_ready, 1)

                for u in range(NG):
                    hidden(u)
                    if u % 2 == 0 and u >= 2:
                        dve.wait_ge(res_done, u)
                        norm2.dve(dve, chain, u - 2)
                    if u >= 4:
                        finish(u - 4)
                dve.wait_ge(res_done, NG)
                norm2.dve(dve, chain, NG - 2)
                for g in range(NG - 4, NG):
                    finish(g)
                dve.wait_ge(h2_ready, NG)

            @block.scalar
            def _(act):
                def gate(g):
                    act.wait_ge(gate_done, g + 1)
                    if g >= 2:
                        act.wait_ge(gate_summed, g - 1)
                    act.activation(gate_out[:, g % 2, :], k.ps[2 + g % 2][:], ACT.Relu, bias=gfc1_b[:, 0:1],
                                   accum_out=sums[:, g:g + 1]).then_inc(gate_summed, 1)

                act.wait_ge(gate_in, 16 * len(gate_loads))
                for g in range(NG + 2):
                    if g < NG:
                        norm.act_apply(act, g)
                    if 1 <= g <= NG:
                        norm.act_copy(act, g - 1)
                    if g >= 2:
                        gate(g - 2)
                act.wait_ge(bias_kept, 1)

                def hidden(u):
                    for m in (0, 1):
                        act.wait_ge(hid_done, NM * u + m + 1)
                        if u >= 2:
                            act.wait_ge(res_done, u - 1)
                        act.activation(hid[:, u % 2, m, :], k.ps[m][:], ACT.Relu,
                                       bias=b1m[:, m, u // 2:u // 2 + 1]).then_inc(hid_act, 1)

                for u in range(NG):
                    hidden(u)
                    if u >= 3:
                        norm2.act_apply(act, u - 3)
                for g in range(NG - 3, NG):
                    norm2.act_apply(act, g)

            @block.tensor
            def _(pe):
                def gate(g):
                    pe.wait_ge(norm.x_t_ready, g + 1)
                    if g >= 2:
                        pe.wait_ge(gate_summed, g - 1)
                    pe.matmul(k.ps[2 + g % 2][:], gfc1_t[:], x_t[:, g * GC:(g + 1) * GC], start=True,
                              stop=True).then_inc(gate_done, 1)

                pe.wait_ge(gate_in, 16 * len(gate_loads))
                for g in range(NG + 1):
                    if g < NG:
                        norm.pe(pe, g)
                    if g >= 1:
                        gate(g - 1)
                pe.wait_ge(mean_ready, 1)
                pe.matmul(k.ps[4][:, 0:B], gfc2_rep[:].rearrange("p e r -> p (e r)"), mean[:], start=True, stop=True)
                pe.matmul(k.ps[4][0:NE0, B:2 * B], gfc2_t[:], mean[:], start=True, stop=True).then_inc(g_done, 1)
                pe.wait_ge(g_ready, 1)
                pe.wait_ge(merge_in, 16 * len(merge_loads))
                pe.wait_ge(gate_summed, NG)
                g_cols = spread[:].rearrange("p b r -> p (b r)")
                for q in range(4):
                    for j in range(8):
                        last = pe.matmul(k.ps[q][:, j * B * R:(j + 1) * B * R], tv_w1[:, 8 * q + j, :], g_cols,
                                         start=True, stop=True)
                    last.then_inc(merged, 1)
                for m in range(NM):
                    for j in range(G2):
                        last = pe.matmul(k.ps[4 + m][:, j * B * R:(j + 1) * B * R],
                                         tv_w2[:, j, m * P:(m + 1) * P], g_cols, start=True, stop=True)
                    last.then_inc(merged, 1)
                pe.wait_ge(merge_kept, 2)
                for m in range(NM):
                    pe.matmul(k.ps[0][:, m * B:(m + 1) * B], tv_b1[:, m * P:(m + 1) * P], g9[:], start=True, stop=True)
                pe.matmul(k.ps[1][:, 0:2 * H], merge_w[:], tv_ln[:], start=True, stop=True).then_inc(bias_done, 1)
                pe.wait_ge(merge_kept, 8)
                pe.wait_ge(bias_kept, 2)

                def hidden(u):
                    for m in range(NM):
                        if u >= 1:
                            pe.wait_ge((hid_act, hid_dve)[m // 2], 2 * (u - 1) + m % 2 + 1)
                        pe.matmul(k.ps[m][:], w1m[:, u // 2, m * P:(m + 1) * P], x_t[:, u * GC:(u + 1) * GC],
                                  start=True, stop=True).then_inc(hid_done, 1)

                def product(u):
                    pe.wait_ge(hid_act, 2 * (u + 1))
                    pe.wait_ge(hid_dve, 2 * (u + 1))
                    if u >= 4:
                        pe.wait_ge(norm2.xn_ready, u - 3)
                    for j in range(GT):
                        n = GT * u + j
                        pe.matmul(res(n), x_t[:, n * P:(n + 1) * P], k.ident[:], start=True, stop=False)
                        pe.matmul(res(n), g9_wide[:, u // 2, :], tv_b2[:], start=False, stop=False)
                        for m in range(NM):
                            last = pe.matmul(res(n), hid[:, u % 2, m, j * P:(j + 1) * P], w2m[:, m, u // 2, :],
                                             start=False, stop=(m == NM - 1))
                    last.then_inc(res_done, 1)

                for u in range(NG + 1):
                    if u < NG:
                        hidden(u)
                    if u >= 1:
                        product(u - 1)


def linear_attention(nc, d, k):
    hres = k.hres
    BT = 2 * GC
    with Stage(nc, k, "lin_", recycle=True) as st:
        sb, sem = st.sb, st.sem
        xn = sb("xn", [P, NT, H], F32)
        x_t = sb("x_t", [P, B, S + 2], F32)
        w_qk = sb("w_qk", [P, 2 * H], F32)
        b_q = sb("b_q", [P, 1], F32)
        b_k = sb("b_k", [1, H], F32)
        ones = sb("ones", [P, P], F32)
        cos_tok, sin_tok = sb("cos_tok", [P, TB, H], F32), sb("sin_tok", [P, TB, H], F32)
        cos_feat, sin_feat = sb("cos_feat", [P, S], F32), sb("sin_feat", [P, S], F32)
        rot, rot_t = sb("rot", [P, P], F32), sb("rot_t", [P, P], F32)
        head_mask = sb("head_mask", [P, P], F32)
        head_cols = sb("head_cols", [P, NH], F32)
        lepe_w = sb("lepe_w", [P, 3], F32)
        lepe_diag = sb("lepe_diag", [P, 3, P], F32)
        lepe_b = sb("lepe_b", [P, H], F32)
        ex = sb("ex", [P, 4, GC], F32)
        rl = sb("rl", [P, 4, GC], F32)
        kk = sb("kk", [P, 2, TB, H], F32)
        k_cos, k_sin = sb("k_cos", [P, 2, TB, H], F32), sb("k_sin", [P, 2, TB, H], F32)
        qq = sb("qq", [P, 2, BT], F32)
        q_cos, q_sin = sb("q_cos", [P, 2, BT], F32), sb("q_sin", [P, 2, BT], F32)
        k_sum = sb("k_sum", [P, 2, H], F32)
        m2 = sb("m2", [P, H], F32)
        kv, kv_rot = sb("kv", [P, H], F32), sb("kv_rot", [P, H], F32)
        k_mean = sb("k_mean", [P, 1], F32)
        k_cols = sb("k_cols", [P, NH], F32)
        z = sb("z", [P, GT * NH], F32)
        mixed = sb("mixed", [P, GC], F32)

        loaded = sem("loaded")
        dve_chain, pool_chain = sem("dve_chain"), sem("pool_chain")
        pads_ready, lepe_ready, lepe_b_added = sem("pads_ready"), sem("lepe_ready"), sem("lepe_b_added")
        proj_done, elu_parts, elu_ready = sem("proj_done"), sem("elu_parts"), sem("elu_ready")
        cos_ready, sin_ready, ksum_ready = sem("cos_ready"), sem("sin_ready"), sem("ksum_ready")
        m_done, m2_kept, kv_done, kv_kept = sem("m_done"), sem("m2_kept"), sem("kv_done"), sem("kv_kept")
        kv_rot_done, kv_rot_kept = sem("kv_rot_done"), sem("kv_rot_kept")
        out_done, h3_ready = sem("out_done"), sem("h3_ready")

        def copy_out(act, g, bank):
            at = 1 + g % 2 * GC
            return act.activation(x_t[:, g // 2, at:at + GC], bank[:], ACT.Copy)

        norm = Norm(st, "n0", tile_of(hres), tile_of(xn), [k.ps[0], k.ps[1]], copy_out, k.ident)
        loads = ((w_qk[:], "w_qk"), (b_q[:], "b_q"), (b_k[:], "b_k"), (ones[:], "ones"), (cos_tok[:], "cos_tok"),
                 (sin_tok[:], "sin_tok"), (cos_feat[:], "cos_feat"), (sin_feat[:], "sin_feat"), (rot[:], "rot"),
                 (rot_t[:], "rot_t"), (head_mask[:], "head_mask"), (head_cols[:], "head_cols"),
                 (lepe_w[:], "lepe_w"), (lepe_b[:], "lepe_b"))
        UNITS = 4

        def tok(t, b, h):
            return t[:, b % 2, GT * h:GT * h + GT, :].rearrange("p n c -> p (n c)")

        with nc.Block() as block:
            @block.sync
            def _(sp):
                for dst, src in loads:
                    sp.dma_start(dst, d[src]).then_inc(loaded, 16)

            @block.gpsimd
            def _(pool):
                for b in range(B):
                    pool.memset(x_t[:, b, 0:1], 0.0).then_inc(pads_ready, 1)
                    pool.memset(x_t[:, b, S + 1:S + 2], 0.0).then_inc(pads_ready, 1)
                pool.wait_ge(loaded, 16 * len(loads))
                lepe_b4 = lepe_b[:, None, :].to_broadcast([P, GT, H])
                for g in range(NG):
                    pool.wait_ge(norm.xn_ready, g + 1)
                    hv = hres[:, GT * g:GT * g + GT, :]
                    pool.tensor_tensor(hv, hv, lepe_b4, ALU.add).then_inc(lepe_b_added, 1)
                for b in range(B):
                    for u in range(UNITS):
                        h = u % 2
                        pool.wait_ge(elu_ready, UNITS * b + u + 1)
                        if u < 2:
                            if b >= 2:
                                pool.wait_ge(m_done, b - 1)
                            pool.tensor_tensor(tok(k_sin, b, h), tok(kk, b, h),
                                               sin_tok[:, GT * h:GT * h + GT, :].rearrange("p n c -> p (n c)"),
                                               ALU.mult).then_inc(sin_ready, 1)
                        else:
                            if b >= 2:
                                pool.wait_ge(out_done, 2 * (b - 1))
                            cols = slice(h * GC, (h + 1) * GC)
                            pool.tensor_tensor(q_sin[:, b % 2, cols], qq[:, b % 2, cols], sin_feat[:, cols],
                                               ALU.mult).then_inc(sin_ready, 1)

            @block.vector
            def _(dve):
                chain = Chain(dve, dve_chain)
                dve.wait_ge(loaded, 16 * len(loads))
                for j in range(3):
                    dve.tensor_scalar(lepe_diag[:, j, :], k.ident[:], lepe_w[:, j:j + 1], None,
                                      ALU.mult).then_inc(lepe_ready, 1)
                for g in range(NG):
                    norm.dve(dve, chain, g)

                def elus(b):
                    for u in range(UNITS):
                        h, n = u % 2, UNITS * b + u
                        dve.wait_ge(elu_parts, 2 * (n + 1))
                        if b >= 2:
                            dve.wait_ge(m_done if u < 2 else out_done, b - 1 if u < 2 else 2 * (b - 1))
                            dve.wait_ge(sin_ready, UNITS * (b - 2) + u + 1)
                        v = tok(kk, b, h) if u < 2 else qq[:, b % 2, h * GC:(h + 1) * GC]
                        dve.scalar_tensor_tensor(v, ex[:, n % 4, :], 1.0, rl[:, n % 4, :], ALU.min,
                                                 ALU.add).then_inc(elu_ready, 1)
                        dve.wait_ge(elu_ready, n + 1)
                        if u < 2:
                            dve.tensor_tensor(tok(k_cos, b, h), v,
                                              cos_tok[:, GT * h:GT * h + GT, :].rearrange("p n c -> p (n c)"),
                                              ALU.mult).then_inc(cos_ready, 1)
                        else:
                            cols = slice(h * GC, (h + 1) * GC)
                            dve.tensor_tensor(q_cos[:, b % 2, cols], v, cos_feat[:, cols],
                                              ALU.mult).then_inc(cos_ready, 1)
                    if b >= 2:
                        dve.wait_ge(kv_done, b - 1)
                    dve.tensor_reduce(k_sum[:, b % 2, :], kk[:, b % 2].rearrange("p n c -> p c n"), AXX,
                                      ALU.add).then_inc(ksum_ready, 1)

                def matrices(b):
                    dve.wait_ge(m_done, b + 1)
                    dve.tensor_copy(m2[:], k.ps[5][:, 0:H]).then_inc(m2_kept, 1)
                    chain.do(dve.tensor_copy(k_mean[:], k.ps[5][:, 2 * H:2 * H + 1]))
                    if b:
                        dve.wait_ge(out_done, 2 * b)
                    chain.step(dve.tensor_scalar(k_cols[:], head_cols[:], k_mean[:, 0:1], None, ALU.mult))
                    dve.wait_ge(kv_done, b + 1)
                    chain.do(dve.tensor_tensor(kv[:], k.ps[4][:, 0:H], head_mask[:], ALU.mult))
                    dve.sem_inc(kv_kept, 1)
                    dve.wait_ge(kv_rot_done, b + 1)
                    dve.tensor_copy(kv_rot[:], k.ps[5][:, H:2 * H]).then_inc(kv_rot_kept, 1)

                def outputs(g):
                    dve.wait_ge(out_done, g + 1)
                    chain.do(dve.tensor_scalar(z[:], k.ps[4][:, P:P + GT * NH], 1e-6, None, ALU.add))
                    chain.do(dve.reciprocal(z[:], z[:]))
                    chain.do(dve.tensor_tensor(mixed[:].rearrange("p (m e) -> p m e", e=DH),
                                               k.ps[6][:].rearrange("p (m e) -> p m e", e=DH),
                                               z[:, :, None].to_broadcast([P, GT * NH, DH]), ALU.mult))
                    dve.wait_ge(lepe_b_added, g + 1)
                    hv = hres[:, GT * g:GT * g + GT, :].rearrange("p n c -> p (n c)")
                    chain.do(dve.tensor_tensor(hv, hv, mixed[:], ALU.add))
                    dve.tensor_tensor(hv, hv, k.ps[7][:], ALU.add).then_inc(h3_ready, 1)

                for b in range(B + 1):
                    if b < B:
                        elus(b)
                    if b >= 1:
                        matrices(b - 1)
                        outputs(2 * b - 2)
                        outputs(2 * b - 1)
                dve.wait_ge(h3_ready, NG)

            @block.scalar
            def _(act):
                for g in range(NG + 1):
                    if g < NG:
                        norm.act_apply(act, g)
                    if g >= 1:
                        norm.act_copy(act, g - 1)
                act.wait_ge(loaded, 16 * len(loads))
                for n in range(UNITS * B):
                    u = n % UNITS
                    act.wait_ge(proj_done, n + 1)
                    if n >= 4:
                        act.wait_ge(elu_ready, n - 3)
                    bias = 0.0 if u < 2 else b_q[:, 0:1]
                    act.activation(ex[:, n % 4, :], k.ps[u][:], ACT.Exp, bias=bias).then_inc(elu_parts, 1)
                    act.activation(rl[:, n % 4, :], k.ps[u][:], ACT.Relu, bias=bias).then_inc(elu_parts, 1)

            @block.tensor
            def _(pe):
                for g in range(NG):
                    norm.pe(pe, g)
                pe.wait_ge(norm.x_t_ready, NG)
                pe.wait_ge(loaded, 16 * len(loads))
                pe.wait_ge(pads_ready, 2 * B)
                pe.wait_ge(lepe_ready, 3)

                def project(b):
                    for u in range(UNITS):
                        h = u % 2
                        if b:
                            pe.wait_ge(elu_parts, 2 * (UNITS * (b - 1) + u + 1))
                        if u < 2:
                            for j in range(GT):
                                at = 1 + (GT * h + j) * P
                                out = k.ps[u][:, j * P:(j + 1) * P]
                                pe.matmul(out, ones[0:1, :], b_k[:], start=True, stop=False)
                                last = pe.matmul(out, x_t[:, b, at:at + P], w_qk[:, H:2 * H], start=False, stop=True)
                        else:
                            last = pe.matmul(k.ps[u][:], w_qk[:, 0:H], x_t[:, b, 1 + h * GC:1 + (h + 1) * GC],
                                             start=True, stop=True)
                        last.then_inc(proj_done, 1)

                def matrices(b):
                    pe.wait_ge(cos_ready, UNITS * b + 2)
                    pe.wait_ge(sin_ready, UNITS * b + 2)
                    pe.wait_ge(ksum_ready, b + 1)
                    if b:
                        pe.wait_ge(h3_ready, 2 * b)
                    for part, bank in ((k_cos, k.ps[4]), (k_sin, k.ps[5])):
                        for n in range(TB):
                            pe.matmul(bank[:, 0:H], part[:, b % 2, n, :], xn[:, TB * b + n, :], start=(n == 0),
                                      stop=(n == TB - 1 and part is k_sin))
                    pe.matmul(k.ps[5][:, 2 * H:2 * H + 1], k_sum[:, b % 2, :], ones[:, 0:1], start=True,
                              stop=True).then_inc(m_done, 1)
                    pe.wait_ge(m2_kept, b + 1)
                    pe.matmul(k.ps[4][:, 0:H], rot_t[:], m2[:], start=False, stop=True).then_inc(kv_done, 1)
                    pe.wait_ge(kv_kept, b + 1)
                    pe.matmul(k.ps[5][:, H:2 * H], rot[:], kv[:], start=True, stop=True).then_inc(kv_rot_done, 1)
                    pe.wait_ge(kv_rot_kept, b + 1)

                def outputs(g):
                    b, h = g // 2, g % 2
                    pe.wait_ge(cos_ready, UNITS * b + 4)
                    pe.wait_ge(sin_ready, UNITS * b + 4)
                    if g:
                        pe.wait_ge(h3_ready, g)
                    for j in range(GT):
                        cols = slice(h * GC + j * P, h * GC + (j + 1) * P)
                        pe.matmul(k.ps[4][:, P + j * NH:P + (j + 1) * NH], qq[:, b % 2, cols], k_cols[:], start=True, stop=True)
                        num = k.ps[6][:, j * P:(j + 1) * P]
                        pe.matmul(num, q_cos[:, b % 2, cols], kv[:], start=True, stop=False)
                        pe.matmul(num, q_sin[:, b % 2, cols], kv_rot[:], start=False, stop=True)
                        for t in range(3):
                            last = pe.matmul(k.ps[7][:, j * P:(j + 1) * P], x_t[:, b, cols.start + t:cols.stop + t],
                                             lepe_diag[:, t, :], start=(t == 0), stop=(t == 2))
                    last.then_inc(out_done, 1)

                for b in range(B + 1):
                    if b < B:
                        project(b)
                    if b >= 1:
                        matrices(b - 1)
                        outputs(2 * b - 2)
                        outputs(2 * b - 1)


def softmax_attention(nc, d, k):
    hres = k.hres
    HG = 4
    UNITS = B * NH // HG
    STEPS = 2 * (TB // 2) * HG
    MAXES = HG * TB * 2
    AHEAD = MAXES + 12
    Q_TERMS, K_TERMS = (0, 0, 0, 1, 1, 2), (0, 1, 2, 0, 1, 0)
    ROWS = len(Q_TERMS) * DH
    SLOTS, P_SLOTS = 3, 8
    LAST = UNITS * STEPS
    GROUPS = LAST // HG

    terms_dram = nc.dram_tensor("terms_dram", (2, B, 3, H, S), BF16).ap()
    max_dram = nc.dram_tensor("max_dram", (UNITS, 3, HG, S), BF16).ap()
    with Stage(nc, k, "att_") as st:
        sb, sem = st.sb, st.sem
        xa = k.xa
        x1 = sb("x1", [P, 2, GT, H], F32)
        x_t = sb("x_t", [P, T], F32)
        att = x_t[:].rearrange("p (n c) -> p n c", c=H)
        w_q, w_k, w_v, w_o = (sb(n, [P, H], F32) for n in ("w_q", "w_k", "w_v", "w_o"))
        ln_g, ln_b = sb("ln_g", [P, 1], F32), sb("ln_b", [P, 1], F32)
        ident16 = sb("ident16", [P, P], BF16)
        vv = sb("vv", [P, NT, NH, 2 * DH], F32)
        terms = sb("terms", [P, 4, 3, GC], BF16)
        rest = sb("rest", [P, 4, GC], F32)
        q6 = sb("q6", [P, SLOTS, HG, S], BF16)
        k6 = sb("k6", [P, SLOTS, HG, S], BF16)
        probs = sb("probs", [P, P_SLOTS, 2 * GC], F32)
        maxes = sb("maxes", [P, 2, MAXES], F32)
        row_max = sb("row_max", [P, 2, MAXES // 2], F32)
        max_terms = sb("max_terms", [P, 3, MAXES // 2], BF16)
        max_rows = sb("max_rows", [3 * MAXES // 2, P], BF16)
        mixed = sb("mixed", [P, GC], F32)
        r_sum = sb("r_sum", [P, GT, HG], F32)
        att_t = sb("att_t", [P, 2, GC], F32)

        loaded, v_set, ones_set = sem("loaded"), sem("v_set"), sem("ones_set")
        dve_chain = sem("dve_chain")
        qk_done, v_done, v_kept = sem("qk_done"), sem("v_done"), sem("v_kept")
        term1, rest1, term2, term3 = sem("term1"), sem("rest1"), sem("term2"), sem("term3")
        terms_out = [sem(f"terms_out{i}") for i in range(4)]
        qk_in = [sem(f"qk_in{i}") for i in range(SLOTS)]
        max_in = [sem(f"max_in{i}") for i in range(SLOTS)]
        tile_scored, bank_freed = sem("tile_scored"), sem("bank_freed")
        max_split, max_turned, max_out = sem("max_split"), sem("max_turned"), sem("max_out")
        scored, exp_done, pv_done = sem("scored"), sem("exp_done"), sem("pv_done")
        mixed_kept, mixed_turned = sem("mixed_kept"), sem("mixed_turned")
        att_turned, att_t_ready, wo_done, h4_ready = sem("att_turned"), sem("att_t_ready"), sem("wo_done"), sem("h4_ready")
        norm = Norm(st, "n0", tile_of(hres), tile_of(xa), [k.ps[0], k.ps[1]],
                    lambda act, g, bank: act.activation(x_t[:, g * GC:(g + 1) * GC], bank[:], ACT.Identity,
                                                        bias=ln_b[:, 0:1], scale=ln_g[:, 0:1]), k.ident,
                    again=lambda n: x1[:, n // GT % 2, n % GT, :])
        loads = ((w_q[:], "w_q"), (w_k[:], "w_k"), (w_v[:], "w_v"), (w_o[:], "w_o"), (ln_g[:], "ln1_g"),
                 (ln_b[:], "ln1_b"))

        def step_of(t):
            u, s = divmod(t, STEPS)
            return u, s // (STEPS // 2), s // HG % (TB // 2), s % HG

        def max_of(i):
            u, r = divmod(i, MAXES)
            return u, r // (2 * TB), r // 2 % TB, r % 2

        def maxes_at(t):
            if t < 0:
                return range(AHEAD)
            return range(min(AHEAD + 2 * t, UNITS * MAXES), min(AHEAD + 2 * t + 2, UNITS * MAXES))

        PV_LAG, KEEP_LAG, TURN_LAG = 5, 8, 9

        def group_at(t, lag):
            n = t - lag
            return n // HG if n >= 0 and n % HG == 0 and n // HG < GROUPS else None

        def output_at(t, lag):
            g = group_at(t, lag)
            return None if g is None or g % (TB // 2) != TB // 2 - 1 else g // (TB // 2)

        SPARE = (4, 5, 7)
        stream, use_of = {}, {}

        def use(t, kind, x):
            stream[t].append((len(use_of), kind, x))
            use_of[kind, x] = len(use_of)

        for t in range(-1, LAST + TURN_LAG):
            stream[t] = []
            for i in maxes_at(t):
                use(t, "max", i)
                if i >= MAXES and i % MAXES == 3:
                    use(t, "turn_max", i // MAXES - 1)
                if i == UNITS * MAXES - 1:
                    use(t, "turn_max", UNITS - 1)
            if output_at(t, TURN_LAG) is not None:
                use(t, "turn", output_at(t, TURN_LAG))

        def spare_bank(n):
            return k.ps[SPARE[n % len(SPARE)]]

        with nc.Block() as block:
            @block.sync
            def _(sp):
                for dst, src in loads:
                    sp.dma_start(dst, d[src]).then_inc(loaded, 16)
                for n in range(2 * NG):
                    g, j = n // 2, n % 2
                    sp.wait_ge(term1, n + 1)
                    sp.wait_ge(term2, n + 1)
                    sp.wait_ge(term3, n + 1)
                    dst = terms_dram[j, g // 2, :, :, g % 2 * GC:(g % 2 + 1) * GC].rearrange("t c s -> c t s")
                    sp.dma_start(dst, terms[:, n % 4]).then_inc(terms_out[n % 4], 16)

                def load(u):
                    b, hg, slot = u // 2, u % 2, u % SLOTS
                    if u >= SLOTS:
                        sp.wait_ge(scored, STEPS * (u - SLOTS + 1))
                    for j, (dst, order) in enumerate(((q6, Q_TERMS), (k6, K_TERMS))):
                        for r, term in enumerate(order):
                            src = terms_dram[j, b, term, hg * HG * DH:(hg + 1) * HG * DH, :].rearrange(
                                "(h e) s -> e h s", e=DH)
                            sp.dma_start(dst[r * DH:(r + 1) * DH, slot], src).then_inc(qk_in[slot], 16)

                def max_rows_in(u):
                    sp.wait_ge(bank_freed, use_of["turn_max", u] + 1)
                    sp.dma_start(max_dram[u].rearrange("t h (n p) -> (t h n) p", p=P), max_rows[:]).then_inc(max_out, 16)
                    sp.wait_ge(max_out, 16 * (u + 1))
                    sp.dma_start(q6[ROWS:ROWS + 3, u % SLOTS], max_dram[u]).then_inc(max_in[u % SLOTS], 16)

                for i in range(4):
                    sp.wait_ge(terms_out[i], 16 * 2 * NG // 4)
                for u in range(SLOTS):
                    load(u)
                for u in range(UNITS):
                    max_rows_in(u)
                    if 1 <= u and u + SLOTS - 1 < UNITS:
                        load(u + SLOTS - 1)

            @block.gpsimd
            def _(pool):
                pool.memset(vv[:], 0.0).then_inc(v_set, 1)
                pool.wait_ge(v_set, 1)
                pool.memset(vv[:, :, :, DH:DH + 1], 1.0).then_inc(v_set, 1)
                for n in range(2 * NG):
                    pool.wait_ge(term2, n + 1)
                    if n >= 4:
                        pool.wait_ge(terms_out[n % 4], 16 * (n // 4))
                    pool.tensor_tensor(terms[:, n % 4, 2, :], rest[:, n % 4, :], terms[:, n % 4, 1, :],
                                       ALU.subtract).then_inc(term3, 1)

            @block.vector
            def _(dve):
                chain = Chain(dve, dve_chain)
                dve.tensor_copy(ident16[:], k.ident[:]).then_inc(ones_set, 1)

                def split(g):
                    for n in (2 * g, 2 * g + 1):
                        dve.wait_ge(term1, n + 1)
                        if n >= 4:
                            dve.wait_ge(term3, n - 3)
                        dve.tensor_tensor(rest[:, n % 4, :], k.ps[2 + n % 2][:], terms[:, n % 4, 0, :],
                                          ALU.subtract).then_inc(rest1, 1)
                    dve.wait_ge(v_done, g + 1)
                    dve.wait_ge(v_set, 2)
                    dve.tensor_copy(vv[:, GT * g:GT * g + GT, :, 0:DH].rearrange("p n h e -> p (n h) e"),
                                    k.ps[4 + g % 2][:].rearrange("p (m e) -> p m e", e=DH)).then_inc(v_kept, 1)

                for g in range(NG):
                    norm.dve(dve, chain, g)
                    if g % 2 and g >= 3:
                        split(g - 3)
                        split(g - 2)
                split(NG - 2)
                split(NG - 1)
                dve.memset(k6[ROWS:ROWS + 3], 1.0).then_inc(ones_set, 1)

                def tile_max(n, i):
                    u, _, _, _ = max_of(i)
                    dve.wait_ge(tile_scored, i + 1)
                    dve.reduce_max(maxes[:, u % 2, i % MAXES:i % MAXES + 1], spare_bank(n)[:], AXX).then_inc(bank_freed, 1)

                def split_max(u):
                    dve.wait_ge(bank_freed, use_of["max", MAXES * (u + 1) - 1] + 1)
                    pair = maxes[:, u % 2, :].rearrange("p (m t) -> p m t", t=2)
                    m, r = row_max[:, 0, :], row_max[:, 1, :]
                    chain.do(dve.tensor_tensor(m, pair[:, :, 0], pair[:, :, 1], ALU.max))
                    if u:
                        dve.wait_ge(max_turned, u)
                    chain.do(dve.tensor_scalar(max_terms[:, 0, :], m, -1.0, None, ALU.mult))
                    chain.do(dve.scalar_tensor_tensor(r, m, -1.0, max_terms[:, 0, :], ALU.mult, ALU.subtract))
                    chain.do(dve.tensor_copy(max_terms[:, 1, :], r))
                    dve.tensor_tensor(max_terms[:, 2, :], r, max_terms[:, 1, :], ALU.subtract).then_inc(max_split, 1)

                def keep_max(n, u):
                    dve.wait_ge(max_turned, u + 1)
                    if u:
                        dve.wait_ge(max_out, 16 * u)
                    dve.tensor_copy(max_rows[:], spare_bank(n)[0:3 * MAXES // 2, 0:P // 2].bitcast(BF16)).then_inc(bank_freed, 1)

                def normalise(n, o):
                    u, qh = divmod(o, 2)
                    b, hg = u // 2, u % 2
                    dve.wait_ge(mixed_turned, o + 1)
                    if o:
                        dve.wait_ge(bank_freed, use_of["turn", o - 1] + 1)
                    acc = spare_bank(n)[:].rearrange("p (n h e) -> p n h e", n=GT, h=HG)
                    chain.do(dve.reciprocal(r_sum[:], acc[:, :, :, DH]))
                    n0 = TB * b + GT * qh
                    dst = att[:, n0:n0 + GT, hg * HG * DH:(hg + 1) * HG * DH].rearrange("p n (h e) -> p n h e", e=DH)
                    for j in range(GT):
                        last = dve.tensor_tensor(dst[:, j], acc[:, j, :, 0:DH],
                                                 r_sum[:, j, :, None].to_broadcast([P, HG, DH]), ALU.mult)
                    last.then_inc(bank_freed, 1)

                free = {"max": tile_max, "turn_max": keep_max, "turn": normalise}
                for t in range(-1, LAST + TURN_LAG):
                    for n, kind, x in stream[t]:
                        free[kind](n, x)
                        if kind == "max" and x % MAXES == MAXES - 1:
                            split_max(x // MAXES)
                for g in range(NG):
                    dve.wait_ge(wo_done, g + 1)
                    hv = xa[:, GT * g:GT * g + GT, :].rearrange("p n c -> p (n c)")
                    dve.tensor_tensor(hv, hv, k.ps[2 + g % 2][:], ALU.add).then_inc(h4_ready, 1)
                dve.wait_ge(h4_ready, NG)

            @block.scalar
            def _(act):
                act.wait_ge(loaded, 16 * len(loads))
                act.wait_ge(k.buf_cleared, 16 * k.CLEARS)

                def split(g):
                    for n in (2 * g, 2 * g + 1):
                        act.wait_ge(qk_done, n + 1)
                        if n >= 4:
                            act.wait_ge(terms_out[n % 4], 16 * (n // 4))
                        act.activation(terms[:, n % 4, 0, :], k.ps[2 + n % 2][:], ACT.Copy).then_inc(term1, 1)
                    for n in (2 * g, 2 * g + 1):
                        act.wait_ge(rest1, n + 1)
                        act.activation(terms[:, n % 4, 1, :], rest[:, n % 4, :], ACT.Copy).then_inc(term2, 1)

                for g in range(NG + 2):
                    if g < NG:
                        norm.act_apply(act, g)
                    if 1 <= g <= NG:
                        norm.act_copy(act, g - 1)
                    if g >= 2:
                        split(g - 2)
                for t in range(LAST + KEEP_LAG):
                    o = output_at(t, KEEP_LAG)
                    if o is not None:
                        act.wait_ge(pv_done, (o + 1) * TB // 2)
                        if o:
                            act.wait_ge(mixed_turned, o)
                        act.activation(mixed[:], k.ps[6][:], ACT.Copy).then_inc(mixed_kept, 1)
                    if t < LAST:
                        act.wait_ge(scored, t + 1)
                        if t >= P_SLOTS:
                            act.wait_ge(pv_done, (t - P_SLOTS) // HG + 1)
                        pair = k.psum[:, t % 2 * 2 * GC:(t % 2 + 1) * 2 * GC]
                        act.activation(probs[:, t % P_SLOTS, :], pair, ACT.Exp, scale=DH ** -0.5).then_inc(exp_done, 1)
                for g in range(NG):
                    act.wait_ge(att_turned, g + 1)
                    if g >= 2:
                        act.wait_ge(wo_done, g - 1)
                    act.activation(att_t[:, g % 2, :], k.ps[g % 2][:], ACT.Copy).then_inc(att_t_ready, 1)

            @block.tensor
            def _(pe):
                pe.wait_ge(loaded, 16 * len(loads))

                def project(g):
                    pe.wait_ge(norm.x_t_ready, g + 1)
                    for j, w in enumerate((w_q, w_k)):
                        if g:
                            pe.wait_ge(rest1, 2 * g - 1 + j)
                        pe.matmul(k.ps[2 + j][:], w[:], x_t[:, g * GC:(g + 1) * GC], start=True,
                                  stop=True).then_inc(qk_done, 1)
                    if g >= 2:
                        pe.wait_ge(v_kept, g - 1)
                    for j in range(GT):
                        n = GT * g + j
                        last = pe.matmul(k.ps[4 + g % 2][:, j * P:(j + 1) * P], x_t[:, n * P:(n + 1) * P], w_v[:],
                                         start=True, stop=True)
                    last.then_inc(v_done, 1)

                for g in range(NG + 1):
                    if g < NG:
                        norm.pe(pe, g)
                    if g >= 1:
                        project(g - 1)
                pe.wait_ge(v_kept, NG)
                pe.wait_ge(rest1, 2 * NG)

                def take_bank(n):
                    if n >= len(SPARE):
                        pe.wait_ge(bank_freed, n - len(SPARE) + 1)
                    return spare_bank(n)

                def first_pass(n, i):
                    u, h, qt, half = max_of(i)
                    slot = u % SLOTS
                    if i % MAXES == 0:
                        pe.wait_ge(qk_in[slot], 16 * 12 * (u // SLOTS + 1))
                    pe.matmul(take_bank(n)[:], q6[0:ROWS, slot, h, qt * P:(qt + 1) * P],
                              k6[0:ROWS, slot, h, half * GC:(half + 1) * GC], start=True,
                              stop=True).then_inc(tile_scored, 1)

                def turn_max(n, u):
                    pe.wait_ge(max_split, u + 1)
                    pe.wait_ge(ones_set, 1)
                    pe.transpose(take_bank(n)[0:3 * MAXES // 2, 0:P // 2].bitcast(BF16),
                                 max_terms[:].rearrange("p t m -> p (t m)"), ident16[:]).then_inc(max_turned, 1)

                def second_pass(t):
                    u, qh, kp, h = step_of(t)
                    slot = u % SLOTS
                    if t % STEPS == 0:
                        pe.wait_ge(max_in[slot], 16 * (u // SLOTS + 1))
                        pe.wait_ge(ones_set, 2)
                    if t >= 2:
                        pe.wait_ge(exp_done, t - 1)
                    for j in range(2):
                        kt = 2 * kp + j
                        last = pe.matmul(k.ps[t % 2 * 2 + j][:], k6[0:ROWS + 3, slot, h, kt * P:(kt + 1) * P],
                                         q6[0:ROWS + 3, slot, h, qh * GC:(qh + 1) * GC], start=True, stop=True)
                    last.then_inc(scored, 1)

                def times_v(g, j):
                    u, qh, kp, _ = step_of(HG * g)
                    b, hg = u // 2, u % 2
                    kt = 2 * kp + j
                    pe.wait_ge(exp_done, HG * (g + 1))
                    if kt == 0 and g:
                        pe.wait_ge(mixed_kept, g // (TB // 2))
                    for h in range(HG):
                        last = pe.matmul(k.ps[6][32 * h:32 * h + 32, :], vv[:, TB * b + kt, hg * HG + h, :],
                                         probs[:, (HG * g + h) % P_SLOTS, j * GC:(j + 1) * GC],
                                         start=(kt == 0), stop=(kt == TB - 1))
                    if j:
                        last.then_inc(pv_done, 1)

                def turn(n, o):
                    pe.wait_ge(mixed_kept, o + 1)
                    bank = take_bank(n)
                    for j in range(GT):
                        last = pe.transpose(bank[:, j * P:(j + 1) * P], mixed[:, j * P:(j + 1) * P], k.ident[:])
                    last.then_inc(mixed_turned, 1)

                fill = {"max": first_pass, "turn_max": turn_max, "turn": turn}
                for t in range(-1, LAST + TURN_LAG):
                    if 0 <= t < LAST:
                        second_pass(t)
                    uses = stream[t]
                    for n, kind, x in uses[:1]:
                        fill[kind](n, x)
                    for j in range(2):
                        g = group_at(t, PV_LAG + 2 * j)
                        if g is not None:
                            times_v(g, j)
                    for n, kind, x in uses[1:]:
                        fill[kind](n, x)
                pe.wait_ge(bank_freed, len(use_of))
                pe.wait_ge(exp_done, LAST)

                def out_proj(g):
                    pe.wait_ge(att_t_ready, g + 1)
                    if g >= 2:
                        pe.wait_ge(h4_ready, g - 1)
                    for j in range(GT):
                        last = pe.matmul(k.ps[2 + g % 2][:, j * P:(j + 1) * P], att_t[:, g % 2, j * P:(j + 1) * P],
                                         w_o[:], start=True, stop=True)
                    last.then_inc(wo_done, 1)

                for g in range(NG + 1):
                    if g < NG:
                        if g >= 2:
                            pe.wait_ge(att_t_ready, g - 1)
                        for j in range(GT):
                            last = pe.transpose(k.ps[g % 2][:, j * P:(j + 1) * P], att[:, GT * g + j, :], k.ident[:])
                        last.then_inc(att_turned, 1)
                    if g >= 1:
                        out_proj(g - 1)


def experts(nc, d, k, out):
    hres, xa = k.hres, k.xa
    A = 2 * NT
    SLOT_ROWS = E1 * CAP
    FAR = float(SLOT_ROWS)
    buf, y_dram = k.buf, k.y_dram
    RT = 512 // E1
    W_SLOTS, X_SLOTS = 16, 8
    W_LAG = 6
    BITS = 16
    WORDS = E1 // BITS

    with Stage(nc, k, "rt_") as st:
        sb, sem = st.sb, st.sem
        gate = sb("gate", [P, NT, 2], F32)
        mask = sb("mask", [P, WORDS], I32)
        w1 = sb("w1", [P, W_SLOTS, FFN], F32)
        w2 = sb("w2", [P, W_SLOTS, NM, H], F32)
        b2 = sb("b2", [P, W_SLOTS, H], F32)
        w_in = [sem(f"w_in{i}") for i in range(W_SLOTS)]

        def load_weights(sp, e):
            s = e % W_SLOTS
            sp.dma_start(w1[:, s], d["moe_w1"][e]).then_inc(w_in[s], 16)
            sp.dma_start(w2[:, s].rearrange("p m c -> p (m c)"), d["moe_w2"][e]).then_inc(w_in[s], 16)
            sp.dma_start(b2[:, s], d["moe_b2"][e:e + 1, :].to_broadcast([P, H])).then_inc(w_in[s], 16)

        with Stage(nc, k, "rt_") as st2:
            sb, sem = st2.sb, st2.sem
            x2_rows = sb("x2_rows", [P, NT, ROW], F32)
            x2 = x2_rows[:, :, 0:H]
            token = sb("token", [P, NT], F32)
            bit_weight = sb("bit_weight", [P, E1], F32)
            above = sb("above", [P, E1], F32)
            words = sb("words", [P, WORDS], F32)
            x_t = sb("x_t", [P, T], F32)
            g_tok, b_tok = sb("g_tok", [P, H], F32), sb("b_tok", [P, H], F32)
            g_col, b_col = sb("g_col", [P, 1], F32), sb("b_col", [P, 1], F32)
            w_r = sb("w_r", [P, E1], F32)
            before32 = sb("before32", [P, P], F32)
            before = sb("before", [P, P], BF16)
            ones16 = sb("ones16", [P, P], BF16)
            number = sb("number", [P, E1], F32)
            logit = sb("logit", [P, NT, E1], F32)
            top = sb("top", [P, NT, 8], F32)
            top_at = sb("top_at", [P, NT, 8], U32)
            expert = sb("expert", [P, NT, 2], F32)
            hot = sb("hot", [P, 2, NT, E1], BF16)
            both = sb("both", [P, 2, NT, E1], BF16)
            earlier = sb("earlier", [P, NT, E1], BF16)
            picked = sb("picked", [P, RT, E1], F32)
            pos = sb("pos", [P, NT, 2], F32)
            kept = sb("kept", [P, NT, 2], F32)
            high = sb("high", [P, NT, 2], F32)
            addr = sb("addr", [P, NT, 2], F32)
            far = sb("far", [P, NT, 2], F32)
            taddr = sb("taddr", [P, NT, 2], I32)
            lead = sb("lead", [P, NT], F32)

            loaded, dve_chain = sem("loaded"), sem("dve_chain")
            scaled, x2_ready = sem("scaled"), sem("x2_ready")
            logit_done, logit_kept = sem("logit_done"), sem("logit_kept")
            lead_ready, lead_exp = sem("lead_ready"), sem("lead_exp")
            hot_ready, prefix_done, counted = sem("hot_ready"), sem("prefix_done"), sem("counted")
            addr_ready, scattered = sem("addr_ready"), sem("scattered")
            norm = Norm(st2, "n0", tile_of(xa), tile_of(x2), [k.ps[0], k.ps[1]],
                        lambda act, g, bank: act.activation(x_t[:, g * GC:(g + 1) * GC], bank[:], ACT.Identity,
                                                            bias=b_col[:, 0:1], scale=g_col[:, 0:1]), k.ident)
            loads = ((g_tok[:], "ln2_g_tok"), (b_tok[:], "ln2_b_tok"), (g_col[:], "ln2_g"), (b_col[:], "ln2_b"),
                     (w_r[:], "w_r"), (before32[:], "before"), (number[:], "number"),
                     (token[:], "token"), (bit_weight[:], "bit_weight"))
            with nc.Block() as block:
                @block.sync
                def _(sp):
                    for dst, src in loads:
                        sp.dma_start(dst, d[src]).then_inc(loaded, 16)
                    for e in range(W_SLOTS):
                        load_weights(sp, e)

                @block.gpsimd
                def _(pool):
                    pool.wait_ge(loaded, 16 * len(loads))
                    b4 = b_tok[:, None, :].to_broadcast([P, GT, H])
                    for g in range(NG):
                        pool.wait_ge(scaled, g + 1)
                        v = x2[:, GT * g:GT * g + GT, :]
                        pool.tensor_tensor(v, v, b4, ALU.add).then_inc(x2_ready, 1)
                    pool.wait_ge(x2_ready, NG)
                    pool.wait_ge(addr_ready, 1)
                    pool.wait_ge(k.buf_cleared, 16 * k.CLEARS)
                    for n in range(NT):
                        for c in range(2):
                            pool.indirect_dma_start(buf, bass.IndirectOffsetOnAxis(ap=taddr[:, n, c:c + 1], axis=0),
                                                    x2_rows[:, n, :], None, bounds_check=SLOT_ROWS - 1,
                                                    oob_is_err=False).then_inc(scattered, 16)
                    pool.wait_ge(scattered, 16 * A)

                @block.vector
                def _(dve):
                    chain = Chain(dve, dve_chain)
                    dve.wait_ge(loaded, 16 * len(loads))
                    chain.step(dve.tensor_copy(before[:], before32[:]))
                    chain.step(dve.memset(ones16[:], 1.0))
                    g4 = g_tok[:, None, :].to_broadcast([P, GT, H])

                    def scale(g):
                        dve.wait_ge(norm.turned, g + 1)
                        v = x2[:, GT * g:GT * g + GT, :]
                        dve.tensor_tensor(v, v, g4, ALU.mult).then_inc(scaled, 1)

                    def choose(j):
                        dve.wait_ge(logit_kept, j + 1)
                        for n in range(RT * j, RT * j + RT):
                            chain.step(dve.max(top[:, n, :], logit[:, n, :]))
                        chain.wait()
                        for n in range(RT * j, RT * j + RT):
                            chain.step(dve.max_index(top_at[:, n, :], top[:, n, :], logit[:, n, :]))

                    for g in range(NG):
                        norm.dve(dve, chain, g)
                        if g % 2 and g >= 3:
                            scale(g - 3)
                            scale(g - 2)
                            if g >= 5:
                                choose((g - 5) // 2)
                    scale(NG - 2)
                    scale(NG - 1)
                    choose(2)
                    choose(3)
                    chain.wait()
                    dve.tensor_tensor(lead[:], top[:, :, 1], top[:, :, 0], ALU.subtract).then_inc(lead_ready, 1)
                    chain.do(dve.tensor_copy(expert[:], top_at[:, :, 0:2]))
                    chain.step(dve.tensor_copy(x2_rows[:, :, H], token[:]))
                    chain.step(dve.tensor_copy(x2_rows[:, :, H + 1], expert[:, :, 0]))
                    for c in range(2):
                        chain.step(dve.tensor_tensor(hot[:, c], number[:, None, :].to_broadcast([P, NT, E1]),
                                                     expert[:, :, c:c + 1].to_broadcast([P, NT, E1]), ALU.is_equal))
                    chain.wait()
                    chain.do(dve.tensor_tensor(both[:, 0], hot[:, 0], hot[:, 1], ALU.add))
                    dve.sem_inc(hot_ready, 1)
                    chain.do(dve.tensor_copy(earlier[:], both[:, 0]))
                    chain.do(dve.tensor_copy(both[:, 1], both[:, 0]))
                    old, new = both[:, 1], earlier
                    for j in range(5):
                        sh = 1 << j
                        chain.step(dve.tensor_tensor(new[:, sh:, :], old[:, sh:, :], old[:, 0:NT - sh, :], ALU.add))
                        if j:
                            chain.step(dve.tensor_copy(new[:, 0:sh, :], old[:, 0:sh, :]))
                        chain.wait()
                        old, new = new, old
                    chain.do(dve.tensor_copy(both[:, 1, 1:, :], earlier[:, 0:NT - 1, :]))
                    chain.do(dve.memset(both[:, 1, 0:1, :], 0.0))
                    dve.sem_inc(hot_ready, 1)
                    dve.wait_ge(lead_exp, 1)
                    chain.do(dve.tensor_scalar(gate[:, :, 1], lead[:], 1.0, None, ALU.add))
                    chain.do(dve.reciprocal(gate[:, :, 0], gate[:, :, 1]))
                    chain.do(dve.tensor_tensor(gate[:, :, 1], gate[:, :, 0], lead[:], ALU.mult))
                    for j in range(NT // RT):
                        dve.wait_ge(prefix_done, j + 1)
                        for c in range(2):
                            tiles = slice(RT * j, RT * j + RT)
                            chain.do(dve.tensor_tensor(picked[:], k.ps[2 + j][:].rearrange("p (n e) -> p n e", e=E1),
                                                       hot[:, c, tiles, :], ALU.mult))
                            chain.do(dve.tensor_reduce(pos[:, tiles, c], picked[:], AXX, ALU.add))
                    chain.do(dve.tensor_scalar(kept[:], pos[:], float(CAP), None, ALU.is_lt))
                    chain.do(dve.tensor_scalar(pos[:], pos[:], float(CAP - 1), None, ALU.min))
                    chain.do(dve.tensor_scalar(high[:], pos[:], float(P), None, ALU.is_ge))
                    chain.do(dve.scalar_tensor_tensor(pos[:], high[:], -float(P), pos[:], ALU.mult, ALU.add))
                    chain.do(dve.scalar_tensor_tensor(addr[:], pos[:], float(HALVES), high[:], ALU.mult, ALU.add))
                    chain.do(dve.scalar_tensor_tensor(addr[:], expert[:], float(CAP), addr[:], ALU.mult, ALU.add))
                    chain.do(dve.tensor_scalar(far[:], kept[:], -FAR, FAR, ALU.mult, ALU.add))
                    chain.do(dve.tensor_tensor(addr[:], addr[:], far[:], ALU.add))
                    chain.do(dve.tensor_copy(taddr[:], addr[:]))
                    dve.sem_inc(addr_ready, 1)
                    chain.step(dve.tensor_tensor(gate[:], gate[:], kept[:], ALU.mult))
                    dve.wait_ge(counted, 1)
                    chain.do(dve.scalar_tensor_tensor(above[:], k.ps[0][:, 0:E1], float(P), bit_weight[:],
                                                      ALU.is_gt, ALU.mult))
                    chain.do(dve.tensor_reduce(words[:], above[:].rearrange("p (w b) -> p w b", b=BITS), AXX, ALU.add))
                    chain.do(dve.tensor_copy(mask[:], words[:]))

                @block.scalar
                def _(act):
                    def logits(act, j):
                        act.wait_ge(logit_done, j + 1)
                        act.activation(logit[:, RT * j:RT * j + RT, :].rearrange("p n e -> p (n e)"), k.ps[2 + j][:],
                                       ACT.Copy).then_inc(logit_kept, 1)

                    act.wait_ge(loaded, 16 * len(loads))
                    for g in range(NG + 1):
                        if g < NG:
                            norm.act_apply(act, g)
                        if g >= 1:
                            norm.act_copy(act, g - 1)
                        if g >= 2 and g % 2 == 0:
                            logits(act, (g - 2) // 2)
                    act.wait_ge(lead_ready, 1)
                    act.activation(lead[:], lead[:], ACT.Exp).then_inc(lead_exp, 1)

                @block.tensor
                def _(pe):
                    pe.wait_ge(loaded, 16 * len(loads))
                    for g in range(NG + 1):
                        if g < NG:
                            norm.pe(pe, g)
                        if g >= 1:
                            pe.wait_ge(norm.x_t_ready, g)
                            for n in range(GT * (g - 1), GT * g):
                                last = pe.matmul(k.ps[2 + n // RT][:, n % RT * E1:(n % RT + 1) * E1],
                                                 x_t[:, n * P:(n + 1) * P], w_r[:], start=True, stop=True)
                            if g % 2 == 0:
                                last.then_inc(logit_done, 1)
                    pe.wait_ge(logit_kept, NT // RT)
                    pe.wait_ge(hot_ready, 2)
                    for j in range(NT // RT):
                        tiles = slice(RT * j, RT * j + RT)
                        pe.matmul(k.ps[2 + j][:], before[:], both[:, 0, tiles, :].rearrange("p n e -> p (n e)"),
                                  start=True, stop=False)
                        pe.matmul(k.ps[2 + j][:], ones16[:], both[:, 1, tiles, :].rearrange("p n e -> p (n e)"),
                                  start=False, stop=True).then_inc(prefix_done, 1)
                    pe.matmul(k.ps[0][:, 0:E1], ones16[:], earlier[:, NT - 1, :], start=True,
                              stop=True).then_inc(counted, 1)

        with Stage(nc, k, "moe_") as st3:
            sb, sem = st3.sb, st3.sem
            b1 = sb("b1", [P, E1, NM], F32)
            xe = sb("xe", [P, X_SLOTS, HALVES, ROW], F32)
            xe_t = sb("xe_t", [P, 2, CAP], F32)
            he = sb("he", [P, 2, NM, CAP], F32)
            ye = sb("ye", [P, X_SLOTS, HALVES, H], F32)
            dest_f = sb("dest_f", [P, 2, HALVES], F32)
            dest = sb("dest", [P, 2 * X_SLOTS, HALVES], I32)
            y_got = sb("y_got", [P, NT, 2, H], F32)
            b1_in, xe_set = sem("b1_in"), sem("xe_set")
            x_in = [sem(f"x_in{i}") for i in range(X_SLOTS)]
            y_out = [sem(f"y_out{i}") for i in range(X_SLOTS)]
            second_write, second_out = sem("second_write"), sem("second_out")
            turned, x_kept, dest_part = sem("turned"), sem("x_kept"), sem("dest_part")
            hid_done, hid_kept = sem("hid_done"), sem("hid_kept")
            y_done, y_kept = sem("y_done"), sem("y_kept")
            got = [sem(f"got{g}") for g in range(NG)]
            summed, dve_chain, stored = sem("summed"), sem("dve_chain"), k.stored
            buf_v = buf.rearrange("(e p t) c -> e p t c", p=P, t=HALVES)

            def load_masks(eng):
                return [eng.value_load(mask[0:1, i:i + 1], min_val=0, max_val=2 ** BITS - 1) for i in range(WORDS)]

            def has_second(masks, e):
                return (masks[e // BITS] & (1 << e % BITS)) > 0

            def load_results(eng, g):
                for i in range(X_SLOTS):
                    eng.wait_ge(y_out[i], 16 * E1 // X_SLOTS)
                eng.wait_ge(second_out, E1)
                src = y_dram[2 * GC * g:2 * GC * (g + 1), :].rearrange("(n p c) h -> p n (c h)", p=P, c=2)
                eng.dma_start(y_got[:, GT * g:GT * g + GT].rearrange("p n c h -> p n (c h)"), src).then_inc(got[g], 16)

            with nc.Block() as block:
                @block.sync
                def _(sp):
                    sp.dma_start(b1[:], d["moe_b1"]).then_inc(b1_in, 16)
                    masks = load_masks(sp)
                    sp.wait_ge(xe_set, 1)
                    for e in range(E1):
                        if e >= X_SLOTS:
                            sp.wait_ge(x_kept, e - X_SLOTS + 1)
                        s = e % X_SLOTS
                        with sp.If(has_second(masks, e)):
                            sp.dma_start(xe[:, s].rearrange("p t c -> p (t c)"),
                                         buf_v[e].rearrange("p t c -> p (t c)")).then_inc(x_in[s], 16)
                        with sp.Else():
                            sp.dma_start(xe[:, s, 0, :], buf_v[e][:, 0, :]).then_inc(x_in[s], 16)
                        w = e - W_LAG + W_SLOTS
                        if e >= W_LAG and w < E1:
                            sp.wait_ge(y_kept, e - W_LAG + 1)
                            load_weights(sp, w)
                    for g in range(0, NG, 2):
                        load_results(sp, g)
                    for g in range(NG):
                        sp.wait_ge(summed, g + 1)
                        sp.dma_start(out[g * GC:(g + 1) * GC, :].rearrange("(n p) c -> p n c", p=P),
                                     hres[:, GT * g:GT * g + GT, :]).then_inc(stored, 16)
                    sp.wait_ge(stored, 16 * NG)

                @block.gpsimd
                def _(pool):
                    masks = load_masks(pool)
                    second_count = pool.alloc_register("second_count")
                    pool.reg_mov(second_count, 0)
                    pool.wait_ge(k.buf_cleared, 16 * k.CLEARS)
                    for e in range(E1):
                        pool.wait_ge(y_kept, e + 1)
                        s = e % X_SLOTS

                        def write(t, done):
                            at = dest[:, e % (2 * X_SLOTS), t:t + 1]
                            pool.indirect_dma_start(y_dram, bass.IndirectOffsetOnAxis(ap=at, axis=0), ye[:, s, t, :],
                                                    None, bounds_check=2 * T - 1,
                                                    oob_is_err=False).then_inc(done, 16)

                        write(0, y_out[s])
                        with pool.If(has_second(masks, e)):
                            write(1, second_write)
                            pool.reg_add(second_count, second_count, 16)
                            pool.wait_ge(second_write, second_count)
                        pool.sem_inc(second_out, 1)

                @block.vector
                def _(dve):
                    dve.memset(xe[:], 0.0).then_inc(xe_set, 1)
                    chain = Chain(dve, dve_chain)
                    for e in range(E1 + 2):
                        if e < E1:
                            x, f = xe[:, e % X_SLOTS], dest_f[:, e % 2]
                            dve.wait_ge(x_in[e % X_SLOTS], 16 * (e // X_SLOTS + 1))
                            dve.scalar_tensor_tensor(f, x[:, :, H + 1], float(e), x[:, :, H], ALU.not_equal,
                                                     ALU.add).then_inc(dest_part, 1)
                            dve.wait_ge(dest_part, e + 1)
                            dve.tensor_scalar(dest[:, e % (2 * X_SLOTS), :], f, float(2 * T), None, ALU.add)
                            dve.wait_ge(turned, e + 1)
                            if e >= 2:
                                dve.wait_ge(hid_done, NM * (e - 1))
                            dve.tensor_copy(xe_t[:, e % 2, :], k.ps[e % 2][:, 0:CAP]).then_inc(x_kept, 1)
                        if e >= 2:
                            f = e - 2
                            dve.wait_ge(y_done, f + 1)
                            if f >= X_SLOTS:
                                dve.wait_ge(y_out[f % X_SLOTS], 16 * (f // X_SLOTS))
                                dve.wait_ge(second_out, f - X_SLOTS + 1)
                            dve.tensor_tensor(ye[:, f % X_SLOTS], k.ps[6 + f % 2][:, 0:CAP].rearrange("p (t c) -> p t c", c=H),
                                              b2[:, f % W_SLOTS, None, :].to_broadcast([P, HALVES, H]),
                                              ALU.add).then_inc(y_kept, 1)
                    chain.do(dve.tensor_tensor(hres[:], hres[:], xa[:], ALU.add))
                    for g in range(NG):
                        dve.wait_ge(got[g], 16)
                        for c in range(2):
                            for n in range(GT * g, GT * g + GT):
                                chain.step(dve.scalar_tensor_tensor(hres[:, n, :], y_got[:, n, c, :], gate[:, n, c:c + 1],
                                                                    hres[:, n, :], ALU.mult, ALU.add))
                            chain.wait()
                        dve.sem_inc(summed, 1)

                @block.scalar
                def _(act):
                    act.wait_ge(b1_in, 16)
                    for e in range(E1):
                        for m in range(NM):
                            act.wait_ge(hid_done, NM * e + m // 2 * 2 + 2)
                            if e >= 2:
                                act.wait_ge(y_done, e - 1)
                            bank = k.ps[2 + 2 * (e % 2) + m // 2]
                            act.activation(he[:, e % 2, m, :], bank[:, m % 2 * CAP:(m % 2 + 1) * CAP],
                                           ACT.Gelu_apprx_tanh, bias=b1[:, e, m:m + 1]).then_inc(hid_kept, 1)
                    for g in range(1, NG, 2):
                        load_results(act, g)

                @block.tensor
                def _(pe):
                    masks = load_masks(pe)

                    def turn(e):
                        pe.wait_ge(x_in[e % X_SLOTS], 16 * (e // X_SLOTS + 1))
                        if e >= 2:
                            pe.wait_ge(x_kept, e - 1)
                        for t in range(HALVES):
                            last = pe.transpose(k.ps[e % 2][:, t * P:(t + 1) * P], xe[:, e % X_SLOTS, t, 0:H], k.ident[:])
                        last.then_inc(turned, 1)

                    def up(e, halves):
                        for m in range(NM):
                            if e >= 2:
                                pe.wait_ge(hid_kept, NM * (e - 2) + m // 2 * 2 + 2)
                            bank = k.ps[2 + 2 * (e % 2) + m // 2]
                            pe.matmul(bank[:, m % 2 * CAP:m % 2 * CAP + halves * P], w1[:, e % W_SLOTS, m * P:(m + 1) * P],
                                      xe_t[:, e % 2, 0:halves * P], start=True, stop=True).then_inc(hid_done, 1)

                    def down(e, halves):
                        for t in range(halves):
                            for m in range(NM):
                                last = pe.matmul(k.ps[6 + e % 2][:, t * P:(t + 1) * P], he[:, e % 2, m, t * P:(t + 1) * P],
                                                 w2[:, e % W_SLOTS, m, :], start=(m == 0), stop=(m == NM - 1))
                        last.then_inc(y_done, 1)

                    for e in range(E1 + 2):
                        if e < E1:
                            turn(e)
                        if 1 <= e <= E1:
                            pe.wait_ge(x_kept, e)
                            pe.wait_ge(w_in[(e - 1) % W_SLOTS], 16 * 3 * ((e - 1) // W_SLOTS + 1))
                            with pe.If(has_second(masks, e - 1)):
                                up(e - 1, 2)
                            with pe.Else():
                                up(e - 1, 1)
                        if e >= 2:
                            pe.wait_ge(hid_kept, NM * (e - 1))
                            if e >= 4:
                                pe.wait_ge(y_kept, e - 3)
                            with pe.If(has_second(masks, e - 2)):
                                down(e - 2, 2)
                            with pe.Else():
                                down(e - 2, 1)


def clear_buffer(nc, d, k):
    k.buf = nc.dram_tensor("buf_dram", (E1 * CAP, ROW), F32).ap()
    k.y_dram = nc.dram_tensor("y_dram", (2 * T, H), F32).ap()
    zeros = k.xa[:].rearrange("p n c -> p (n c)")
    with nc.Block() as block:
        @block.vector
        def _(dve):
            dve.memset(k.xa[:], 0.0).then_inc(k.zeroed, 1)

        @block.sync
        def _(sp):
            sp.wait_ge(k.zeroed, 1)
            for dram, cols in ((k.buf, E1 * CAP * ROW // P), (k.y_dram, 2 * T * H // P)):
                flat = dram.rearrange("(p r) c -> p (r c)", p=P)
                for c0 in range(0, cols, NT * H):
                    width = min(NT * H, cols - c0)
                    sp.dma_start(flat[:, c0:c0 + width], zeros[:, 0:width]).then_inc(k.buf_cleared, 16)


class Keep:
    CLEARS = -(-E1 * CAP * ROW // (T * H)) + 2 * T * H // (T * H)


STAGES = [clear_buffer, embed_and_scan, task_ffn, linear_attention, softmax_attention]


def build(nc, d, out, stages=None, last=True):
    with ExitStack() as ctx:
        k = Keep()
        k.ctx = ctx
        k.hres = ctx.enter_context(nc.sbuf_tensor("hres", [P, NT, H], F32))
        k.ident = ctx.enter_context(nc.sbuf_tensor("ident", [P, P], F32))
        k.xa = ctx.enter_context(nc.sbuf_tensor("xa", [P, NT, H], F32))
        k.psum = ctx.enter_context(nc.psum_tensor("psum", [P, 8 * 512], F32))
        k.ps = [k.psum[:, 512 * i:512 * i + 512] for i in range(8)]
        k.stored = ctx.enter_context(nc.semaphore("stored"))
        k.zeroed = ctx.enter_context(nc.semaphore("zeroed"))
        k.buf_cleared = ctx.enter_context(nc.semaphore("buf_cleared"))
        for stage in (stages or STAGES):
            stage(nc, d, k)
        if last:
            experts(nc, d, k, out)
            return
        stored = k.stored
        with nc.Block() as block:
            @block.sync
            def _(sp):
                sp.dma_start(out.rearrange("(n p) c -> p n c", p=P), k.hres[:]).then_inc(stored, 16)
                sp.wait_ge(stored, 16)


def layout(inp):
    f = lambda n: np.asarray(inp[n])
    c = np.ascontiguousarray
    bc = lambda n: c(np.broadcast_to(f(n), (P, H)))
    tiles = lambda a: a.reshape(NT, P).T
    a = {
        "ids": c(np.stack([tiles(f("x")), tiles(f("itok_BS_2_50255"))], 1)),
        "table": c(f("L0_tok_weight")),
        "ident": np.eye(P, dtype=np.float32),
        "bm_t": c(f("L0_attn_Bm").T), "c_t": c(f("L0_attn_C").T),
        "a_t": c(f("L0_attn_A").T), "a": c(f("L0_attn_A")),
        "gamma_b": bc("L0_attn_gamma"), "beta_b": bc("L0_attn_beta"),
    }
    R, K9 = P // NE0, NE0 + 1
    gb, g2 = f("L0_ffn_gfc2_b"), f("L0_ffn_gfc2_w")
    with_base = lambda tv, base: c(np.concatenate([f(tv), f(base)[None]], 0))
    merge_w = np.full((K9, P), 0.03, np.float32)
    merge_w[NE0] = 1.0 - 0.03 * NE0
    a.update({
        "gfc1_t": c(f("L0_ffn_gfc1_w").T), "gfc1_b": c(f("L0_ffn_gfc1_b")[:, None]),
        "gfc2_rep": c(np.broadcast_to(g2.T[:, :, None], (P, NE0, R))),
        "gfc2_b_rep": c(np.broadcast_to(gb[:, None, None], (NE0, R, 1)).reshape(P, 1)),
        "gfc2_t": c(g2.T), "gfc2_b": c(gb[:, None]),
        "delta": c(np.tile(np.eye(R, dtype=np.float32), (NE0, 1))),
        "tv_w1": c(f("L0_ffn_tv_W1").reshape(P, FFN // R, H)), "tv_w2": c(f("L0_ffn_tv_W2").reshape(P, H // R, FFN)),
        "w1_t": c(f("L0_ffn_W1").T), "w2_t": c(f("L0_ffn_W2").T.reshape(NM, P, H).transpose(1, 0, 2)),
        "tv_b1": with_base("L0_ffn_tv_b1", "L0_ffn_b1"), "tv_b2": with_base("L0_ffn_tv_b2", "L0_ffn_b2"),
        "tv_ln": c(np.concatenate([with_base("L0_ffn_tv_ln_g", "L0_ffn_ln_g"), with_base("L0_ffn_tv_ln_b", "L0_ffn_ln_b")], 1)),
        "merge_w": merge_w,
    })
    inv_freq = (1.0 / 10000.0 ** (np.arange(0, DH, 2, dtype=np.float32) / DH)).astype(np.float32)
    freqs = np.outer(np.arange(S, dtype=np.float32), inv_freq)
    angle = np.tile(np.concatenate([freqs, freqs], -1), (1, NH))
    cos, sin = np.cos(angle).astype(np.float32), np.sin(angle).astype(np.float32)
    rot = np.zeros((P, P), np.float32)
    for h in range(NH):
        for e in range(DH // 2):
            rot[h * DH + e, h * DH + e + DH // 2] = -1.0
            rot[h * DH + e + DH // 2, h * DH + e] = 1.0
    head = np.arange(P) // DH
    b_qk = f("L1_attn_bqk")
    by_tile = lambda t: c(t.reshape(TB, P, H).transpose(1, 0, 2))
    a.update({
        "w_qk": c(f("L1_attn_Wqk")), "b_q": c(b_qk[:H, None]), "b_k": c(b_qk[None, H:]),
        "ones": np.ones((P, P), np.float32), "cos_tok": by_tile(cos), "sin_tok": by_tile(sin),
        "cos_feat": c(cos.T), "sin_feat": c(sin.T), "rot": rot, "rot_t": c(rot.T),
        "head_mask": (head[:, None] == head[None, :]).astype(np.float32) / np.float32(S),
        "head_cols": (head[:, None] == np.arange(NH)[None, :]).astype(np.float32) / np.float32(S),
        "lepe_w": c(f("L1_attn_lepe_w")[:, 0, :]), "lepe_b": bc("L1_attn_lepe_b"),
    })
    a.update({
        "w_q": c(f("L1_ffn_wq")), "w_k": c(f("L1_ffn_wk")), "w_v": c(f("L1_ffn_wv")), "w_o": c(f("L1_ffn_wo")),
        "ln1_g": c(f("L1_ffn_ln1_g")[:, None]), "ln1_b": c(f("L1_ffn_ln1_b")[:, None]),
        "ln2_g_tok": bc("L1_ffn_ln2_g"), "ln2_b_tok": bc("L1_ffn_ln2_b"),
        "ln2_g": c(f("L1_ffn_ln2_g")[:, None]), "ln2_b": c(f("L1_ffn_ln2_b")[:, None]), "w_r": c(f("L1_ffn_wr")),
        "before": c(np.triu(np.ones((P, P), np.float32), 1)),
        "number": c(np.broadcast_to(np.arange(E1, dtype=np.float32), (P, E1))),
        "token": c(2 * tiles(np.arange(T, dtype=np.float32)) - np.float32(2 * T)),
        "bit_weight": c(np.broadcast_to(2.0 ** (np.arange(E1) % 16), (P, E1)).astype(np.float32)),
        "moe_w1": c(f("L1_ffn_w1")), "moe_b1": c(f("L1_ffn_b1").reshape(E1, NM, P).transpose(2, 0, 1)),
        "moe_w2": c(f("L1_ffn_w2").reshape(E1, NM, P, H).transpose(0, 2, 1, 3).reshape(E1, P, NM * H)),
        "moe_b2": c(f("L1_ffn_b2")),
    })
    return a


def kernel(**inputs):
    import concourse.bacc as _bacc
    from concourse.bass_utils import run_bass_kernel_spmd as _run

    nc = _bacc.Bacc("TRN2", target_bir_lowering=False, num_devices=1)
    arrays = layout(inputs)
    d = {n: nc.dram_tensor("in_" + n, a.shape, mybir.dt.from_np(a.dtype), kind="ExternalInput").ap() for n, a in arrays.items()}
    out = nc.dram_tensor("out", (T, H), F32, kind="ExternalOutput").ap()
    build(nc, d, out)
    r = _run(nc, [{"in_" + n: a for n, a in arrays.items()}], core_ids=[0])
    return r.results[0]["out"].reshape(B, S, H)
```

```python
from contextlib import ExitStack

import numpy as np
import concourse.bass as bass
from concourse import mybir

F32 = mybir.dt.float32
BF16 = mybir.dt.bfloat16
I32 = mybir.dt.int32
U32 = mybir.dt.uint32
ALU = mybir.AluOpType
ACT = mybir.ActivationFunctionType
AXX = mybir.AxisListType.X

P = 128
B, S, H = 4, 1024, 128
T = B * S
NT = T // P
TB = S // P
GT = 4
NG = NT // GT
GC = GT * P
EPS = 1e-5
RSQRT_MAGIC = 1597463007.0
D_STATE = 64
CHUNK = 16
NC = S // CHUNK
CLAMP = 1e6
FLT_MAX = 3.4028234e38
FFN = 512
NE0 = 8
NM = FFN // P
NH, DH = 8, 16
E1 = 64
CAP = 2 * (T * 2 // E1)
HALVES = CAP // P
ROW = H + 2


class Chain:

    def __init__(self, eng, sem):
        self.eng, self.sem, self.n = eng, sem, 0

    def step(self, ins):
        self.n += 1
        ins.then_inc(self.sem, 1)
        return ins

    def wait(self):
        self.eng.wait_ge(self.sem, self.n)

    def do(self, ins):
        self.step(ins)
        self.wait()


class Norm:

    def __init__(self, stage, tag, src, xn, banks, copy_out, ident, again=None):
        self.src, self.xn, self.banks, self.copy_out, self.ident = src, xn, banks, copy_out, ident
        self.taken = set()
        self.again = again
        if again is not None:
            self.rstd2 = stage.sb(f"{tag}_rstd2", [P, NT], F32)
            self.shift2 = stage.sb(f"{tag}_shift2", [P, NT], F32)
        self.stats = stage.sb(f"{tag}_stats", [P, NT, 6], F32)
        self.mv = stage.sb(f"{tag}_meanvar", [P, NT, 2], F32)
        self.var = stage.sb(f"{tag}_var", [P, NT], F32)
        self.rstd = stage.sb(f"{tag}_rstd", [P, NT], F32)
        self.shift = stage.sb(f"{tag}_shift", [P, NT], F32)
        self.stats_ready = stage.sem(f"{tag}_stats_ready")
        self.xn_ready = stage.sem(f"{tag}_xn_ready")
        self.turned = stage.sem(f"{tag}_turned")
        self.x_t_ready = stage.sem(f"{tag}_x_t_ready")

    def dve(self, dve, chain, g, ahead=False):
        if g % 2:
            return
        tiles = range(GT * g, GT * (g + 2))
        for n in tiles:
            if n not in self.taken:
                self.take(dve, chain, n)
        chain.wait()
        for n in tiles:
            chain.step(dve.bn_aggr(self.mv[:, n, :], self.stats[:, n, :]))
        chain.wait()
        between = list(range(tiles[-1] + 1, min(tiles[-1] + 1 + 2 * GT, NT))) if ahead else []

        def do(ins):
            chain.step(ins)
            at = chain.n
            if between:
                self.take(dve, chain, between.pop(0))
            dve.wait_ge(chain.sem, at)

        cols = slice(tiles[0], tiles[-1] + 1)
        mean, var = self.mv[:, cols, 0], self.mv[:, cols, 1]
        r, shift = self.rstd[:, cols], self.shift[:, cols]
        do(dve.tensor_scalar(self.var[:, cols], var, EPS, None, ALU.add))
        self.rsqrt(dve, do, r, self.var[:, cols], shift)
        if self.again is None:
            dve.scalar_tensor_tensor(shift, mean, -1.0, r, ALU.mult, ALU.mult).then_inc(self.stats_ready, 2)
            return
        r2, shift2 = self.rstd2[:, cols], self.shift2[:, cols]
        chain.step(dve.scalar_tensor_tensor(shift, mean, -1.0, r, ALU.mult, ALU.mult))
        do(dve.tensor_tensor(shift2, r, r, ALU.mult))
        do(dve.tensor_tensor(shift2, shift2, var, ALU.mult))
        do(dve.tensor_scalar(self.var[:, cols], shift2, EPS, None, ALU.add))
        self.rsqrt(dve, do, r2, self.var[:, cols], shift2)
        do(dve.tensor_tensor(shift2, shift, r2, ALU.mult))
        dve.tensor_tensor(r2, r2, r, ALU.mult).then_inc(self.stats_ready, 2)

    def take(self, dve, chain, n):
        self.taken.add(n)
        chain.step(dve.bn_stats(self.stats[:, n, :], self.src(n)))

    def rsqrt(self, dve, do, r, var, sq):
        do(dve.tensor_scalar(r.bitcast(I32), var.bitcast(I32), -0.5, RSQRT_MAGIC, ALU.mult, ALU.add))
        for _ in range(3):
            do(dve.tensor_tensor(sq, r, r, ALU.mult))
            do(dve.scalar_tensor_tensor(sq, sq, -0.5, var, ALU.mult, ALU.mult))
            do(dve.scalar_tensor_tensor(r, sq, 1.5, r, ALU.add, ALU.mult))

    def act_apply(self, act, g):
        act.wait_ge(self.stats_ready, g + 1)
        for n in range(GT * g, GT * g + GT):
            last = act.activation(self.xn(n), self.src(n), ACT.Identity,
                                  bias=self.shift[:, n:n + 1], scale=self.rstd[:, n:n + 1])
        if self.again is not None:
            if g >= 2:
                act.wait_ge(self.turned, g - 1)
            for n in range(GT * g, GT * g + GT):
                last = act.activation(self.again(n), self.src(n), ACT.Identity,
                                      bias=self.shift2[:, n:n + 1], scale=self.rstd2[:, n:n + 1])
        last.then_inc(self.xn_ready, 1)

    def pe(self, pe, g):
        pe.wait_ge(self.xn_ready, g + 1)
        if g >= 2:
            pe.wait_ge(self.x_t_ready, g - 1)
        bank = self.banks[g % 2]
        for j in range(GT):
            last = pe.transpose(bank[:, j * P:(j + 1) * P], (self.again or self.xn)(GT * g + j), self.ident[:])
        last.then_inc(self.turned, 1)

    def act_copy(self, act, g):
        act.wait_ge(self.turned, g + 1)
        self.copy_out(act, g, self.banks[g % 2]).then_inc(self.x_t_ready, 1)


def tile_of(t):
    return lambda n: t[:, n, :]


class Stage:

    def __init__(self, nc, k, tag, recycle=False):
        self.nc, self.tag, self.ctx, self.recycle, self.sems = nc, tag, ExitStack(), recycle, []

    def __enter__(self):
        self.ctx.__enter__()
        return self

    def __exit__(self, *exc):
        if self.recycle and exc[0] is None:
            self.nc.clear_and_free_semaphores(self.sems)
            self.nc.all_engine_barrier()
        return self.ctx.__exit__(*exc)

    def sb(self, name, shape, dt):
        return self.ctx.enter_context(self.nc.sbuf_tensor(self.tag + name, shape, dt))

    def sem(self, name):
        self.sems.append(self.nc.alloc_semaphore(name=self.tag + name))
        return self.sems[-1]


def embed_and_scan(nc, d, k):
    hres = k.hres
    with Stage(nc, k, "scan_", recycle=True) as st:
        sb, sem = st.sb, st.sem
        ids = sb("ids", [P, 2, NT], I32)
        differ = sb("differ", [P, NT], F32)
        e1 = sb("e1", [P, NT, H], F32)
        e2 = sb("e2", [P, NT, H], F32)
        x_t = sb("x_t", [P, T], F32)
        xs = sb("xs", [D_STATE, T], F32)
        q_pow = sb("q_pow", [D_STATE, CHUNK, D_STATE], F32)
        p_pow = sb("p_pow", [D_STATE, 2, D_STATE], F32)
        q_big = sb("q_big", [D_STATE, 6, D_STATE], F32)
        bm_t = sb("bm_t", [P, D_STATE], F32)
        c_t = sb("c_t", [D_STATE, H], F32)
        carry = sb("carry", [D_STATE, 2, B, NC + 1], F32)
        gamma = sb("gamma", [P, H], F32)
        beta = sb("beta", [P, H], F32)
        gel = sb("gel", [P, NT, H], F32)
        yn = sb("yn", [P, NT, H], F32)
        ya = sb("ya", [P, 2, GC], F32)
        yb = sb("yb", [P, 2, GC], F32)
        yc = sb("yc", [P, 2, GC], F32)
        yd = sb("yd", [P, 2, GC], F32)
        finite = sb("finite", [P, 2, GC], F32)
        known = sb("known", [P, 2, GC], F32)

        ids_in, small_in = sem("ids_in"), sem("small_in")
        gathered = [sem(f"gathered{g}") for g in range(NG)]
        dve_chain = sem("dve_chain")
        h0_ready = sem("h0_ready")
        pow_done, pow_kept = sem("pow_done"), sem("pow_kept")
        step_done = [sem(f"step_done{s}") for s in range(2)]
        step_kept = [sem(f"step_kept{s}") for s in range(2)]
        carry_done, carry_kept = sem("carry_done"), sem("carry_kept")
        fix_done, fix_kept = sem("fix_done"), sem("fix_kept")
        y_done, y_kept = sem("y_done"), sem("y_kept")
        st2_ready, yn_ready, scaled, guarded = sem("st2_ready"), sem("yn_ready"), sem("scaled"), sem("guarded")
        pool_chain, h1_ready = sem("pool_chain"), sem("h1_ready")
        norm = Norm(st, "n0", tile_of(hres), tile_of(e1), [k.ps[0], k.ps[1]],
                    lambda act, g, bank: act.activation(x_t[:, g * GC:(g + 1) * GC], bank[:], ACT.Copy), k.ident)
        norm2 = Norm(st, "n1", tile_of(gel), tile_of(yn), None, None, None)

        def at_pos(t, i, s):
            half = T // 2
            return t[:, s * half:(s + 1) * half].rearrange("c (m i) -> c i m", i=CHUNK)[:, i, :]

        with nc.Block() as block:
            @block.sync
            def _(sp):
                sp.dma_start(ids[:], d["ids"]).then_inc(ids_in, 16)
                for dst, src in ((k.ident[:], d["ident"]), (bm_t[:], d["bm_t"]), (c_t[:], d["c_t"]),
                                 (q_pow[:, 0, :], d["a_t"]), (p_pow[:, 0, :], d["a"]),
                                 (gamma[:], d["gamma_b"]), (beta[:], d["beta_b"])):
                    sp.dma_start(dst, src).then_inc(small_in, 16)

            @block.gpsimd
            def _(pool):
                pool.wait_ge(ids_in, 16)
                for n in range(NT):
                    for j, e in ((0, e1), (1, e2)):
                        pool.indirect_dma_start(e[:, n, :], None, d["table"],
                                                bass.IndirectOffsetOnAxis(ap=ids[:, j, n:n + 1], axis=0)
                                                ).then_inc(gathered[n // GT], 16)
                chain = Chain(pool, pool_chain)
                beta4 = beta[:, None, :].to_broadcast([P, GT, H])
                for g in range(NG):
                    s = g % 2
                    pool.wait_ge(scaled, g + 1)
                    if g >= 2:
                        pool.wait_ge(h1_ready, g - 1)
                    v = yb[:, s, :]
                    chain.do(pool.tensor_tensor(v.rearrange("p (n c) -> p n c", c=H),
                                                ya[:, s, :].rearrange("p (n c) -> p n c", c=H), beta4, ALU.add))
                    pool.tensor_scalar(yc[:, s, :], v, -CLAMP, CLAMP, ALU.max, ALU.min).then_inc(guarded, 1)
                    pool.memset(yd[:, s, :], 0.0).then_inc(guarded, 1)

            @block.vector
            def _(dve):
                chain = Chain(dve, dve_chain)
                dve.wait_ge(ids_in, 16)
                chain.do(dve.tensor_tensor(differ[:], ids[:, 0, :], ids[:, 1, :], ALU.not_equal))
                dve.wait_ge(small_in, 16 * 7)
                chain.do(dve.memset(carry[:], 0.0))
                n = 0
                for j in range(9):
                    dve.wait_ge(pow_done, 2 * (j + 1))
                    a = 1 << j
                    if a < CHUNK:
                        dve.tensor_copy(q_pow[:, a:2 * a, :], k.ps[2][0:D_STATE, 0:a * D_STATE].rearrange("s (m t) -> s m t", t=D_STATE)).then_inc(pow_kept, 1)
                    else:
                        dve.tensor_copy(q_big[:, j - 3, :], k.ps[2][0:D_STATE, 0:D_STATE]).then_inc(pow_kept, 1)
                    if j == 3:
                        chain.do(dve.tensor_copy(q_big[:, 0, :], k.ps[2][0:D_STATE, 7 * D_STATE:8 * D_STATE]))
                    dve.tensor_copy(p_pow[:, (j + 1) % 2, :], k.ps[3][0:D_STATE, 0:D_STATE]).then_inc(pow_kept, 1)
                for g in range(NG):
                    dve.wait_ge(gathered[g], 16 * 2 * GT)
                    for n in range(GT * g, GT * g + GT):
                        chain.step(dve.scalar_tensor_tensor(hres[:, n, :], e2[:, n, :], differ[:, n:n + 1],
                                                            e1[:, n, :], ALU.mult, ALU.add))
                    chain.wait()
                    if g % 2:
                        norm.dve(dve, chain, g - 1)
                for i in range(CHUNK):
                    dve.wait_ge(step_done[0], i + 1)
                    dve.tensor_copy(at_pos(xs, i, 0), k.ps[i % 2][0:D_STATE, 0:P]).then_inc(step_kept[0], 1)
                dve.wait_ge(step_kept[0], CHUNK)
                dve.wait_ge(step_kept[1], CHUNK)
                fin = xs[:].rearrange("s (b c i) -> s b c i", b=B, i=CHUNK)[:, :, :, CHUNK - 1]
                chain.do(dve.tensor_copy(carry[:, 0, :, 1:NC + 1], fin))
                dve.sem_inc(carry_kept, 1)
                for j in range(6):
                    sh = 1 << j
                    old, new = carry[:, j % 2], carry[:, (j + 1) % 2]
                    dve.wait_ge(carry_done, j + 1)
                    acc = k.ps[4 + j % 2][0:D_STATE, 0:B * (NC - sh)].rearrange("s (b c) -> s b c", b=B)
                    chain.step(dve.tensor_copy(new[:, :, 1:1 + sh], old[:, :, 1:1 + sh]))
                    chain.step(dve.tensor_tensor(new[:, :, 1 + sh:], acc, old[:, :, 1 + sh:], ALU.add))
                    chain.wait()
                    dve.sem_inc(carry_kept, 1)
                for i in range(CHUNK):
                    dve.wait_ge(fix_done, i + 1)
                    v = xs[:].rearrange("s (m i) -> s i m", i=CHUNK)[:, i, :]
                    dve.tensor_tensor(v, k.ps[i % 4][0:D_STATE, 0:B * NC], v, ALU.add).then_inc(fix_kept, 1)
                gamma4 = gamma[:, None, :].to_broadcast([P, GT, H])

                def stats(g):
                    if g % 2 == 0:
                        dve.wait_ge(y_kept, min(g + 4, NG) if g else 2)
                    norm2.dve(dve, chain, g, ahead=g > 0)

                def scale(g):
                    dve.wait_ge(norm2.xn_ready, g + 1)
                    if g >= 2:
                        dve.wait_ge(guarded, 2 * (g - 1))
                    dve.tensor_tensor(ya[:, g % 2, :].rearrange("p (n c) -> p n c", c=H),
                                      yn[:, GT * g:GT * g + GT, :], gamma4, ALU.mult).then_inc(scaled, 1)

                def guard(g):
                    s = g % 2
                    dve.wait_ge(guarded, 2 * (g + 1))
                    chain.step(dve.tensor_scalar(finite[:, s, :], yb[:, s, :], 0.0, 0.0, ALU.mult, ALU.is_equal))
                    chain.do(dve.tensor_tensor(known[:, s, :], yb[:, s, :], yb[:, s, :], ALU.is_equal))
                    chain.do(dve.copy_predicated(yd[:, s, :], known[:, s, :].bitcast(U32), yc[:, s, :]))
                    chain.do(dve.copy_predicated(yd[:, s, :], finite[:, s, :].bitcast(U32), yb[:, s, :]))
                    hv = hres[:, GT * g:GT * g + GT, :]
                    dve.tensor_tensor(hv, hv, yd[:, s, :].rearrange("p (n c) -> p n c", c=H), ALU.add).then_inc(h1_ready, 1)

                for g in range(NG + 2):
                    if g < NG:
                        stats(g)
                    if 1 <= g <= NG:
                        scale(g - 1)
                    if g >= 2:
                        guard(g - 2)
                dve.wait_ge(h1_ready, NG)

            @block.scalar
            def _(act):
                act.wait_ge(small_in, 16 * 7)
                for g in range(NG + 1):
                    if g < NG:
                        norm.act_apply(act, g)
                    if g >= 1:
                        norm.act_copy(act, g - 1)
                for i in range(CHUNK):
                    act.wait_ge(step_done[1], i + 1)
                    act.activation(at_pos(xs, i, 1), k.ps[2 + i % 2][0:D_STATE, 0:P], ACT.Copy).then_inc(step_kept[1], 1)

                def gelu(g):
                    act.wait_ge(y_done, g + 1)
                    act.activation(gel[:, GT * g:GT * g + GT, :].rearrange("p n c -> p (n c)"), k.ps[4 + g % 4][:],
                                   ACT.Gelu).then_inc(y_kept, 1)

                for g in range(NG):
                    gelu(g)
                for g in range(NG):
                    norm2.act_apply(act, g)

            @block.tensor
            def _(pe):
                pe.wait_ge(small_in, 16 * 7)
                for j in range(9):
                    a = 1 << j
                    if j:
                        pe.wait_ge(pow_kept, 2 * j)
                    p_a = p_pow[:, j % 2, :]
                    if a < CHUNK:
                        pe.matmul(k.ps[2][0:D_STATE, 0:a * D_STATE], p_a, q_pow[:, 0:a, :].rearrange("s m t -> s (m t)"),
                                  start=True, stop=True).then_inc(pow_done, 1)
                        q_a = q_pow[:, a - 1, :]
                    else:
                        q_a = q_big[:, j - 4, :]
                        if j == 4:
                            pe.wait_ge(dve_chain, 3)
                        pe.matmul(k.ps[2][0:D_STATE, 0:D_STATE], p_a, q_a, start=True, stop=True).then_inc(pow_done, 1)
                    pe.matmul(k.ps[3][0:D_STATE, 0:D_STATE], q_a, p_a, start=True, stop=True).then_inc(pow_done, 1)
                for g in range(NG):
                    norm.pe(pe, g)
                pe.wait_ge(norm.x_t_ready, NG)
                pe.wait_ge(pow_kept, 18)
                for i in range(CHUNK):
                    for s in range(2):
                        out = k.ps[2 * s + i % 2][0:D_STATE, 0:P]
                        if i >= 2:
                            pe.wait_ge(step_kept[s], i - 1)
                        mm = pe.matmul(out, bm_t[:], at_pos(x_t, i, s), start=True, stop=(i == 0))
                        if i >= 1:
                            pe.wait_ge(step_kept[s], i)
                            mm = pe.matmul(out, q_pow[:, 0, :], at_pos(xs, i - 1, s), start=False, stop=True)
                        mm.then_inc(step_done[s], 1)
                for j in range(6):
                    sh = 1 << j
                    pe.wait_ge(carry_kept, j + 1)
                    pe.matmul(k.ps[4 + j % 2][0:D_STATE, 0:B * (NC - sh)].rearrange("s (b c) -> s b c", b=B),
                              q_big[:, j, :], carry[:, j % 2, :, 1:1 + NC - sh], start=True, stop=True).then_inc(carry_done, 1)
                pe.wait_ge(carry_kept, 7)
                for i in range(CHUNK):
                    if i >= 4:
                        pe.wait_ge(fix_kept, i - 3)
                    pe.matmul(k.ps[i % 4][0:D_STATE, 0:B * NC].rearrange("s (b c) -> s b c", b=B), q_pow[:, i, :],
                              carry[:, 0, :, 0:NC], start=True, stop=True).then_inc(fix_done, 1)
                pe.wait_ge(fix_kept, CHUNK)
                for g in range(NG):
                    if g >= 4:
                        pe.wait_ge(y_kept, g - 3)
                    for j in range(GT):
                        n = GT * g + j
                        last = pe.matmul(k.ps[4 + g % 4][:, j * P:(j + 1) * P], xs[:, n * P:(n + 1) * P], c_t[:],
                                         start=True, stop=True)
                    last.then_inc(y_done, 1)


def task_ffn(nc, d, k):
    hres = k.hres
    R = P // NE0
    G1, G2 = FFN // R, H // R
    K9 = NE0 + 1
    with Stage(nc, k, "ffn_") as st:
        sb, sem = st.sb, st.sem
        xn = sb("xn", [P, NT, H], F32)
        x_t = sb("x_t", [P, T], F32)
        gfc1_t = sb("gfc1_t", [P, H], F32)
        gfc1_b = sb("gfc1_b", [P, 1], F32)
        gfc2_rep = sb("gfc2_rep", [P, NE0, R], F32)
        gfc2_b_rep = sb("gfc2_b_rep", [P, 1], F32)
        gfc2_t = sb("gfc2_t", [P, NE0], F32)
        gfc2_b = sb("gfc2_b", [NE0, 1], F32)
        delta = sb("delta", [P, R], F32)
        tv_w1 = sb("tv_w1", [P, G1, H], F32)
        tv_w2 = sb("tv_w2", [P, G2, FFN], F32)
        w1_t = sb("w1_t", [P, FFN], F32)
        w2_t = sb("w2_t", [P, NM, H], F32)
        tv_b1 = sb("tv_b1", [K9, FFN], F32)
        tv_b2 = sb("tv_b2", [K9, H], F32)
        tv_ln = sb("tv_ln", [K9, 2 * H], F32)
        merge_w = sb("merge_w", [K9, P], F32)
        gate_out = sb("gate_out", [P, 2, GC], F32)
        sums = sb("sums", [P, NG], F32)
        mean = sb("mean", [P, B], F32)
        g_rep = sb("g_rep", [P, B], F32)
        g9 = sb("g9", [K9, B], F32)
        g9_wide = sb("g9_wide", [K9, B, P], F32)
        spread = sb("spread", [P, B, R], F32)
        w1m = sb("w1m", [P, B, FFN], F32)
        w2m = sb("w2m", [P, NM, B, H], F32)
        b1m = sb("b1m", [P, NM, B], F32)
        ln_gb = sb("ln_gb", [P, 2 * H], F32)
        hid = sb("hid", [P, 2, NM, GC], F32)
        rn = sb("rn", [P, NT, H], F32)
        b2m = sb("b2m", [P, B, H], F32)

        gate_in, merge_in = sem("gate_in"), sem("merge_in")
        dve_chain = sem("dve_chain")
        gate_done, gate_summed = sem("gate_done"), sem("gate_summed")
        mean_ready, g_done, g_ready = sem("mean_ready"), sem("g_done"), sem("g_ready")
        merged, merge_kept = sem("merged"), sem("merge_kept")
        bias_done, bias_kept = sem("bias_done"), sem("bias_kept")
        hid_done = sem("hid_done")
        hid_act, hid_dve = sem("hid_act"), sem("hid_dve")
        res_done, x_b2_ready, res_kept = sem("res_done"), sem("x_b2_ready"), sem("res_kept")
        lnb_added, h2_ready = sem("lnb_added"), sem("h2_ready")
        norm = Norm(st, "n0", tile_of(hres), tile_of(xn), [k.ps[0], k.ps[1]],
                    lambda act, g, bank: act.activation(x_t[:, g * GC:(g + 1) * GC], bank[:], ACT.Copy), k.ident)
        res = lambda n: k.ps[4 + n // GT % 4][:, n % GT * P:(n % GT + 1) * P]
        norm2 = Norm(st, "n1", tile_of(rn), tile_of(rn), None, None, None)
        gate_loads = ((gfc1_t[:], "gfc1_t"), (gfc1_b[:], "gfc1_b"), (gfc2_rep[:], "gfc2_rep"),
                      (gfc2_b_rep[:], "gfc2_b_rep"), (gfc2_t[:], "gfc2_t"), (gfc2_b[:], "gfc2_b"), (delta[:], "delta"))
        merge_loads = ((tv_w1[:], "tv_w1"), (tv_w2[:], "tv_w2"), (w1_t[:], "w1_t"), (w2_t[:], "w2_t"),
                       (tv_b1[:], "tv_b1"), (tv_b2[:], "tv_b2"), (tv_ln[:], "tv_ln"), (merge_w[:], "merge_w"))

        with nc.Block() as block:
            @block.sync
            def _(sp):
                for dst, src in gate_loads:
                    sp.dma_start(dst, d[src]).then_inc(gate_in, 16)
                for dst, src in merge_loads:
                    sp.dma_start(dst, d[src]).then_inc(merge_in, 16)

            @block.gpsimd
            def _(pool):
                lnb4 = ln_gb[:, None, H:2 * H].to_broadcast([P, GT, H])
                pool.wait_ge(bias_kept, 3)
                pool.wait_ge(norm.turned, NG)
                for g in range(NG):
                    xv = xn[:, GT * g:GT * g + GT, :]
                    pool.tensor_tensor(xv, xv, b2m[:, g // 2, None, :].to_broadcast([P, GT, H]),
                                       ALU.add).then_inc(x_b2_ready, 1)
                    hv = hres[:, GT * g:GT * g + GT, :]
                    pool.tensor_tensor(hv, hv, lnb4, ALU.add).then_inc(lnb_added, 1)

            @block.vector
            def _(dve):
                chain = Chain(dve, dve_chain)
                chain.step(dve.memset(g9[:], 1.0))
                for g in range(NG):
                    norm.dve(dve, chain, g, ahead=True)
                dve.wait_ge(gate_summed, NG)
                pair = sums[:].rearrange("p (b t) -> p b t", t=2)
                chain.do(dve.tensor_tensor(mean[:], pair[:, :, 0], pair[:, :, 1], ALU.add))
                chain.do(dve.tensor_scalar(mean[:], mean[:], 1.0 / S, None, ALU.mult))
                dve.sem_inc(mean_ready, 1)
                dve.wait_ge(gate_in, 16 * len(gate_loads))
                dve.wait_ge(g_done, 1)
                chain.do(dve.tensor_scalar(g_rep[:], k.ps[4][:, 0:B], gfc2_b_rep[:, 0:1], None, ALU.add))
                chain.do(dve.tensor_scalar(g9[0:NE0, :], k.ps[4][0:NE0, B:2 * B], gfc2_b[:, 0:1], None, ALU.add))
                for b in range(B):
                    chain.step(dve.tensor_scalar(spread[:, b, :], delta[:], g_rep[:, b:b + 1], None, ALU.mult))
                chain.do(dve.tensor_copy(g9_wide[:], g9[:, :, None].to_broadcast([K9, B, P])))
                dve.sem_inc(g_ready, 1)
                dve.wait_ge(merge_in, 16 * len(merge_loads))
                for q in range(4):
                    dve.wait_ge(merged, q + 1)
                    acc = k.ps[q][:].rearrange("p (j b r) -> p b r j", j=8, b=B)
                    out = w1m[:].rearrange("p b (r g) -> p b r g", g=G1)[:, :, :, 8 * q:8 * q + 8]
                    base = w1_t[:].rearrange("p (r g) -> p r g", g=G1)[:, None, :, 8 * q:8 * q + 8]
                    for b in range(B):
                        last = dve.tensor_tensor(out[:, b], acc[:, b], base[:, 0], ALU.add)
                    last.then_inc(merge_kept, 1)
                for m in range(NM):
                    dve.wait_ge(merged, 4 + m + 1)
                    acc = k.ps[4 + m][:].rearrange("p (j b r) -> p b r j", j=G2, b=B)
                    for b in range(B):
                        last = dve.tensor_tensor(w2m[:, m, b, :].rearrange("p (r g) -> p r g", g=G2), acc[:, b],
                                                 w2_t[:, m, :].rearrange("p (r g) -> p r g", g=G2), ALU.add)
                    last.then_inc(merge_kept, 1)
                dve.wait_ge(bias_done, 1)
                dve.tensor_copy(b1m[:].rearrange("p m b -> p (m b)"), k.ps[0][:, 0:NM * B]).then_inc(bias_kept, 1)
                dve.tensor_copy(ln_gb[:], k.ps[1][:, 0:2 * H]).then_inc(bias_kept, 1)
                dve.tensor_copy(b2m[:].rearrange("p b c -> p (b c)"), k.ps[2][:]).then_inc(bias_kept, 1)
                dve.wait_ge(bias_kept, 3)
                lng4 = ln_gb[:, None, 0:H].to_broadcast([P, GT, H])

                def hidden(u):
                    for m in (2, 3):
                        dve.wait_ge(hid_done, NM * u + m + 1)
                        if u >= 2:
                            dve.wait_ge(res_done, u - 1)
                        dve.tensor_scalar(hid[:, u % 2, m, :], k.ps[m][:], b1m[:, m, u // 2:u // 2 + 1], 0.0,
                                          ALU.add, ALU.max).then_inc(hid_dve, 1)

                def finish(g):
                    dve.wait_ge(norm2.xn_ready, g + 1)
                    rv = rn[:, GT * g:GT * g + GT, :]
                    hv = hres[:, GT * g:GT * g + GT, :]
                    chain.do(dve.tensor_tensor(rv, rv, lng4, ALU.mult))
                    dve.wait_ge(lnb_added, g + 1)
                    dve.tensor_tensor(hv, hv, rv, ALU.add).then_inc(h2_ready, 1)

                def residual(g):
                    dve.wait_ge(res_done, g + 1)
                    dve.wait_ge(x_b2_ready, g + 1)
                    tiles = slice(GT * g, GT * g + GT)
                    dve.tensor_tensor(rn[:, tiles, :].rearrange("p n c -> p (n c)"), k.ps[4 + g % 4][:],
                                      xn[:, tiles, :].rearrange("p n c -> p (n c)"), ALU.add).then_inc(res_kept, 1)

                for u in range(NG):
                    hidden(u)
                    if u >= 1:
                        residual(u - 1)
                    if u % 2 == 0 and u >= 2:
                        dve.wait_ge(res_kept, u)
                        norm2.dve(dve, chain, u - 2)
                    if u >= 4:
                        finish(u - 4)
                residual(NG - 1)
                dve.wait_ge(res_kept, NG)
                norm2.dve(dve, chain, NG - 2)
                for g in range(NG - 4, NG):
                    finish(g)
                dve.wait_ge(h2_ready, NG)

            @block.scalar
            def _(act):
                def gate(g):
                    act.wait_ge(gate_done, g + 1)
                    if g >= 2:
                        act.wait_ge(gate_summed, g - 1)
                    act.activation(gate_out[:, g % 2, :], k.ps[2 + g % 2][:], ACT.Relu, bias=gfc1_b[:, 0:1],
                                   accum_out=sums[:, g:g + 1]).then_inc(gate_summed, 1)

                act.wait_ge(gate_in, 16 * len(gate_loads))
                for g in range(NG + 2):
                    if g < NG:
                        norm.act_apply(act, g)
                    if 1 <= g <= NG:
                        norm.act_copy(act, g - 1)
                    if g >= 2:
                        gate(g - 2)
                act.wait_ge(bias_kept, 1)

                def hidden(u):
                    for m in (0, 1):
                        act.wait_ge(hid_done, NM * u + m + 1)
                        if u >= 2:
                            act.wait_ge(res_done, u - 1)
                        act.activation(hid[:, u % 2, m, :], k.ps[m][:], ACT.Relu,
                                       bias=b1m[:, m, u // 2:u // 2 + 1]).then_inc(hid_act, 1)

                for u in range(NG):
                    hidden(u)
                    if u >= 3:
                        norm2.act_apply(act, u - 3)
                for g in range(NG - 3, NG):
                    norm2.act_apply(act, g)

            @block.tensor
            def _(pe):
                def gate(g):
                    pe.wait_ge(norm.x_t_ready, g + 1)
                    if g >= 2:
                        pe.wait_ge(gate_summed, g - 1)
                    pe.matmul(k.ps[2 + g % 2][:], gfc1_t[:], x_t[:, g * GC:(g + 1) * GC], start=True,
                              stop=True).then_inc(gate_done, 1)

                pe.wait_ge(gate_in, 16 * len(gate_loads))
                for g in range(NG + 1):
                    if g < NG:
                        norm.pe(pe, g)
                    if g >= 1:
                        gate(g - 1)
                pe.wait_ge(mean_ready, 1)
                pe.matmul(k.ps[4][:, 0:B], gfc2_rep[:].rearrange("p e r -> p (e r)"), mean[:], start=True, stop=True)
                pe.matmul(k.ps[4][0:NE0, B:2 * B], gfc2_t[:], mean[:], start=True, stop=True).then_inc(g_done, 1)
                pe.wait_ge(g_ready, 1)
                pe.wait_ge(merge_in, 16 * len(merge_loads))
                pe.wait_ge(gate_summed, NG)
                g_cols = spread[:].rearrange("p b r -> p (b r)")
                for q in range(4):
                    for j in range(8):
                        last = pe.matmul(k.ps[q][:, j * B * R:(j + 1) * B * R], tv_w1[:, 8 * q + j, :], g_cols,
                                         start=True, stop=True)
                    last.then_inc(merged, 1)
                for m in range(NM):
                    for j in range(G2):
                        last = pe.matmul(k.ps[4 + m][:, j * B * R:(j + 1) * B * R],
                                         tv_w2[:, j, m * P:(m + 1) * P], g_cols, start=True, stop=True)
                    last.then_inc(merged, 1)
                pe.wait_ge(merge_kept, 3)
                for m in range(NM):
                    pe.matmul(k.ps[0][:, m * B:(m + 1) * B], tv_b1[:, m * P:(m + 1) * P], g9[:], start=True, stop=True)
                for b in range(B):
                    pe.matmul(k.ps[2][:, b * H:(b + 1) * H], g9_wide[:, b, :], tv_b2[:], start=True, stop=True)
                pe.matmul(k.ps[1][:, 0:2 * H], merge_w[:], tv_ln[:], start=True, stop=True).then_inc(bias_done, 1)
                pe.wait_ge(merge_kept, 8)
                pe.wait_ge(bias_kept, 3)

                def hidden(u):
                    for m in range(NM):
                        if u >= 1:
                            pe.wait_ge((hid_act, hid_dve)[m // 2], 2 * (u - 1) + m % 2 + 1)
                        pe.matmul(k.ps[m][:], w1m[:, u // 2, m * P:(m + 1) * P], x_t[:, u * GC:(u + 1) * GC],
                                  start=True, stop=True).then_inc(hid_done, 1)

                def product(u):
                    pe.wait_ge(hid_act, 2 * (u + 1))
                    pe.wait_ge(hid_dve, 2 * (u + 1))
                    if u >= 4:
                        pe.wait_ge(res_kept, u - 3)
                    for j in range(GT):
                        n = GT * u + j
                        for m in range(NM):
                            last = pe.matmul(res(n), hid[:, u % 2, m, j * P:(j + 1) * P], w2m[:, m, u // 2, :],
                                             start=(m == 0), stop=(m == NM - 1))
                    last.then_inc(res_done, 1)

                for u in range(NG + 1):
                    if u < NG:
                        hidden(u)
                    if u >= 1:
                        product(u - 1)


def linear_attention(nc, d, k):
    hres = k.hres
    BT = 2 * GC
    with Stage(nc, k, "lin_", recycle=True) as st:
        sb, sem = st.sb, st.sem
        xn = sb("xn", [P, NT, H], F32)
        x_t = sb("x_t", [P, B, S + 2], F32)
        w_qk = sb("w_qk", [P, 2 * H], F32)
        b_q = sb("b_q", [P, 1], F32)
        b_k = sb("b_k", [1, H], F32)
        ones = sb("ones", [P, P], F32)
        cos_tok, sin_tok = sb("cos_tok", [P, TB, H], F32), sb("sin_tok", [P, TB, H], F32)
        cos_feat, sin_feat = sb("cos_feat", [P, S], F32), sb("sin_feat", [P, S], F32)
        rot, rot_t = sb("rot", [P, P], F32), sb("rot_t", [P, P], F32)
        head_mask = sb("head_mask", [P, P], F32)
        head_cols = sb("head_cols", [P, NH], F32)
        lepe_w = sb("lepe_w", [P, 3], F32)
        lepe_diag = sb("lepe_diag", [P, 3, P], F32)
        lepe_b = sb("lepe_b", [P, H], F32)
        ex = sb("ex", [P, 4, GC], F32)
        rl = sb("rl", [P, 4, GC], F32)
        kk = sb("kk", [P, 2, TB, H], F32)
        k_cos, k_sin = sb("k_cos", [P, 2, TB, H], F32), sb("k_sin", [P, 2, TB, H], F32)
        qq = sb("qq", [P, 2, BT], F32)
        q_cos, q_sin = sb("q_cos", [P, 2, BT], F32), sb("q_sin", [P, 2, BT], F32)
        k_sum = sb("k_sum", [P, 2, H], F32)
        m2 = sb("m2", [P, H], F32)
        kv, kv_rot = sb("kv", [P, H], F32), sb("kv_rot", [P, H], F32)
        k_mean = sb("k_mean", [P, 1], F32)
        k_cols = sb("k_cols", [P, NH], F32)
        z = sb("z", [P, GT * NH], F32)
        mixed = sb("mixed", [P, GC], F32)

        loaded = sem("loaded")
        dve_chain, pool_chain = sem("dve_chain"), sem("pool_chain")
        pads_ready, lepe_ready, lepe_b_added = sem("pads_ready"), sem("lepe_ready"), sem("lepe_b_added")
        proj_done, elu_parts, elu_ready = sem("proj_done"), sem("elu_parts"), sem("elu_ready")
        cos_ready, sin_ready, ksum_ready = sem("cos_ready"), sem("sin_ready"), sem("ksum_ready")
        m_done, m2_kept, kv_done, kv_kept = sem("m_done"), sem("m2_kept"), sem("kv_done"), sem("kv_kept")
        kv_rot_done, kv_rot_kept = sem("kv_rot_done"), sem("kv_rot_kept")
        out_done, num_used, h3_ready = sem("out_done"), sem("num_used"), sem("h3_ready")

        def copy_out(act, g, bank):
            at = 1 + g % 2 * GC
            return act.activation(x_t[:, g // 2, at:at + GC], bank[:], ACT.Copy)

        norm = Norm(st, "n0", tile_of(hres), tile_of(xn), [k.ps[0], k.ps[1]], copy_out, k.ident)
        loads = ((w_qk[:], "w_qk"), (b_q[:], "b_q"), (b_k[:], "b_k"), (ones[:], "ones"), (cos_tok[:], "cos_tok"),
                 (sin_tok[:], "sin_tok"), (cos_feat[:], "cos_feat"), (sin_feat[:], "sin_feat"), (rot[:], "rot"),
                 (rot_t[:], "rot_t"), (head_mask[:], "head_mask"), (head_cols[:], "head_cols"),
                 (lepe_w[:], "lepe_w"), (lepe_b[:], "lepe_b"))
        UNITS = 4

        def tok(t, b, h):
            return t[:, b % 2, GT * h:GT * h + GT, :].rearrange("p n c -> p (n c)")

        with nc.Block() as block:
            @block.sync
            def _(sp):
                for dst, src in loads:
                    sp.dma_start(dst, d[src]).then_inc(loaded, 16)
                zeros_out(sp, k)

            @block.gpsimd
            def _(pool):
                pool.memset(k.xa[:], 0.0).then_inc(k.zeroed, 1)
                for b in range(B):
                    pool.memset(x_t[:, b, 0:1], 0.0).then_inc(pads_ready, 1)
                    pool.memset(x_t[:, b, S + 1:S + 2], 0.0).then_inc(pads_ready, 1)
                pool.wait_ge(loaded, 16 * len(loads))
                lepe_b4 = lepe_b[:, None, :].to_broadcast([P, GT, H])
                for b in range(B):
                    for g in (2 * b, 2 * b + 1):
                        pool.wait_ge(norm.xn_ready, g + 1)
                        hv = hres[:, GT * g:GT * g + GT, :]
                        pool.tensor_tensor(hv, hv, lepe_b4, ALU.add).then_inc(lepe_b_added, 1)
                    for u in range(UNITS):
                        h = u % 2
                        pool.wait_ge(elu_ready, UNITS * b + u + 1)
                        if u < 2:
                            if b >= 2:
                                pool.wait_ge(m_done, b - 1)
                            pool.tensor_tensor(tok(k_sin, b, h), tok(kk, b, h),
                                               sin_tok[:, GT * h:GT * h + GT, :].rearrange("p n c -> p (n c)"),
                                               ALU.mult).then_inc(sin_ready, 1)
                        else:
                            if b >= 2:
                                pool.wait_ge(out_done, 2 * (b - 1))
                            cols = slice(h * GC, (h + 1) * GC)
                            pool.tensor_tensor(q_sin[:, b % 2, cols], qq[:, b % 2, cols], sin_feat[:, cols],
                                               ALU.mult).then_inc(sin_ready, 1)

            @block.vector
            def _(dve):
                chain = Chain(dve, dve_chain)
                norm.dve(dve, chain, 0, ahead=True)
                norm.dve(dve, chain, 2, ahead=True)
                dve.wait_ge(loaded, 16 * len(loads))
                for j in range(3):
                    dve.tensor_scalar(lepe_diag[:, j, :], k.ident[:], lepe_w[:, j:j + 1], None,
                                      ALU.mult).then_inc(lepe_ready, 1)

                def elus(b):
                    for u in range(UNITS):
                        h, n = u % 2, UNITS * b + u
                        dve.wait_ge(elu_parts, 2 * (n + 1))
                        if b >= 2:
                            dve.wait_ge(m_done if u < 2 else out_done, b - 1 if u < 2 else 2 * (b - 1))
                            dve.wait_ge(sin_ready, UNITS * (b - 2) + u + 1)
                        v = tok(kk, b, h) if u < 2 else qq[:, b % 2, h * GC:(h + 1) * GC]
                        dve.scalar_tensor_tensor(v, ex[:, n % 4, :], 1.0, rl[:, n % 4, :], ALU.min,
                                                 ALU.add).then_inc(elu_ready, 1)
                        dve.wait_ge(elu_ready, n + 1)
                        if u < 2:
                            dve.tensor_tensor(tok(k_cos, b, h), v,
                                              cos_tok[:, GT * h:GT * h + GT, :].rearrange("p n c -> p (n c)"),
                                              ALU.mult).then_inc(cos_ready, 1)
                        else:
                            cols = slice(h * GC, (h + 1) * GC)
                            dve.tensor_tensor(q_cos[:, b % 2, cols], v, cos_feat[:, cols],
                                              ALU.mult).then_inc(cos_ready, 1)
                    if b >= 2:
                        dve.wait_ge(kv_done, b - 1)
                    dve.tensor_reduce(k_sum[:, b % 2, :], kk[:, b % 2].rearrange("p n c -> p c n"), AXX,
                                      ALU.add).then_inc(ksum_ready, 1)

                def matrices(b):
                    dve.wait_ge(m_done, b + 1)
                    dve.tensor_copy(m2[:], k.ps[5][:, 0:H]).then_inc(m2_kept, 1)
                    chain.do(dve.tensor_copy(k_mean[:], k.ps[5][:, 2 * H:2 * H + 1]))
                    if b:
                        dve.wait_ge(out_done, 2 * b)
                    chain.step(dve.tensor_scalar(k_cols[:], head_cols[:], k_mean[:, 0:1], None, ALU.mult))
                    dve.wait_ge(kv_done, b + 1)
                    chain.do(dve.tensor_tensor(kv[:], k.ps[4][:, 0:H], head_mask[:], ALU.mult))
                    dve.sem_inc(kv_kept, 1)
                    dve.wait_ge(kv_rot_done, b + 1)
                    dve.tensor_copy(kv_rot[:], k.ps[5][:, H:2 * H]).then_inc(kv_rot_kept, 1)

                def outputs(g):
                    dve.wait_ge(out_done, g + 1)
                    chain.do(dve.tensor_scalar(z[:], k.ps[4][:, P:P + GT * NH], 1e-6, None, ALU.add))
                    chain.do(dve.reciprocal(z[:], z[:]))
                    chain.do(dve.tensor_tensor(mixed[:].rearrange("p (m e) -> p m e", e=DH),
                                               k.ps[6][:].rearrange("p (m e) -> p m e", e=DH),
                                               z[:, :, None].to_broadcast([P, GT * NH, DH]), ALU.mult))
                    dve.sem_inc(num_used, 1)
                    dve.wait_ge(lepe_b_added, g + 1)
                    hv = hres[:, GT * g:GT * g + GT, :].rearrange("p n c -> p (n c)")
                    chain.do(dve.tensor_tensor(hv, hv, mixed[:], ALU.add))
                    dve.tensor_tensor(hv, hv, k.ps[7][:], ALU.add).then_inc(h3_ready, 1)

                for b in range(B + 1):
                    if b + 2 < B:
                        norm.dve(dve, chain, 2 * (b + 2), ahead=True)
                    if b < B:
                        elus(b)
                    if b >= 1:
                        matrices(b - 1)
                        outputs(2 * b - 2)
                        outputs(2 * b - 1)
                dve.wait_ge(h3_ready, NG)

            @block.scalar
            def _(act):
                for g in (0, 1):
                    norm.act_apply(act, g)
                for g in (0, 1):
                    norm.act_copy(act, g)
                act.wait_ge(loaded, 16 * len(loads))
                for n in range(UNITS * B):
                    u = n % UNITS
                    if u == 0:
                        for g in range(n // 2 + 2, min(n // 2 + 4, NG)):
                            norm.act_apply(act, g)
                    act.wait_ge(proj_done, n + 1)
                    if n >= 4:
                        act.wait_ge(elu_ready, n - 3)
                    bias = 0.0 if u < 2 else b_q[:, 0:1]
                    act.activation(ex[:, n % 4, :], k.ps[2 + u % 2][:], ACT.Exp, bias=bias).then_inc(elu_parts, 1)
                    act.activation(rl[:, n % 4, :], k.ps[2 + u % 2][:], ACT.Relu, bias=bias).then_inc(elu_parts, 1)
                    if u == UNITS - 1:
                        for g in range(n // UNITS * 2 + 2, min(n // UNITS * 2 + 4, NG)):
                            norm.act_copy(act, g)

            @block.tensor
            def _(pe):
                for g in (0, 1):
                    norm.pe(pe, g)
                pe.wait_ge(loaded, 16 * len(loads))
                pe.wait_ge(pads_ready, 2 * B)
                pe.wait_ge(lepe_ready, 3)

                def project(b):
                    pe.wait_ge(norm.x_t_ready, 2 * b + 2)
                    for u in range(UNITS):
                        h = u % 2
                        if UNITS * b + u >= 2:
                            pe.wait_ge(elu_parts, 2 * (UNITS * b + u - 1))
                        bank = k.ps[2 + u % 2]
                        if u < 2:
                            for j in range(GT):
                                at = 1 + (GT * h + j) * P
                                out = bank[:, j * P:(j + 1) * P]
                                pe.matmul(out, ones[0:1, :], b_k[:], start=True, stop=False)
                                last = pe.matmul(out, x_t[:, b, at:at + P], w_qk[:, H:2 * H], start=False, stop=True)
                        else:
                            last = pe.matmul(bank[:], w_qk[:, 0:H], x_t[:, b, 1 + h * GC:1 + (h + 1) * GC],
                                             start=True, stop=True)
                        last.then_inc(proj_done, 1)

                def matrices(b):
                    pe.wait_ge(cos_ready, UNITS * b + 2)
                    pe.wait_ge(sin_ready, UNITS * b + 2)
                    pe.wait_ge(ksum_ready, b + 1)
                    if b:
                        pe.wait_ge(num_used, 2 * b)
                    for part, bank in ((k_cos, k.ps[4]), (k_sin, k.ps[5])):
                        for n in range(TB):
                            pe.matmul(bank[:, 0:H], part[:, b % 2, n, :], xn[:, TB * b + n, :], start=(n == 0),
                                      stop=(n == TB - 1 and part is k_sin))
                    pe.matmul(k.ps[5][:, 2 * H:2 * H + 1], k_sum[:, b % 2, :], ones[:, 0:1], start=True,
                              stop=True).then_inc(m_done, 1)
                    pe.wait_ge(m2_kept, b + 1)
                    pe.matmul(k.ps[4][:, 0:H], rot_t[:], m2[:], start=False, stop=True).then_inc(kv_done, 1)
                    pe.wait_ge(kv_kept, b + 1)
                    pe.matmul(k.ps[5][:, H:2 * H], rot[:], kv[:], start=True, stop=True).then_inc(kv_rot_done, 1)
                    pe.wait_ge(kv_rot_kept, b + 1)

                def outputs(g):
                    b, h = g // 2, g % 2
                    pe.wait_ge(cos_ready, UNITS * b + 4)
                    pe.wait_ge(sin_ready, UNITS * b + 4)
                    if g:
                        pe.wait_ge(num_used, g)
                    for j in range(GT):
                        cols = slice(h * GC + j * P, h * GC + (j + 1) * P)
                        pe.matmul(k.ps[4][:, P + j * NH:P + (j + 1) * NH], qq[:, b % 2, cols], k_cols[:], start=True, stop=True)
                        num = k.ps[6][:, j * P:(j + 1) * P]
                        pe.matmul(num, q_cos[:, b % 2, cols], kv[:], start=True, stop=False)
                        pe.matmul(num, q_sin[:, b % 2, cols], kv_rot[:], start=False, stop=True)
                    if g:
                        pe.wait_ge(h3_ready, g)
                    for j in range(GT):
                        cols = slice(h * GC + j * P, h * GC + (j + 1) * P)
                        for t in range(3):
                            last = pe.matmul(k.ps[7][:, j * P:(j + 1) * P], x_t[:, b, cols.start + t:cols.stop + t],
                                             lepe_diag[:, t, :], start=(t == 0), stop=(t == 2))
                    last.then_inc(out_done, 1)

                for b in range(B + 1):
                    if b < B:
                        project(b)
                    if b >= 1:
                        matrices(b - 1)
                        outputs(2 * b - 2)
                    for g in range(2 * b + 2, min(2 * b + 4, NG)):
                        norm.pe(pe, g)
                    if b >= 1:
                        outputs(2 * b - 1)


def softmax_attention(nc, d, k):
    hres = k.hres
    HG = 4
    UNITS = B * NH // HG
    STEPS = 2 * (TB // 2) * HG
    PARTS = 2 * UNITS
    MAXES = HG * TB
    AHEAD = MAXES + 12
    Q_TERMS, K_TERMS = (0, 0, 0, 1, 1, 2), (0, 1, 2, 0, 1, 0)
    ROWS = len(Q_TERMS) * DH
    SLOTS, P_SLOTS = 3, 8
    LAST = UNITS * STEPS
    GROUPS = LAST // HG

    terms_dram = nc.dram_tensor("terms_dram", (2, B, 3, H, S), BF16).ap()
    max_dram = nc.dram_tensor("max_dram", (PARTS, 3, HG, GC), BF16).ap()
    with Stage(nc, k, "att_") as st:
        sb, sem = st.sb, st.sem
        xa = k.xa
        x1 = sb("x1", [P, 2, GT, H], F32)
        x_t = sb("x_t", [P, T], F32)
        att = x_t[:].rearrange("p (n c) -> p n c", c=H)
        w_q, w_k, w_v, w_o = (sb(n, [P, H], F32) for n in ("w_q", "w_k", "w_v", "w_o"))
        ln_g, ln_b = sb("ln_g", [P, 1], F32), sb("ln_b", [P, 1], F32)
        ident16 = sb("ident16", [P, P], BF16)
        vv = sb("vv", [P, NT, NH, 2 * DH], F32)
        terms = sb("terms", [P, 4, 3, GC], BF16)
        rest = sb("rest", [P, 4, GC], F32)
        q6 = sb("q6", [P, SLOTS, HG, S], BF16)
        k6 = sb("k6", [P, SLOTS, HG, S], BF16)
        probs = sb("probs", [P, P_SLOTS, 2 * GC], F32)
        maxes = sb("maxes", [P, 2, MAXES], F32)
        row_max = sb("row_max", [P, 2, MAXES // 2], F32)
        neg_max = sb("neg_max", [P, 2, MAXES // 2], F32)
        max_terms = sb("max_terms", [P, 3, MAXES // 2], BF16)
        max_rows = sb("max_rows", [3 * MAXES // 2, P], BF16)
        mixed = sb("mixed", [P, GC], F32)
        r_sum = sb("r_sum", [P, GT, HG], F32)
        att_t = sb("att_t", [P, 2, GC], F32)

        loaded, v_set, ident_set, k_ones_set = sem("loaded"), sem("v_set"), sem("ident_set"), sem("k_ones_set")
        dve_chain = sem("dve_chain")
        qk_done, v_done, v_kept = sem("qk_done"), sem("v_done"), sem("v_kept")
        term1, rest1, term2, term3 = sem("term1"), sem("rest1"), sem("term2"), sem("term3")
        terms_out = [sem(f"terms_out{i}") for i in range(4)]
        qk_in = [sem(f"qk_in{i}") for i in range(SLOTS)]
        max_in = [[sem(f"max_in{i}_{qh}") for qh in range(2)] for i in range(SLOTS)]
        tile_scored, bank_freed = sem("tile_scored"), sem("bank_freed")
        row_max_ready, pool_chain = sem("row_max_ready"), sem("pool_chain")
        max_split, max_turned, max_out = sem("max_split"), sem("max_turned"), sem("max_out")
        scored, exp_done, pv_done = sem("scored"), sem("exp_done"), sem("pv_done")
        mixed_kept, mixed_turned = sem("mixed_kept"), sem("mixed_turned")
        att_turned, att_t_ready, wo_done, h4_ready = sem("att_turned"), sem("att_t_ready"), sem("wo_done"), sem("h4_ready")
        norm = Norm(st, "n0", tile_of(hres), tile_of(xa), [k.ps[0], k.ps[1]],
                    lambda act, g, bank: act.activation(x_t[:, g * GC:(g + 1) * GC], bank[:], ACT.Identity,
                                                        bias=ln_b[:, 0:1], scale=ln_g[:, 0:1]), k.ident,
                    again=lambda n: x1[:, n // GT % 2, n % GT, :])
        loads = ((w_q[:], "w_q"), (w_k[:], "w_k"), (w_v[:], "w_v"), (w_o[:], "w_o"), (ln_g[:], "ln1_g"),
                 (ln_b[:], "ln1_b"))

        def step_of(t):
            u, s = divmod(t, STEPS)
            return u, s // (STEPS // 2), s // HG % (TB // 2), s % HG

        def max_of(i):
            w, r = divmod(i, MAXES)
            return w, r // TB, w % 2 * GT + r // 2 % GT, r % 2

        def maxes_at(t):
            if t < 0:
                return range(AHEAD)
            return range(min(AHEAD + 2 * t, PARTS * MAXES), min(AHEAD + 2 * t + 2, PARTS * MAXES))

        PV_LAG, KEEP_LAG, TURN_LAG = 5, 8, 9

        def group_at(t, lag):
            n = t - lag
            return n // HG if n >= 0 and n % HG == 0 and n // HG < GROUPS else None

        def output_at(t, lag):
            g = group_at(t, lag)
            return None if g is None or g % (TB // 2) != TB // 2 - 1 else g // (TB // 2)

        SPARE = (4, 5, 7)
        stream, use_of = {}, {}

        def use(t, kind, x):
            stream[t].append((len(use_of), kind, x))
            use_of[kind, x] = len(use_of)

        for t in range(-1, LAST + TURN_LAG):
            stream[t] = []
            for i in maxes_at(t):
                use(t, "max", i)
                if i >= MAXES and i % MAXES == 3:
                    use(t, "turn_max", i // MAXES - 1)
                if i == PARTS * MAXES - 1:
                    use(t, "turn_max", PARTS - 1)
            if output_at(t, TURN_LAG) is not None:
                use(t, "turn", output_at(t, TURN_LAG))

        def spare_bank(n):
            return k.ps[SPARE[n % len(SPARE)]]

        def qk_bank(n):
            return k.ps[2 + n % 4]

        def v_bank(g):
            return k.ps[6 + g % 2]

        with nc.Block() as block:
            @block.sync
            def _(sp):
                for dst, src in loads:
                    sp.dma_start(dst, d[src]).then_inc(loaded, 16)
                def load(u):
                    b, hg, slot = u // 2, u % 2, u % SLOTS
                    if u >= SLOTS:
                        sp.wait_ge(scored, STEPS * (u - SLOTS + 1))
                    for j, (dst, order) in enumerate(((q6, Q_TERMS), (k6, K_TERMS))):
                        for r, term in enumerate(order):
                            src = terms_dram[j, b, term, hg * HG * DH:(hg + 1) * HG * DH, :].rearrange(
                                "(h e) s -> e h s", e=DH)
                            sp.dma_start(dst[r * DH:(r + 1) * DH, slot], src).then_inc(qk_in[slot], 16)

                def max_rows_in(w):
                    slot, qh = w // 2 % SLOTS, w % 2
                    sp.wait_ge(bank_freed, use_of["turn_max", w] + 1)
                    sp.dma_start(max_dram[w].rearrange("t h (n p) -> (t h n) p", p=P), max_rows[:]).then_inc(max_out, 16)
                    sp.wait_ge(max_out, 16 * (w + 1))
                    sp.dma_start(q6[ROWS:ROWS + 3, slot, :, qh * GC:(qh + 1) * GC],
                                 max_dram[w]).then_inc(max_in[slot][qh], 16)

                for n in range(2 * NG):
                    g, j = n // 2, n % 2
                    sp.wait_ge(term1, n + 1)
                    sp.wait_ge(term2, n + 1)
                    sp.wait_ge(term3, n + 1)
                    dst = terms_dram[j, g // 2, :, :, g % 2 * GC:(g % 2 + 1) * GC].rearrange("t c s -> c t s")
                    sp.dma_start(dst, terms[:, n % 4]).then_inc(terms_out[n % 4], 16)
                    if n % 4 == 1 and n >= 5:
                        batch = n // 4 - 1
                        for i in range(4):
                            sp.wait_ge(terms_out[i], 16 * (batch + 1))
                        for u in range(2 * batch, min(2 * batch + 2, SLOTS)):
                            load(u)
                for i in range(4):
                    sp.wait_ge(terms_out[i], 16 * 2 * NG // 4)
                for u in range(UNITS):
                    max_rows_in(2 * u)
                    max_rows_in(2 * u + 1)
                    if 1 <= u and u + SLOTS - 1 < UNITS:
                        load(u + SLOTS - 1)

            @block.gpsimd
            def _(pool):
                pool.memset(vv[:], 0.0).then_inc(v_set, 1)
                pool.wait_ge(v_set, 1)
                pool.memset(vv[:, :, :, DH:DH + 1], 1.0).then_inc(v_set, 1)
                pool.wait_ge(v_set, 2)
                pool.memset(k6[ROWS:ROWS + 3], 1.0).then_inc(k_ones_set, 1)
                pool.wait_ge(k_ones_set, 1)
                for n in range(2 * NG):
                    pool.wait_ge(term2, n + 1)
                    if n >= 4:
                        pool.wait_ge(terms_out[n % 4], 16 * (n // 4))
                    pool.tensor_tensor(terms[:, n % 4, 2, :], rest[:, n % 4, :], terms[:, n % 4, 1, :],
                                       ALU.subtract).then_inc(term3, 1)
                chain = Chain(pool, pool_chain)
                pool.wait_ge(term3, 2 * NG)
                for w in range(PARTS):
                    pool.wait_ge(row_max_ready, w + 1)
                    if w:
                        pool.wait_ge(max_turned, w)
                    neg, r = neg_max[:, 0, :], neg_max[:, 1, :]
                    chain.do(pool.tensor_scalar(neg, row_max[:, w % 2, :], -1.0, None, ALU.mult))
                    chain.do(pool.tensor_copy(max_terms[:, 0, :], neg))
                    chain.do(pool.tensor_tensor(r, neg, max_terms[:, 0, :], ALU.subtract))
                    chain.do(pool.tensor_copy(max_terms[:, 1, :], r))
                    chain.do(pool.tensor_tensor(max_terms[:, 2, :], r, max_terms[:, 1, :], ALU.subtract))
                    pool.sem_inc(max_split, 1)

            @block.vector
            def _(dve):
                chain = Chain(dve, dve_chain)
                dve.tensor_copy(ident16[:], k.ident[:]).then_inc(ident_set, 1)

                def split(g):
                    for n in (2 * g, 2 * g + 1):
                        dve.wait_ge(term1, n + 1)
                        if n >= 4:
                            dve.wait_ge(term3, n - 3)
                        dve.tensor_tensor(rest[:, n % 4, :], qk_bank(n)[:], terms[:, n % 4, 0, :],
                                          ALU.subtract).then_inc(rest1, 1)
                    dve.wait_ge(v_done, g + 1)
                    dve.wait_ge(v_set, 2)
                    dve.tensor_copy(vv[:, GT * g:GT * g + GT, :, 0:DH].rearrange("p n h e -> p (n h) e"),
                                    v_bank(g)[:].rearrange("p (m e) -> p m e", e=DH)).then_inc(v_kept, 1)

                def tile_max(n, i):
                    w, _, _, _ = max_of(i)
                    dve.wait_ge(tile_scored, i + 1)
                    dve.reduce_max(maxes[:, w % 2, i % MAXES:i % MAXES + 1], spare_bank(n)[:], AXX).then_inc(bank_freed, 1)

                def row_max_of(w):
                    dve.wait_ge(bank_freed, use_of["max", MAXES * (w + 1) - 1] + 1)
                    if w >= 2:
                        dve.wait_ge(max_split, w - 1)
                    pair = maxes[:, w % 2, :].rearrange("p (m t) -> p m t", t=2)
                    dve.tensor_tensor(row_max[:, w % 2, :], pair[:, :, 0], pair[:, :, 1],
                                      ALU.max).then_inc(row_max_ready, 1)

                def keep_max(n, w):
                    dve.wait_ge(max_turned, w + 1)
                    if w:
                        dve.wait_ge(max_out, 16 * w)
                    dve.tensor_copy(max_rows[:], spare_bank(n)[0:3 * MAXES // 2, 0:P // 2].bitcast(BF16)).then_inc(bank_freed, 1)

                def normalise(n, o):
                    u, qh = divmod(o, 2)
                    b, hg = u // 2, u % 2
                    dve.wait_ge(mixed_turned, o + 1)
                    if o:
                        dve.wait_ge(bank_freed, use_of["turn", o - 1] + 1)
                    acc = spare_bank(n)[:].rearrange("p (n h e) -> p n h e", n=GT, h=HG)
                    chain.do(dve.reciprocal(r_sum[:], acc[:, :, :, DH]))
                    n0 = TB * b + GT * qh
                    dst = att[:, n0:n0 + GT, hg * HG * DH:(hg + 1) * HG * DH].rearrange("p n (h e) -> p n h e", e=DH)
                    for j in range(GT):
                        last = dve.tensor_tensor(dst[:, j], acc[:, j, :, 0:DH],
                                                 r_sum[:, j, :, None].to_broadcast([P, HG, DH]), ALU.mult)
                    last.then_inc(bank_freed, 1)

                free = {"max": tile_max, "turn_max": keep_max, "turn": normalise}

                def free_banks(uses):
                    for n, kind, x in uses:
                        free[kind](n, x)
                        if kind == "max" and x % MAXES == MAXES - 1:
                            row_max_of(x // MAXES)

                for g in range(NG):
                    norm.dve(dve, chain, g, ahead=True)
                    if g % 2 and g >= 3:
                        split(g - 3)
                        split(g - 2)
                split(NG - 2)
                split(NG - 1)
                for t in range(-1, LAST + TURN_LAG):
                    free_banks(stream[t])
                for g in range(NG):
                    dve.wait_ge(wo_done, g + 1)
                    hv = xa[:, GT * g:GT * g + GT, :].rearrange("p n c -> p (n c)")
                    dve.tensor_tensor(hv, hv, k.ps[2 + g % 2][:], ALU.add).then_inc(h4_ready, 1)
                dve.wait_ge(h4_ready, NG)

            @block.scalar
            def _(act):
                act.wait_ge(loaded, 16 * len(loads))
                act.wait_ge(k.buf_cleared, 16 * k.CLEARS)

                def first_terms(g):
                    for n in (2 * g, 2 * g + 1):
                        act.wait_ge(qk_done, n + 1)
                        if n >= 4:
                            act.wait_ge(terms_out[n % 4], 16 * (n // 4))
                        act.activation(terms[:, n % 4, 0, :], qk_bank(n)[:], ACT.Copy).then_inc(term1, 1)

                def second_terms(g):
                    for n in (2 * g, 2 * g + 1):
                        act.wait_ge(rest1, n + 1)
                        act.activation(terms[:, n % 4, 1, :], rest[:, n % 4, :], ACT.Copy).then_inc(term2, 1)

                for g in range(NG + 2):
                    if g >= 2:
                        first_terms(g - 2)
                    if g < NG:
                        norm.act_apply(act, g)
                    if 1 <= g <= NG:
                        norm.act_copy(act, g - 1)
                    if g >= 2:
                        second_terms(g - 2)
                for t in range(LAST + KEEP_LAG):
                    o = output_at(t, KEEP_LAG)
                    if o is not None:
                        act.wait_ge(pv_done, (o + 1) * TB // 2)
                        if o:
                            act.wait_ge(mixed_turned, o)
                        act.activation(mixed[:], k.ps[6][:], ACT.Copy).then_inc(mixed_kept, 1)
                    if t < LAST:
                        act.wait_ge(scored, t + 1)
                        if t >= P_SLOTS:
                            act.wait_ge(pv_done, (t - P_SLOTS) // HG + 1)
                        pair = k.psum[:, t % 2 * 2 * GC:(t % 2 + 1) * 2 * GC]
                        act.activation(probs[:, t % P_SLOTS, :], pair, ACT.Exp, scale=DH ** -0.5).then_inc(exp_done, 1)
                for g in range(NG):
                    act.wait_ge(att_turned, g + 1)
                    if g >= 2:
                        act.wait_ge(wo_done, g - 1)
                    act.activation(att_t[:, g % 2, :], k.ps[g % 2][:], ACT.Copy).then_inc(att_t_ready, 1)

            @block.tensor
            def _(pe):
                pe.wait_ge(loaded, 16 * len(loads))

                def project(g):
                    pe.wait_ge(norm.x_t_ready, g + 1)
                    for j, w in enumerate((w_q, w_k)):
                        if g >= 2:
                            pe.wait_ge(rest1, 2 * g - 3 + j)
                        pe.matmul(qk_bank(2 * g + j)[:], w[:], x_t[:, g * GC:(g + 1) * GC], start=True,
                                  stop=True).then_inc(qk_done, 1)
                    if g >= 2:
                        pe.wait_ge(v_kept, g - 1)
                    for j in range(GT):
                        n = GT * g + j
                        last = pe.matmul(v_bank(g)[:, j * P:(j + 1) * P], x_t[:, n * P:(n + 1) * P], w_v[:],
                                         start=True, stop=True)
                    last.then_inc(v_done, 1)

                def take_bank(n):
                    if n >= len(SPARE):
                        pe.wait_ge(bank_freed, n - len(SPARE) + 1)
                    return spare_bank(n)

                def first_pass(n, i):
                    w, h, qt, half = max_of(i)
                    u, slot = w // 2, w // 2 % SLOTS
                    if i % (2 * MAXES) == 0:
                        pe.wait_ge(qk_in[slot], 16 * 12 * (u // SLOTS + 1))
                    pe.matmul(take_bank(n)[:], q6[0:ROWS, slot, h, qt * P:(qt + 1) * P],
                              k6[0:ROWS, slot, h, half * GC:(half + 1) * GC], start=True,
                              stop=True).then_inc(tile_scored, 1)

                def turn_max(n, w):
                    pe.wait_ge(max_split, w + 1)
                    pe.transpose(take_bank(n)[0:3 * MAXES // 2, 0:P // 2].bitcast(BF16),
                                 max_terms[:].rearrange("p t m -> p (t m)"), ident16[:]).then_inc(max_turned, 1)

                def second_pass(t):
                    u, qh, kp, h = step_of(t)
                    slot = u % SLOTS
                    if t % (STEPS // 2) == 0:
                        pe.wait_ge(max_in[slot][qh], 16 * (u // SLOTS + 1))
                        pe.wait_ge(k_ones_set, 1)
                    if t >= 2:
                        pe.wait_ge(exp_done, t - 1)
                    for j in range(2):
                        kt = 2 * kp + j
                        last = pe.matmul(k.ps[t % 2 * 2 + j][:], k6[0:ROWS + 3, slot, h, kt * P:(kt + 1) * P],
                                         q6[0:ROWS + 3, slot, h, qh * GC:(qh + 1) * GC], start=True, stop=True)
                    last.then_inc(scored, 1)

                def times_v(g, j):
                    u, qh, kp, _ = step_of(HG * g)
                    b, hg = u // 2, u % 2
                    kt = 2 * kp + j
                    pe.wait_ge(exp_done, HG * (g + 1))
                    if kt == 0 and g:
                        pe.wait_ge(mixed_kept, g // (TB // 2))
                    for h in range(HG):
                        last = pe.matmul(k.ps[6][32 * h:32 * h + 32, :], vv[:, TB * b + kt, hg * HG + h, :],
                                         probs[:, (HG * g + h) % P_SLOTS, j * GC:(j + 1) * GC],
                                         start=(kt == 0), stop=(kt == TB - 1))
                    if j:
                        last.then_inc(pv_done, 1)

                def turn(n, o):
                    pe.wait_ge(mixed_kept, o + 1)
                    bank = take_bank(n)
                    for j in range(GT):
                        last = pe.transpose(bank[:, j * P:(j + 1) * P], mixed[:, j * P:(j + 1) * P], k.ident[:])
                    last.then_inc(mixed_turned, 1)

                fill = {"max": first_pass, "turn_max": turn_max, "turn": turn}
                pe.wait_ge(ident_set, 1)
                for g in range(NG + 1):
                    if g < NG:
                        norm.pe(pe, g)
                    if g >= 1:
                        project(g - 1)
                pe.wait_ge(v_kept, NG)
                pe.wait_ge(rest1, 2 * NG)
                for t in range(-1, LAST + TURN_LAG):
                    if 0 <= t < LAST:
                        second_pass(t)
                    uses = stream[t]
                    for n, kind, x in uses[:1]:
                        fill[kind](n, x)
                    for j in range(2):
                        g = group_at(t, PV_LAG + 2 * j)
                        if g is not None:
                            times_v(g, j)
                    for n, kind, x in uses[1:]:
                        fill[kind](n, x)
                pe.wait_ge(bank_freed, len(use_of))
                pe.wait_ge(exp_done, LAST)

                def out_proj(g):
                    pe.wait_ge(att_t_ready, g + 1)
                    if g >= 2:
                        pe.wait_ge(h4_ready, g - 1)
                    for j in range(GT):
                        last = pe.matmul(k.ps[2 + g % 2][:, j * P:(j + 1) * P], att_t[:, g % 2, j * P:(j + 1) * P],
                                         w_o[:], start=True, stop=True)
                    last.then_inc(wo_done, 1)

                for g in range(NG + 1):
                    if g < NG:
                        if g >= 2:
                            pe.wait_ge(att_t_ready, g - 1)
                        for j in range(GT):
                            last = pe.transpose(k.ps[g % 2][:, j * P:(j + 1) * P], att[:, GT * g + j, :], k.ident[:])
                        last.then_inc(att_turned, 1)
                    if g >= 1:
                        out_proj(g - 1)


def experts(nc, d, k, out):
    hres, xa = k.hres, k.xa
    A = 2 * NT
    SLOT_ROWS = E1 * CAP
    FAR = float(SLOT_ROWS)
    buf, y_dram = k.buf, k.y_dram
    RT = 512 // E1
    W_SLOTS, X_SLOTS = 16, 8
    W_LAG = 6
    BITS = 16
    WORDS = E1 // BITS

    with Stage(nc, k, "rt_") as st:
        sb, sem = st.sb, st.sem
        gate = sb("gate", [P, NT, 2], F32)
        mask = sb("mask", [P, WORDS], I32)
        w1 = sb("w1", [P, W_SLOTS, FFN], F32)
        w2 = sb("w2", [P, W_SLOTS, NM, H], F32)
        b2 = sb("b2", [P, W_SLOTS, H], F32)
        w_in = [sem(f"w_in{i}") for i in range(W_SLOTS)]

        def load_weights(sp, e):
            s = e % W_SLOTS
            sp.dma_start(w1[:, s], d["moe_w1"][e]).then_inc(w_in[s], 16)
            sp.dma_start(w2[:, s].rearrange("p m c -> p (m c)"), d["moe_w2"][e]).then_inc(w_in[s], 16)
            sp.dma_start(b2[:, s], d["moe_b2"][e:e + 1, :].to_broadcast([P, H])).then_inc(w_in[s], 16)

        with Stage(nc, k, "rt_") as st2:
            sb, sem = st2.sb, st2.sem
            x2_rows = sb("x2_rows", [P, NT, ROW], F32)
            x2 = x2_rows[:, :, 0:H]
            token = sb("token", [P, NT], F32)
            bit_weight = sb("bit_weight", [P, E1], F32)
            above = sb("above", [P, E1], F32)
            words = sb("words", [P, WORDS], F32)
            x_t = sb("x_t", [P, T], F32)
            g_tok, b_tok = sb("g_tok", [P, H], F32), sb("b_tok", [P, H], F32)
            g_col, b_col = sb("g_col", [P, 1], F32), sb("b_col", [P, 1], F32)
            w_r = sb("w_r", [P, E1], F32)
            before32 = sb("before32", [P, P], F32)
            before = sb("before", [P, P], BF16)
            ones16 = sb("ones16", [P, P], BF16)
            number = sb("number", [P, E1], F32)
            logit = sb("logit", [P, NT, E1], F32)
            top = sb("top", [P, NT, 8], F32)
            top_at = sb("top_at", [P, NT, 8], U32)
            expert = sb("expert", [P, NT, 2], F32)
            hot = sb("hot", [P, 2, NT, E1], BF16)
            both = sb("both", [P, 2, NT, E1], BF16)
            upto = sb("upto", [P, 2, RT, E1], BF16)
            so_far = sb("so_far", [P, E1], BF16)
            picked = sb("picked", [P, 2, RT, E1], F32)
            pos = sb("pos", [P, NT, 2], F32)
            kept = sb("kept", [P, NT, 2], F32)
            high = sb("high", [P, NT, 2], F32)
            addr = sb("addr", [P, NT, 2], F32)
            far = sb("far", [P, NT, 2], F32)
            taddr = sb("taddr", [P, NT, 2], I32)
            lead = sb("lead", [P, NT], F32)

            loaded, dve_chain = sem("loaded"), sem("dve_chain")
            scaled, x2_ready = sem("scaled"), sem("x2_ready")
            logit_done, logit_kept = sem("logit_done"), sem("logit_kept")
            lead_ready, lead_exp = sem("lead_ready"), sem("lead_exp")
            hot_ready, prefix_done, counted = sem("hot_ready"), sem("prefix_done"), sem("counted")
            addr_ready, scattered = sem("addr_ready"), sem("scattered")
            norm = Norm(st2, "n0", tile_of(xa), tile_of(x2), [k.ps[0], k.ps[1]],
                        lambda act, g, bank: act.activation(x_t[:, g * GC:(g + 1) * GC], bank[:], ACT.Identity,
                                                            bias=b_col[:, 0:1], scale=g_col[:, 0:1]), k.ident)
            loads = ((g_tok[:], "ln2_g_tok"), (b_tok[:], "ln2_b_tok"), (g_col[:], "ln2_g"), (b_col[:], "ln2_b"),
                     (w_r[:], "w_r"), (before32[:], "before"), (number[:], "number"),
                     (token[:], "token"), (bit_weight[:], "bit_weight"))
            with nc.Block() as block:
                @block.sync
                def _(sp):
                    for dst, src in loads:
                        sp.dma_start(dst, d[src]).then_inc(loaded, 16)
                    for e in range(W_SLOTS):
                        load_weights(sp, e)

                @block.gpsimd
                def _(pool):
                    pool.wait_ge(loaded, 16 * len(loads))
                    b4 = b_tok[:, None, :].to_broadcast([P, GT, H])
                    pool.wait_ge(k.buf_cleared, 16 * k.CLEARS)
                    for j in range(NT // RT):
                        for g in (2 * j, 2 * j + 1):
                            pool.wait_ge(scaled, g + 1)
                            v = x2[:, GT * g:GT * g + GT, :]
                            pool.tensor_tensor(v, v, b4, ALU.add).then_inc(x2_ready, 1)
                        pool.wait_ge(x2_ready, 2 * j + 2)
                        pool.wait_ge(addr_ready, j + 1)
                        for n in range(RT * j, RT * j + RT):
                            for c in range(2):
                                pool.indirect_dma_start(buf, bass.IndirectOffsetOnAxis(ap=taddr[:, n, c:c + 1], axis=0),
                                                        x2_rows[:, n, :], None, bounds_check=SLOT_ROWS - 1,
                                                        oob_is_err=False).then_inc(scattered, 16)
                    pool.wait_ge(scattered, 16 * A)

                @block.vector
                def _(dve):
                    chain = Chain(dve, dve_chain)
                    norm.dve(dve, chain, 0, ahead=True)
                    dve.wait_ge(loaded, 16 * len(loads))
                    chain.step(dve.tensor_copy(before[:], before32[:]))
                    chain.step(dve.memset(ones16[:], 1.0))
                    chain.step(dve.memset(so_far[:], 0.0))
                    g4 = g_tok[:, None, :].to_broadcast([P, GT, H])

                    def scale(g):
                        dve.wait_ge(norm.turned, g + 1)
                        v = x2[:, GT * g:GT * g + GT, :]
                        dve.tensor_tensor(v, v, g4, ALU.mult).then_inc(scaled, 1)

                    def choose(j):
                        dve.wait_ge(logit_kept, j + 1)
                        for n in range(RT * j, RT * j + RT):
                            chain.step(dve.max(top[:, n, :], logit[:, n, :]))
                        chain.wait()
                        for n in range(RT * j, RT * j + RT):
                            chain.step(dve.max_index(top_at[:, n, :], top[:, n, :], logit[:, n, :]))

                    def mark(j):
                        tiles = slice(RT * j, RT * j + RT)
                        chain.wait()
                        chain.step(dve.tensor_tensor(lead[:, tiles], top[:, tiles, 1], top[:, tiles, 0], ALU.subtract))
                        chain.do(dve.tensor_copy(expert[:, tiles, :], top_at[:, tiles, 0:2]))
                        chain.step(dve.tensor_copy(x2_rows[:, tiles, H], token[:, tiles]))
                        chain.step(dve.tensor_copy(x2_rows[:, tiles, H + 1], expert[:, tiles, 0]))
                        for c in range(2):
                            chain.step(dve.tensor_tensor(hot[:, c, tiles], number[:, None, :].to_broadcast([P, RT, E1]),
                                                         expert[:, tiles, c:c + 1].to_broadcast([P, RT, E1]), ALU.is_equal))
                        chain.wait()
                        chain.do(dve.tensor_tensor(both[:, 0, tiles], hot[:, 0, tiles], hot[:, 1, tiles], ALU.add))
                        old, new = both[:, 0, tiles], upto[:, 0]
                        for r in range(3):
                            sh = 1 << r
                            chain.step(dve.tensor_tensor(new[:, sh:, :], old[:, sh:, :], old[:, 0:RT - sh, :], ALU.add))
                            chain.do(dve.tensor_copy(new[:, 0:sh, :], old[:, 0:sh, :]))
                            old, new = new, upto[:, (r + 1) % 2]
                        chain.step(dve.tensor_tensor(both[:, 1, RT * j + 1:RT * j + RT, :], old[:, 0:RT - 1, :],
                                                     so_far[:, None, :].to_broadcast([P, RT - 1, E1]), ALU.add))
                        chain.do(dve.tensor_copy(both[:, 1, RT * j, :], so_far[:]))
                        chain.do(dve.tensor_tensor(so_far[:], so_far[:], old[:, RT - 1, :], ALU.add))
                        dve.sem_inc(hot_ready, 1)

                    def address(j):
                        tiles = slice(RT * j, RT * j + RT)
                        dve.wait_ge(prefix_done, j + 1)
                        for c in range(2):
                            chain.do(dve.tensor_tensor(picked[:, c], k.ps[2 + j][:].rearrange("p (n e) -> p n e", e=E1),
                                                       hot[:, c, tiles, :], ALU.mult))
                        for c in range(2):
                            chain.step(dve.tensor_reduce(pos[:, tiles, c], picked[:, c], AXX, ALU.add))
                        chain.wait()
                        at, far_t, high_t = pos[:, tiles], far[:, tiles], high[:, tiles]
                        kept_t, addr_t = kept[:, tiles], addr[:, tiles]
                        chain.step(dve.tensor_scalar(kept_t, at, float(CAP), None, ALU.is_lt))
                        chain.do(dve.tensor_scalar(high_t, at, float(P), None, ALU.is_ge))
                        chain.step(dve.tensor_scalar(far_t, kept_t, -FAR, FAR, ALU.mult, ALU.add))
                        chain.do(dve.scalar_tensor_tensor(at, high_t, -float(P), at, ALU.mult, ALU.add))
                        chain.do(dve.scalar_tensor_tensor(addr_t, at, float(HALVES), high_t, ALU.mult, ALU.add))
                        chain.do(dve.scalar_tensor_tensor(addr_t, expert[:, tiles], float(CAP), addr_t, ALU.mult, ALU.add))
                        dve.tensor_tensor(taddr[:, tiles], addr_t, far_t, ALU.add).then_inc(addr_ready, 1)

                    for g in range(1, NG):
                        norm.dve(dve, chain, g, ahead=True)
                        if g % 2 and g >= 3:
                            scale(g - 3)
                            scale(g - 2)
                            j = (g - 3) // 2
                            if j:
                                address(j - 1)
                            choose(j)
                            mark(j)
                    scale(NG - 2)
                    scale(NG - 1)
                    address(2)
                    choose(3)
                    mark(3)
                    dve.sem_inc(lead_ready, 1)
                    address(3)
                    dve.wait_ge(lead_exp, 1)
                    chain.do(dve.tensor_scalar(gate[:, :, 1], lead[:], 1.0, None, ALU.add))
                    chain.do(dve.reciprocal(gate[:, :, 0], gate[:, :, 1]))
                    chain.do(dve.tensor_tensor(gate[:, :, 1], gate[:, :, 0], lead[:], ALU.mult))
                    chain.step(dve.tensor_tensor(gate[:], gate[:], kept[:], ALU.mult))
                    dve.wait_ge(counted, 1)
                    chain.do(dve.scalar_tensor_tensor(above[:], k.ps[0][:, 0:E1], float(P), bit_weight[:],
                                                      ALU.is_gt, ALU.mult))
                    chain.do(dve.tensor_reduce(words[:], above[:].rearrange("p (w b) -> p w b", b=BITS), AXX, ALU.add))
                    chain.do(dve.tensor_copy(mask[:], words[:]))

                @block.scalar
                def _(act):
                    def logits(act, j):
                        act.wait_ge(logit_done, j + 1)
                        act.activation(logit[:, RT * j:RT * j + RT, :].rearrange("p n e -> p (n e)"), k.ps[2 + j][:],
                                       ACT.Copy).then_inc(logit_kept, 1)

                    for g in range(NG + 1):
                        if g < NG:
                            norm.act_apply(act, g)
                        if g == 1:
                            act.wait_ge(loaded, 16 * len(loads))
                        if g >= 1:
                            norm.act_copy(act, g - 1)
                        if g >= 2 and g % 2 == 0:
                            logits(act, (g - 2) // 2)
                    act.wait_ge(lead_ready, 1)
                    act.activation(lead[:], lead[:], ACT.Exp).then_inc(lead_exp, 1)

                @block.tensor
                def _(pe):
                    pe.wait_ge(loaded, 16 * len(loads))

                    def places(j):
                        pe.wait_ge(logit_kept, j + 1)
                        pe.wait_ge(hot_ready, j + 1)
                        tiles = slice(RT * j, RT * j + RT)
                        pe.matmul(k.ps[2 + j][:], before[:], both[:, 0, tiles, :].rearrange("p n e -> p (n e)"),
                                  start=True, stop=False)
                        pe.matmul(k.ps[2 + j][:], ones16[:], both[:, 1, tiles, :].rearrange("p n e -> p (n e)"),
                                  start=False, stop=True).then_inc(prefix_done, 1)

                    for g in range(NG + 1):
                        if g < NG:
                            norm.pe(pe, g)
                        if g >= 1:
                            pe.wait_ge(norm.x_t_ready, g)
                            for n in range(GT * (g - 1), GT * g):
                                last = pe.matmul(k.ps[2 + n // RT][:, n % RT * E1:(n % RT + 1) * E1],
                                                 x_t[:, n * P:(n + 1) * P], w_r[:], start=True, stop=True)
                            if g % 2 == 0:
                                last.then_inc(logit_done, 1)
                            if g >= 4 and g % 2 == 0:
                                places((g - 4) // 2)
                    places(NT // RT - 1)
                    pe.matmul(k.ps[0][:, 0:E1], ones16[:], so_far[:], start=True, stop=True).then_inc(counted, 1)

        with Stage(nc, k, "moe_") as st3:
            sb, sem = st3.sb, st3.sem
            b1 = sb("b1", [P, E1, NM], F32)
            xe = sb("xe", [P, X_SLOTS, HALVES, ROW], F32)
            xe_t = sb("xe_t", [P, 2, CAP], F32)
            he = sb("he", [P, 2, NM, CAP], F32)
            ye = sb("ye", [P, X_SLOTS, HALVES, H], F32)
            dest_f = sb("dest_f", [P, 2, HALVES], F32)
            dest = sb("dest", [P, 2 * X_SLOTS, HALVES], I32)
            y_got = sb("y_got", [P, NT, 2, H], F32)
            b1_in, xe_set = sem("b1_in"), sem("xe_set")
            x_in = [sem(f"x_in{i}") for i in range(X_SLOTS)]
            y_out = [sem(f"y_out{i}") for i in range(X_SLOTS)]
            second_write, second_out = sem("second_write"), sem("second_out")
            turned, x_kept, dest_part = sem("turned"), sem("x_kept"), sem("dest_part")
            hid_done, hid_kept = sem("hid_done"), sem("hid_kept")
            y_done, y_kept = sem("y_done"), sem("y_kept")
            got = [sem(f"got{g}") for g in range(NG)]
            summed, dve_chain, stored = sem("summed"), sem("dve_chain"), k.stored
            buf_v = buf.rearrange("(e p t) c -> e p t c", p=P, t=HALVES)

            def load_masks(eng):
                return [eng.value_load(mask[0:1, i:i + 1], min_val=0, max_val=2 ** BITS - 1) for i in range(WORDS)]

            def has_second(masks, e):
                return (masks[e // BITS] & (1 << e % BITS)) > 0

            def load_results(eng, g):
                for i in range(X_SLOTS):
                    eng.wait_ge(y_out[i], 16 * E1 // X_SLOTS)
                eng.wait_ge(second_out, E1)
                src = y_dram[2 * GC * g:2 * GC * (g + 1), :].rearrange("(n p c) h -> p n (c h)", p=P, c=2)
                eng.dma_start(y_got[:, GT * g:GT * g + GT].rearrange("p n c h -> p n (c h)"), src).then_inc(got[g], 16)

            with nc.Block() as block:
                @block.sync
                def _(sp):
                    sp.dma_start(b1[:], d["moe_b1"]).then_inc(b1_in, 16)
                    masks = load_masks(sp)
                    sp.wait_ge(xe_set, 1)
                    for e in range(E1):
                        if e >= X_SLOTS:
                            sp.wait_ge(x_kept, e - X_SLOTS + 1)
                        s = e % X_SLOTS
                        with sp.If(has_second(masks, e)):
                            sp.dma_start(xe[:, s].rearrange("p t c -> p (t c)"),
                                         buf_v[e].rearrange("p t c -> p (t c)")).then_inc(x_in[s], 16)
                        with sp.Else():
                            sp.dma_start(xe[:, s, 0, :], buf_v[e][:, 0, :]).then_inc(x_in[s], 16)
                        w = e - W_LAG + W_SLOTS
                        if e >= W_LAG and w < E1:
                            sp.wait_ge(y_kept, e - W_LAG + 1)
                            load_weights(sp, w)
                    for g in range(0, NG, 2):
                        load_results(sp, g)
                    for g in range(NG):
                        sp.wait_ge(summed, g + 1)
                        sp.dma_start(out[g * GC:(g + 1) * GC, :].rearrange("(n p) c -> p n c", p=P),
                                     hres[:, GT * g:GT * g + GT, :]).then_inc(stored, 16)
                    sp.wait_ge(stored, 16 * NG)

                @block.gpsimd
                def _(pool):
                    masks = load_masks(pool)
                    second_count = pool.alloc_register("second_count")
                    pool.reg_mov(second_count, 0)
                    pool.wait_ge(k.buf_cleared, 16 * k.CLEARS)
                    for e in range(E1):
                        pool.wait_ge(y_kept, e + 1)
                        s = e % X_SLOTS

                        def write(t, done):
                            at = dest[:, e % (2 * X_SLOTS), t:t + 1]
                            pool.indirect_dma_start(y_dram, bass.IndirectOffsetOnAxis(ap=at, axis=0), ye[:, s, t, :],
                                                    None, bounds_check=2 * T - 1,
                                                    oob_is_err=False).then_inc(done, 16)

                        write(0, y_out[s])
                        with pool.If(has_second(masks, e)):
                            write(1, second_write)
                            pool.reg_add(second_count, second_count, 16)
                            pool.wait_ge(second_write, second_count)
                        pool.sem_inc(second_out, 1)

                @block.vector
                def _(dve):
                    dve.memset(xe[:], 0.0).then_inc(xe_set, 1)
                    chain = Chain(dve, dve_chain)
                    for e in range(E1 + 2):
                        if e < E1:
                            x, f = xe[:, e % X_SLOTS], dest_f[:, e % 2]
                            dve.wait_ge(x_in[e % X_SLOTS], 16 * (e // X_SLOTS + 1))
                            dve.scalar_tensor_tensor(f, x[:, :, H + 1], float(e), x[:, :, H], ALU.not_equal,
                                                     ALU.add).then_inc(dest_part, 1)
                            dve.wait_ge(dest_part, e + 1)
                            dve.tensor_scalar(dest[:, e % (2 * X_SLOTS), :], f, float(2 * T), None, ALU.add)
                            dve.wait_ge(turned, e + 1)
                            if e >= 2:
                                dve.wait_ge(hid_done, NM * (e - 1))
                            dve.tensor_copy(xe_t[:, e % 2, :], k.ps[e % 2][:, 0:CAP]).then_inc(x_kept, 1)
                        if e >= 2:
                            f = e - 2
                            dve.wait_ge(y_done, f + 1)
                            if f >= X_SLOTS:
                                dve.wait_ge(y_out[f % X_SLOTS], 16 * (f // X_SLOTS))
                                dve.wait_ge(second_out, f - X_SLOTS + 1)
                            dve.tensor_tensor(ye[:, f % X_SLOTS], k.ps[6 + f % 2][:, 0:CAP].rearrange("p (t c) -> p t c", c=H),
                                              b2[:, f % W_SLOTS, None, :].to_broadcast([P, HALVES, H]),
                                              ALU.add).then_inc(y_kept, 1)
                    chain.do(dve.tensor_tensor(hres[:], hres[:], xa[:], ALU.add))
                    for g in range(NG):
                        dve.wait_ge(got[g], 16)
                        for c in range(2):
                            for n in range(GT * g, GT * g + GT):
                                chain.step(dve.scalar_tensor_tensor(hres[:, n, :], y_got[:, n, c, :], gate[:, n, c:c + 1],
                                                                    hres[:, n, :], ALU.mult, ALU.add))
                            chain.wait()
                        dve.sem_inc(summed, 1)

                @block.scalar
                def _(act):
                    act.wait_ge(b1_in, 16)
                    for e in range(E1):
                        for m in range(NM):
                            act.wait_ge(hid_done, NM * e + m // 2 * 2 + 2)
                            if e >= 2:
                                act.wait_ge(y_done, e - 1)
                            bank = k.ps[2 + 2 * (e % 2) + m // 2]
                            act.activation(he[:, e % 2, m, :], bank[:, m % 2 * CAP:(m % 2 + 1) * CAP],
                                           ACT.Gelu_apprx_tanh, bias=b1[:, e, m:m + 1]).then_inc(hid_kept, 1)
                    for g in range(1, NG, 2):
                        load_results(act, g)

                @block.tensor
                def _(pe):
                    masks = load_masks(pe)

                    def turn(e):
                        pe.wait_ge(x_in[e % X_SLOTS], 16 * (e // X_SLOTS + 1))
                        if e >= 2:
                            pe.wait_ge(x_kept, e - 1)
                        for t in range(HALVES):
                            last = pe.transpose(k.ps[e % 2][:, t * P:(t + 1) * P], xe[:, e % X_SLOTS, t, 0:H], k.ident[:])
                        last.then_inc(turned, 1)

                    def up(e, halves):
                        for m in range(NM):
                            if e >= 2:
                                pe.wait_ge(hid_kept, NM * (e - 2) + m // 2 * 2 + 2)
                            bank = k.ps[2 + 2 * (e % 2) + m // 2]
                            pe.matmul(bank[:, m % 2 * CAP:m % 2 * CAP + halves * P], w1[:, e % W_SLOTS, m * P:(m + 1) * P],
                                      xe_t[:, e % 2, 0:halves * P], start=True, stop=True).then_inc(hid_done, 1)

                    def down(e, halves):
                        for t in range(halves):
                            for m in range(NM):
                                last = pe.matmul(k.ps[6 + e % 2][:, t * P:(t + 1) * P], he[:, e % 2, m, t * P:(t + 1) * P],
                                                 w2[:, e % W_SLOTS, m, :], start=(m == 0), stop=(m == NM - 1))
                        last.then_inc(y_done, 1)

                    for e in range(E1 + 2):
                        if e < E1:
                            turn(e)
                        if 1 <= e <= E1:
                            pe.wait_ge(x_kept, e)
                            pe.wait_ge(w_in[(e - 1) % W_SLOTS], 16 * 3 * ((e - 1) // W_SLOTS + 1))
                            with pe.If(has_second(masks, e - 1)):
                                up(e - 1, 2)
                            with pe.Else():
                                up(e - 1, 1)
                        if e >= 2:
                            pe.wait_ge(hid_kept, NM * (e - 1))
                            if e >= 4:
                                pe.wait_ge(y_kept, e - 3)
                            with pe.If(has_second(masks, e - 2)):
                                down(e - 2, 2)
                            with pe.Else():
                                down(e - 2, 1)


def zeros_out(sp, k):
    zeros = k.xa[:].rearrange("p n c -> p (n c)")
    sp.wait_ge(k.zeroed, 1)
    for dram, cols in ((k.buf, E1 * CAP * ROW // P), (k.y_dram, 2 * T * H // P)):
        flat = dram.rearrange("(p r) c -> p (r c)", p=P)
        for c0 in range(0, cols, NT * H):
            width = min(NT * H, cols - c0)
            sp.dma_start(flat[:, c0:c0 + width], zeros[:, 0:width]).then_inc(k.buf_cleared, 16)


class Keep:
    CLEARS = -(-E1 * CAP * ROW // (T * H)) + 2 * T * H // (T * H)


STAGES = [embed_and_scan, task_ffn, linear_attention, softmax_attention]


def build(nc, d, out, stages=None, last=True):
    with ExitStack() as ctx:
        k = Keep()
        k.ctx = ctx
        k.hres = ctx.enter_context(nc.sbuf_tensor("hres", [P, NT, H], F32))
        k.ident = ctx.enter_context(nc.sbuf_tensor("ident", [P, P], F32))
        k.xa = ctx.enter_context(nc.sbuf_tensor("xa", [P, NT, H], F32))
        k.psum = ctx.enter_context(nc.psum_tensor("psum", [P, 8 * 512], F32))
        k.ps = [k.psum[:, 512 * i:512 * i + 512] for i in range(8)]
        k.stored = ctx.enter_context(nc.semaphore("stored"))
        k.zeroed = ctx.enter_context(nc.semaphore("zeroed"))
        k.buf_cleared = ctx.enter_context(nc.semaphore("buf_cleared"))
        k.buf = nc.dram_tensor("buf_dram", (E1 * CAP, ROW), F32).ap()
        k.y_dram = nc.dram_tensor("y_dram", (2 * T, H), F32).ap()
        for stage in (stages or STAGES):
            stage(nc, d, k)
        if last:
            experts(nc, d, k, out)
            return
        stored = k.stored
        with nc.Block() as block:
            @block.sync
            def _(sp):
                sp.dma_start(out.rearrange("(n p) c -> p n c", p=P), k.hres[:]).then_inc(stored, 16)
                sp.wait_ge(stored, 16)


def layout(inp):
    f = lambda n: np.asarray(inp[n])
    c = np.ascontiguousarray
    bc = lambda n: c(np.broadcast_to(f(n), (P, H)))
    tiles = lambda a: a.reshape(NT, P).T
    a = {
        "ids": c(np.stack([tiles(f("x")), tiles(f("itok_BS_2_50255"))], 1)),
        "table": c(f("L0_tok_weight")),
        "ident": np.eye(P, dtype=np.float32),
        "bm_t": c(f("L0_attn_Bm").T), "c_t": c(f("L0_attn_C").T),
        "a_t": c(f("L0_attn_A").T), "a": c(f("L0_attn_A")),
        "gamma_b": bc("L0_attn_gamma"), "beta_b": bc("L0_attn_beta"),
    }
    R, K9 = P // NE0, NE0 + 1
    gb, g2 = f("L0_ffn_gfc2_b"), f("L0_ffn_gfc2_w")
    with_base = lambda tv, base: c(np.concatenate([f(tv), f(base)[None]], 0))
    merge_w = np.full((K9, P), 0.03, np.float32)
    merge_w[NE0] = 1.0 - 0.03 * NE0
    a.update({
        "gfc1_t": c(f("L0_ffn_gfc1_w").T), "gfc1_b": c(f("L0_ffn_gfc1_b")[:, None]),
        "gfc2_rep": c(np.broadcast_to(g2.T[:, :, None], (P, NE0, R))),
        "gfc2_b_rep": c(np.broadcast_to(gb[:, None, None], (NE0, R, 1)).reshape(P, 1)),
        "gfc2_t": c(g2.T), "gfc2_b": c(gb[:, None]),
        "delta": c(np.tile(np.eye(R, dtype=np.float32), (NE0, 1))),
        "tv_w1": c(f("L0_ffn_tv_W1").reshape(P, FFN // R, H)), "tv_w2": c(f("L0_ffn_tv_W2").reshape(P, H // R, FFN)),
        "w1_t": c(f("L0_ffn_W1").T), "w2_t": c(f("L0_ffn_W2").T.reshape(NM, P, H).transpose(1, 0, 2)),
        "tv_b1": with_base("L0_ffn_tv_b1", "L0_ffn_b1"), "tv_b2": with_base("L0_ffn_tv_b2", "L0_ffn_b2"),
        "tv_ln": c(np.concatenate([with_base("L0_ffn_tv_ln_g", "L0_ffn_ln_g"), with_base("L0_ffn_tv_ln_b", "L0_ffn_ln_b")], 1)),
        "merge_w": merge_w,
    })
    inv_freq = (1.0 / 10000.0 ** (np.arange(0, DH, 2, dtype=np.float32) / DH)).astype(np.float32)
    freqs = np.outer(np.arange(S, dtype=np.float32), inv_freq)
    angle = np.tile(np.concatenate([freqs, freqs], -1), (1, NH))
    cos, sin = np.cos(angle).astype(np.float32), np.sin(angle).astype(np.float32)
    rot = np.zeros((P, P), np.float32)
    for h in range(NH):
        for e in range(DH // 2):
            rot[h * DH + e, h * DH + e + DH // 2] = -1.0
            rot[h * DH + e + DH // 2, h * DH + e] = 1.0
    head = np.arange(P) // DH
    b_qk = f("L1_attn_bqk")
    by_tile = lambda t: c(t.reshape(TB, P, H).transpose(1, 0, 2))
    a.update({
        "w_qk": c(f("L1_attn_Wqk")), "b_q": c(b_qk[:H, None]), "b_k": c(b_qk[None, H:]),
        "ones": np.ones((P, P), np.float32), "cos_tok": by_tile(cos), "sin_tok": by_tile(sin),
        "cos_feat": c(cos.T), "sin_feat": c(sin.T), "rot": rot, "rot_t": c(rot.T),
        "head_mask": (head[:, None] == head[None, :]).astype(np.float32) / np.float32(S),
        "head_cols": (head[:, None] == np.arange(NH)[None, :]).astype(np.float32) / np.float32(S),
        "lepe_w": c(f("L1_attn_lepe_w")[:, 0, :]), "lepe_b": bc("L1_attn_lepe_b"),
    })
    a.update({
        "w_q": c(f("L1_ffn_wq")), "w_k": c(f("L1_ffn_wk")), "w_v": c(f("L1_ffn_wv")), "w_o": c(f("L1_ffn_wo")),
        "ln1_g": c(f("L1_ffn_ln1_g")[:, None]), "ln1_b": c(f("L1_ffn_ln1_b")[:, None]),
        "ln2_g_tok": bc("L1_ffn_ln2_g"), "ln2_b_tok": bc("L1_ffn_ln2_b"),
        "ln2_g": c(f("L1_ffn_ln2_g")[:, None]), "ln2_b": c(f("L1_ffn_ln2_b")[:, None]), "w_r": c(f("L1_ffn_wr")),
        "before": c(np.triu(np.ones((P, P), np.float32), 1)),
        "number": c(np.broadcast_to(np.arange(E1, dtype=np.float32), (P, E1))),
        "token": c(2 * tiles(np.arange(T, dtype=np.float32)) - np.float32(2 * T)),
        "bit_weight": c(np.broadcast_to(2.0 ** (np.arange(E1) % 16), (P, E1)).astype(np.float32)),
        "moe_w1": c(f("L1_ffn_w1")), "moe_b1": c(f("L1_ffn_b1").reshape(E1, NM, P).transpose(2, 0, 1)),
        "moe_w2": c(f("L1_ffn_w2").reshape(E1, NM, P, H).transpose(0, 2, 1, 3).reshape(E1, P, NM * H)),
        "moe_b2": c(f("L1_ffn_b2")),
    })
    return a


def kernel(**inputs):
    import concourse.bacc as _bacc
    from concourse.bass_utils import run_bass_kernel_spmd as _run

    nc = _bacc.Bacc("TRN2", target_bir_lowering=False, num_devices=1)
    arrays = layout(inputs)
    d = {n: nc.dram_tensor("in_" + n, a.shape, mybir.dt.from_np(a.dtype), kind="ExternalInput").ap() for n, a in arrays.items()}
    out = nc.dram_tensor("out", (T, H), F32, kind="ExternalOutput").ap()
    build(nc, d, out)
    r = _run(nc, [{"in_" + n: a for n, a in arrays.items()}], core_ids=[0])
    return r.results[0]["out"].reshape(B, S, H)
```
